# Optimizing a Trainium2 kernel written in Bass

```python
import numpy as np
import jax
import jax.numpy as jnp

def _softmax(x, axis=-1):
    return jax.nn.softmax(x, axis=axis)

def _gelu(x):
    return jax.nn.gelu(x, approximate=True)

def _silu(x):
    return jax.nn.silu(x)

def _sigmoid(x):
    return jax.nn.sigmoid(x)

def _layernorm(x, axis=-1, eps=1e-05):
    m = jnp.mean(x, axis=axis, keepdims=True)
    v = jnp.var(x, axis=axis, keepdims=True)
    return (x - m) / jnp.sqrt(v + eps)

def _scatter_add(tgt, idx, src, axis=0):
    return tgt.at[idx].add(src)

def _segment_sum(src, seg, n):
    return jax.ops.segment_sum(src, seg, n)
kernel_name = 'mk_lm_tower_d1_tok_ids768_r4_bb73b2'

def setup_inputs(seed: int=0):
    np.random.seed(seed)
    _w = jnp.asarray

    def _rec_inputs():
        import jax
        import jax.numpy as jnp
        _rk = jax.random.key(seed)
        x = jax.random.randint(jax.random.fold_in(_rk, 1), (64, 128), 0, 12564, jnp.int32)
        return x
    x = _rec_inputs()

    def _L0_tok_setup():
        import jax, jax.numpy as jnp
        import numpy as np
        B, T, V, C = (8, 512, 50257, 192)

        def _rosa(x):
            Bx, Tx = x.shape
            eq = (x[:, :, None] == x[:, None, :]).astype(jnp.int32)

            def step(prev, eq_row):
                cur = (jnp.pad(prev[:, :-1], ((0, 0), (1, 0))) + 1) * eq_row
                return (cur, cur)
            init = jnp.zeros((Bx, Tx), jnp.int32)
            _, rows = jax.lax.scan(step, init, jnp.swapaxes(eq, 0, 1)[1:])
            L = jnp.swapaxes(jnp.concatenate([init[None], rows], axis=0), 0, 1)
            mask = jnp.tril(jnp.ones((Tx, Tx), dtype=bool), -1)
            j = jnp.arange(Tx, dtype=jnp.float32)
            TIE = 1e-05
            scored = jnp.where(mask[None], L.astype(jnp.float32) + j[None, None, :] * TIE, -1.0)
            best_j = jnp.argmax(scored, axis=2)
            pred_idx = jnp.minimum(best_j + 1, Tx - 1)
            preds = jnp.take_along_axis(x, pred_idx, axis=1)
            no_match = jnp.max(jnp.where(mask[None], L, 0), axis=2) == 0
            return jnp.where(no_match, -1, preds)
        key = jax.random.key(seed)
        k1, k2 = jax.random.split(key)
        idx = jax.random.randint(k1, (B, T), 0, V)
        emb = jax.random.normal(k2, (V, C), dtype=jnp.float32)
        return {'idx': idx, 'emb': emb}
    _L0_tok_all = _L0_tok_setup()
    _L0_tok_in = {k: v for k, v in _L0_tok_all.items() if k in ('emb',)}
    del _L0_tok_all

    def _L0_attn_setup():
        import jax, jax.numpy as jnp
        import numpy as np
        HIDDEN = 192
        HEADS = 8
        key = jax.random.key(seed)
        ks = jax.random.split(key, 5)
        b, n = (2, 256)
        x = jax.random.normal(ks[0], (b, n, HIDDEN), dtype=jnp.float32)
        W_qkv = jax.random.normal(ks[1], (HIDDEN, 3 * HIDDEN * HEADS), dtype=jnp.float32) * 0.02
        b_qkv = jnp.zeros((3 * HIDDEN * HEADS,), dtype=jnp.float32)
        W_proj = jax.random.normal(ks[2], (HEADS * HIDDEN, HIDDEN), dtype=jnp.float32) * 0.02
        b_proj = jnp.zeros((HIDDEN,), dtype=jnp.float32)
        return {'x': x, 'W_qkv': W_qkv, 'b_qkv': b_qkv, 'W_proj': W_proj, 'b_proj': b_proj}
    _L0_attn_all = _L0_attn_setup()
    _L0_attn_in = {k: v for k, v in _L0_attn_all.items() if k in ('W_qkv', 'b_qkv', 'W_proj', 'b_proj')}
    del _L0_attn_all

    def _L0_ffn_setup():
        import jax, jax.numpy as jnp
        import numpy as np
        CAPACITY_FACTOR = 1.25
        key = jax.random.key(seed)
        ks = jax.random.split(key, 5)
        B, S, D, F, E = (8, 512, 192, 768, 8)
        return {'x': jax.random.normal(ks[0], (B, S, D), jnp.float32), 'switch_w': jax.random.normal(ks[1], (D, E), jnp.float32) * 0.02, 'switch_b': jnp.zeros((E,), jnp.float32), 'w1': jax.random.normal(ks[2], (E, D, F), jnp.float32) * 0.02, 'b1': jnp.zeros((E, F), jnp.float32), 'w2': jax.random.normal(ks[3], (E, F, D), jnp.float32) * 0.02, 'b2': jnp.zeros((E, D), jnp.float32)}
    _L0_ffn_all = _L0_ffn_setup()
    _L0_ffn_in = {k: v for k, v in _L0_ffn_all.items() if k in ('switch_w', 'switch_b', 'w1', 'b1', 'w2', 'b2')}
    del _L0_ffn_all
    return {'x': x, 'L0_tok_emb': _L0_tok_in['emb'], 'L0_attn_W_qkv': _L0_attn_in['W_qkv'], 'L0_attn_b_qkv': _L0_attn_in['b_qkv'], 'L0_attn_W_proj': _L0_attn_in['W_proj'], 'L0_attn_b_proj': _L0_attn_in['b_proj'], 'L0_ffn_switch_w': _L0_ffn_in['switch_w'], 'L0_ffn_switch_b': _L0_ffn_in['switch_b'], 'L0_ffn_w1': _L0_ffn_in['w1'], 'L0_ffn_b1': _L0_ffn_in['b1'], 'L0_ffn_w2': _L0_ffn_in['w2'], 'L0_ffn_b2': _L0_ffn_in['b2']}

def reference(x, L0_tok_emb, L0_attn_W_qkv, L0_attn_b_qkv, L0_attn_W_proj, L0_attn_b_proj, L0_ffn_switch_w, L0_ffn_switch_b, L0_ffn_w1, L0_ffn_b1, L0_ffn_w2, L0_ffn_b2):
    import jax
    import jax.numpy as jnp

    def _L0_tok_ref(idx, emb):
        import jax, jax.numpy as jnp
        import numpy as np
        B, T, V, C = (8, 512, 50257, 192)

        def _rosa(x):
            Bx, Tx = x.shape
            eq = (x[:, :, None] == x[:, None, :]).astype(jnp.int32)

            def step(prev, eq_row):
                cur = (jnp.pad(prev[:, :-1], ((0, 0), (1, 0))) + 1) * eq_row
                return (cur, cur)
            init = jnp.zeros((Bx, Tx), jnp.int32)
            _, rows = jax.lax.scan(step, init, jnp.swapaxes(eq, 0, 1)[1:])
            L = jnp.swapaxes(jnp.concatenate([init[None], rows], axis=0), 0, 1)
            mask = jnp.tril(jnp.ones((Tx, Tx), dtype=bool), -1)
            j = jnp.arange(Tx, dtype=jnp.float32)
            TIE = 1e-05
            scored = jnp.where(mask[None], L.astype(jnp.float32) + j[None, None, :] * TIE, -1.0)
            best_j = jnp.argmax(scored, axis=2)
            pred_idx = jnp.minimum(best_j + 1, Tx - 1)
            preds = jnp.take_along_axis(x, pred_idx, axis=1)
            no_match = jnp.max(jnp.where(mask[None], L, 0), axis=2) == 0
            return jnp.where(no_match, -1, preds)
        p = _rosa(idx)
        out = emb[jnp.clip(p, 0)]
        return jnp.where((p == -1)[..., None], 0.0, out)

    def _L0_attn_ref(x, W_qkv, b_qkv, W_proj, b_proj):
        import jax, jax.numpy as jnp
        import numpy as np
        HIDDEN = 192
        HEADS = 8
        b, n, c = x.shape
        qkv = x @ W_qkv + b_qkv
        q, k, v = jnp.split(qkv, 3, axis=-1)
        q = q.reshape(b, HEADS, n, HIDDEN)
        k = k.reshape(b, HEADS, n, HIDDEN)
        v = v.reshape(b, HEADS, n, HIDDEN)
        energy = jnp.einsum('bhqd,bhkd->bhqk', q, k)
        scaling = jnp.float32(HIDDEN ** 0.5)
        attn = jax.nn.softmax(energy, axis=-1) / scaling
        out = jnp.einsum('bhal,bhlv->bhav', attn, v)
        out = out.reshape(b, n, HEADS * HIDDEN)
        return out @ W_proj + b_proj

    def _L0_ffn_ref(x, switch_w, switch_b, w1, b1, w2, b2):
        import jax, jax.numpy as jnp
        import numpy as np
        CAPACITY_FACTOR = 1.25
        B, S, D = x.shape
        E = w1.shape[0]
        xf = x.reshape(-1, D)
        N = xf.shape[0]
        capacity = int(CAPACITY_FACTOR * N / E)
        probs = jax.nn.softmax(xf @ switch_w + switch_b, axis=-1)
        prob_max = jnp.max(probs, axis=-1)
        routes = jnp.argmax(probs, axis=-1)
        sort_idx = jnp.lexsort((-prob_max, routes))
        counts = jnp.bincount(routes, length=E)
        starts = jnp.concatenate([jnp.zeros((1,), counts.dtype), jnp.cumsum(counts)[:-1]])
        rank_sorted = jnp.arange(N) - starts[routes[sort_idx]]
        rank = jnp.zeros((N,), jnp.int32).at[sort_idx].set(rank_sorted.astype(jnp.int32))
        keep = rank < capacity
        dest_e = jnp.where(keep, routes, E)
        dest_c = jnp.where(keep, rank, 0)
        buf = jnp.zeros((E + 1, capacity, D), xf.dtype).at[dest_e, dest_c].set(xf)
        h = jax.nn.gelu(jnp.einsum('ecd,edf->ecf', buf[:E], w1) + b1[:, None, :], approximate=False)
        o = jnp.einsum('ecf,efd->ecd', h, w2) + b2[:, None, :]
        y_exp = o[routes, dest_c]
        y = jnp.where(keep[:, None], y_exp, xf)
        out = y * prob_max[:, None]
        return out.reshape(B, S, D)
    h = _L0_tok_ref(x, L0_tok_emb)
    h = h + _L0_attn_ref(_layernorm(h, axis=-1), L0_attn_W_qkv, L0_attn_b_qkv, L0_attn_W_proj, L0_attn_b_proj)
    h = h + _L0_ffn_ref(_layernorm(h, axis=-1), L0_ffn_switch_w, L0_ffn_switch_b, L0_ffn_w1, L0_ffn_b1, L0_ffn_w2, L0_ffn_b2)
    return h

_drawn_inputs = setup_inputs


def setup_inputs(seed=0):
    import zlib

    import numpy as np

    out = dict(_drawn_inputs(seed))
    spreads = {'L0_attn_b_qkv': (0.0, 0.1),
     'L0_attn_b_proj': (0.0, 0.1),
     'L0_ffn_switch_b': (0.0, 0.1),
     'L0_ffn_b1': (0.0, 0.8),
     'L0_ffn_b2': (0.0, 0.276)}
    factors = {}
    for name, (base, spread) in spreads.items():
        noise = np.random.default_rng([zlib.crc32(name.encode()), seed]).standard_normal(out[name].shape)
        drawn = base * np.exp(spread * noise) if base else spread * noise
        out[name] = jnp.asarray(drawn.astype(out[name].dtype))
    for name, factor in factors.items():
        out[name] = (out[name] * factor).astype(out[name].dtype)
    return out
```

```python
from contextlib import ExitStack

import concourse.bass as bass
from concourse import mybir

ALU = mybir.AluOpType
ACT = mybir.ActivationFunctionType
AX = mybir.AxisListType
F32 = mybir.dt.float32
I32 = mybir.dt.int32

P = 128
B, T = 64, 128
N = B * T
D = 192
HEADS = 8
HD = HEADS * D
DH = D // 2
GT = T // HEADS
G = N // GT
GC = G // P
CG = P // GT
CHUNKS = (G + 1 + CG - 1) // CG
COLS = 72
E = 8
F = 768
FC = F // P
CAP = int(1.25 * N / E)
TILES = (CHUNKS * P + E * (P - 1)) // P
FILLS = 8
EPS = 1e-5
NOWHERE = 65536.0
VOCAB_PAD = -1.0
assert TILES <= COLS and CHUNKS < COLS

def build(nc, x, emb, w_qkv, b_qkv, w_proj, b_proj, sw, sb_, w1, b1, w2, b2, out):
    ctx = ExitStack()
    with ctx:
        def sb(name, shape, dt=F32):
            return ctx.enter_context(nc.sbuf_tensor(name, shape, dt))

        def sem(name):
            return ctx.enter_context(nc.semaphore(name))

        pred_d = nc.dram_tensor("pred_d", (N,), F32, kind="Internal").ap()
        prob_d = nc.dram_tensor("prob_d", (CHUNKS * CG, 2 * GT), F32, kind="Internal").ap()
        xh_d = nc.dram_tensor("xh_d", (CHUNKS * P, 2 * D), F32, kind="Internal").ap()
        xs_d = nc.dram_tensor("xs_d", (TILES * P, 2 * D), F32, kind="Internal").ap()
        o_d = nc.dram_tensor("o_d", (TILES * P, D), F32, kind="Internal").ap()
        v_d = nc.dram_tensor("v_d", (P, HD), F32, kind="Internal").ap()
        x_rows = x.rearrange("b (t o) -> (b t) o", o=1)
        out_rows = out.rearrange("b t d -> (b t) d")
        out_groups = out.rearrange("b (g r) d -> (b g) (r d)", r=GT)

        area = sb("area", [P, 2 * 3 * HD])
        wqkv_s = area[0:DH + 1, :].rearrange("p (h n) -> p h n", h=2)
        wproj_s = sb("wproj_s", [DH, 2 * HEADS, D])
        bproj_s = sb("bproj_s", [1, D])
        wsw_s = sb("wsw_s", [DH + 1, 2, E])
        w1_s = sb("w1_s", [DH + 1, 2, E, F])
        w2_s = sb("w2_s", [P, FC, E, D])
        WORK = 11264
        work = sb("work", [P, WORK])

        ident = sb("ident", [P, P])
        ones = sb("ones", [P, P])
        before = sb("before", [P, P])
        first = sb("first", [P, P])
        iota_f = sb("iota_f", [P, P])
        iota_q = sb("iota_q", [P, CG, GT])
        iota_g = sb("iota_g", [P, GC])
        iota_z = sb("iota_z", [P, GT])
        tok_of = sb("tok_of", [P, GC, GT])
        pred_base = sb("pred_base", [B, T])
        minus_half = sb("minus_half", [P, 1])
        match_j = sb("match_j", [P, B])

        pred_i = sb("pred_i", [P, COLS], I32)
        match_f = sb("match_f", [P, COLS])
        tok_i = sb("tok_i", [P, COLS], I32)
        valid = sb("valid", [P, COLS])
        prob_c = sb("prob_c", [P, COLS])
        route_c = sb("route_c", [P, COLS])
        keep_c = sb("keep_c", [P, COLS])
        scale_o = sb("scale_o", [P, COLS])
        scale_x = sb("scale_x", [P, COLS])
        slot_f = sb("slot_f", [P, COLS])
        slot_i = sb("slot_i", [P, COLS], I32)
        slot_lo = sb("slot_lo", [P, COLS])
        slot_hi = sb("slot_hi", [P, COLS])
        place_v = sb("place_v", [P, COLS])
        tok_v = sb("tok_v", [P, COLS])
        lists = sb("lists", [P, 3, COLS])
        zero = sb("zero", [P, 2 * D])
        list_i = sb("list_i", [P, COLS], I32)
        expert_i = sb("expert_i", [1, COLS], I32)
        zlist = sb("zlist", [P, 1])
        counts_i = sb("counts_i", [1, 2], I32)
        pick_q = sb("pick_q", [P, GC, P])
        pick_c = sb("pick_c", [P, GC, COLS])
        act = sb("act", [P, GC])
        rank_i = sb("rank_i", [P, GC], I32)

        idx_a = sb("idx_a", [P, 1], I32)
        idx_b = sb("idx_b", [P, 1], I32)
        tid = sb("tid", [P, 1], I32)
        emb_t = sb("emb_t", [P, D])
        h_next = sb("h_next", [P, D])
        h_cur = sb("h_cur", [P, D])
        xn = sb("xn", [P, D])
        xh = sb("xh", [P, 2 * D])
        xf = xh[:, 0:D]
        h1 = xh[:, D:2 * D]
        xt = sb("xt", [DH + 1, 2, P])
        xft = sb("xft", [DH + 1, 2, P])
        st = sb("st", [P, 12])
        st2 = sb("st2", [P, 12])
        rt = sb("rt", [P, 64])
        sm = sb("sm", [P, 4, CG])
        rk = sb("rk", [P, 16, GC])
        rki = sb("rki", [P, 2, GC], I32)

        banks = [ctx.enter_context(nc.psum_tensor(f"bank{i}", [P, 512], F32)) for i in range(8)]
        mm = banks[0:4]
        ps_s = banks[4:6]
        ps_t = banks[6]
        ps_m = banks[7]
        ps_y = ps_m[:, 0:D]
        ps_x = ps_m[:, D:D + P]
        ps_x2 = ps_m[:, D + P:D + 2 * P]
        ps_l = ps_m[:, D + 2 * P:D + 2 * P + E]

        RB = 8
        NB = B // RB
        starts = [T - 16 * (k + 1) for k in range(NB)]
        lens = [T - s for s in starts]
        offs = [RB * sum(lens[:k]) for k in range(NB + 1)]
        XW = 2 * T + 2

        used = [0]

        def cut(base, n):
            a = used[0]
            used[0] += n
            assert used[0] <= base.shape[1]
            return base[:, a:a + n]

        eq = cut(work, offs[-1])
        run = cut(work, offs[-1])
        x_i = cut(work, T).bitcast(I32)
        x_f = cut(work, T)
        x_pad_at = used[0]
        x_pad = cut(work, XW)
        best = cut(work, T)
        tmp_b = cut(work, T)
        tmp_i = cut(work, T).bitcast(I32)
        v4 = cut(work, N // P).rearrange("p (t r) -> p t r", t=GC)
        used[0] = 0
        pick_v = cut(work, GC * P).rearrange("p (t m) -> p t m", t=GC)
        pick_t = cut(work, GC * P).rearrange("p (t m) -> p t m", t=GC)
        pick_z = cut(work, GC * P).rearrange("p (t m) -> p t m", t=GC)

        used[0] = 0
        qt = cut(work, 2 * HEADS * P)[0:DH, :].rearrange("p (h g j r) -> p h g j r", h=2, g=CG, j=HEADS)
        kt = cut(work, 2 * HEADS * P)[0:DH, :].rearrange("p (h g j r) -> p h g j r", h=2, g=CG, j=HEADS)
        vn = cut(work, HD)
        vp = cut(work, CG * D).rearrange("p (g v) -> p g v", g=CG)
        ex = cut(work, CG * P).rearrange("p (g l) -> p g l", g=CG)
        pt = cut(work, CG * P).rearrange("p (g l) -> p g l", g=CG)
        ot = cut(work, 2 * HEADS * P)[0:DH, :].rearrange("p (h j t) -> p h j t", h=2, j=HEADS)

        used[0] = 0
        gx = cut(work, D)
        gxt = cut(work, 2 * P)[0:DH + 1, :].rearrange("p (h t) -> p h t", h=2)
        hs = cut(work, F)
        ht = cut(work, F).rearrange("p (c t) -> p c t", c=FC)
        ob = cut(work, D)
        b2_s = cut(work, E * D)[0:1, :].rearrange("p (e d) -> p e d", e=E)
        sx = cut(work, 2 * D)
        og = cut(work, D)
        xg = cut(work, 2 * D)
        yo = cut(work, D)
        xh0 = cut(work, 2 * D)
        bz = cut(work, D)
        az = cut(work, D)
        oz = cut(work, D)
        zt = cut(work, GT * D).rearrange("p (r d) -> p r d", r=GT)
        zk = cut(work, 2 * GT).rearrange("p (a r) -> p a r", a=2)
        p0 = cut(work, 1)
        zs = cut(work, 4)
        zs_i = cut(work, 2).bitcast(I32)

        TR = GC * GT
        used[0] = 0
        full = cut(area, GC * 2 * GT).rearrange("p (t w r) -> p t w r", t=GC, w=2)
        pT = cut(area, 2 * P)[0:CHUNKS, :].rearrange("p (q w r) -> p q w r", q=CG, w=2)
        member = cut(area, E * TR).rearrange("p (e n) -> p e n", e=E)
        score = cut(area, E * TR).rearrange("p (e n) -> p e n", e=E)
        cmp = cut(area, E * TR).rearrange("p (e n) -> p e n", e=E)
        tie = cut(area, E * TR).rearrange("p (e n) -> p e n", e=E)
        incl = cut(area, E * TR).rearrange("p (e n) -> p e n", e=E)
        reset_r = cut(area, E * TR).rearrange("p (n r) -> p n r", r=GT)
        reset_c = cut(area, E * CHUNKS).rearrange("p (e c) -> p e c", e=E)
        eqc = cut(area, E * CHUNKS).rearrange("p (e c) -> p e c", e=E)
        csum = cut(area, E * CHUNKS).rearrange("p (e c) -> p e c", e=E)
        cinc = cut(area, E * CHUNKS).rearrange("p (e c) -> p e c", e=E)
        posn = cut(area, E * CHUNKS).rearrange("p (e c) -> p e c", e=E)
        thr = cut(area, E)
        cand = cut(area, E)
        red = cut(area, E)
        rem = cut(area, E)
        step = cut(area, 1)
        trow = cut(area, E * GC).rearrange("p (e t) -> p e t", e=E)
        tbase = cut(area, E * GC).rearrange("p (e t) -> p e t", e=E)
        tsum = cut(area, E * GC).rearrange("p (e t) -> p e t", e=E)
        keep = cut(area, TR)
        keep_z = cut(area, TR + 1)
        pick_k = cut(area, GC * P).rearrange("p (t m) -> p t m", t=GC)
        tl = cut(area, 8 * E).rearrange("p (a e) -> p a e", a=8)
        tl_i = cut(area, 2 * E).bitcast(I32).rearrange("p (a e) -> p a e", a=2)
        tcmp = cut(area, TILES * E).rearrange("p (t e) -> p t e", e=E)[0:1]
        texp = cut(area, TILES)[0:1, :]
        sl_i = cut(area, 2 * COLS).bitcast(I32).rearrange("p (a c) -> p a c", a=2)
        row_of = cut(area, 3 * P).rearrange("p (a m) -> p a m", a=3)
        tile_of = cut(area, COLS)

        s_act_ready = sem("s_act_ready")
        s_act_tiles = sem("s_act_tiles")
        s_b2_in = sem("s_b2_in")
        s_best_out = sem("s_best_out")
        s_bz_ready = sem("s_bz_ready")
        s_c_idx = sem("s_c_idx")
        s_consts = sem("s_consts")
        s_counts = sem("s_counts")
        s_cx_in = sem("s_cx_in")
        s_dev_ready = sem("s_dev_ready")
        s_dve_tiles = sem("s_dve_tiles")
        s_emb_in = sem("s_emb_in")
        s_emb_used = sem("s_emb_used")
        s_eqc_mm = sem("s_eqc_mm")
        s_eqc_ready = sem("s_eqc_ready")
        s_exp_ready = sem("s_exp_ready")
        s_fill_out = sem("s_fill_out")
        s_full_in = sem("s_full_in")
        s_gx_in = sem("s_gx_in")
        s_gxt_mm = sem("s_gxt_mm")
        s_gxt_ready = sem("s_gxt_ready")
        s_h_mm = sem("s_h_mm")
        s_hs_ready = sem("s_hs_ready")
        s_ht_act = sem("s_ht_act")
        s_ht_dve = sem("s_ht_dve")
        s_ht_mm = sem("s_ht_mm")
        s_id_in = sem("s_id_in")
        s_idx_set = sem("s_idx_set")
        s_keep_mm = sem("s_keep_mm")
        s_keep_ready = sem("s_keep_ready")
        s_l_mm = sem("s_l_mm")
        s_lexp_ready = sem("s_lexp_ready")
        s_lists_mm = sem("s_lists_mm")
        s_lists_read = sem("s_lists_read")
        s_lists_ready = sem("s_lists_ready")
        s_lmax_ready = sem("s_lmax_ready")
        s_max_ready = sem("s_max_ready")
        s_o_mm = sem("s_o_mm")
        s_o_out = sem("s_o_out")
        s_ob_ready = sem("s_ob_ready")
        s_oz_in = sem("s_oz_in")
        s_p0_mm = sem("s_p0_mm")
        s_p_ready = sem("s_p_ready")
        s_picks = sem("s_picks")
        s_picks_mm = sem("s_picks_mm")
        s_pool_steps = sem("s_pool_steps")
        s_pred_back = sem("s_pred_back")
        s_probT_mm = sem("s_probT_mm")
        s_probT_ready = sem("s_probT_ready")
        s_prob_out = sem("s_prob_out")
        s_pt_mm = sem("s_pt_mm")
        s_pt_ready = sem("s_pt_ready")
        s_rank_mm = sem("s_rank_mm")
        s_red_mm = sem("s_red_mm")
        s_red_ready = sem("s_red_ready")
        s_s_mm = sem("s_s_mm")
        s_slots_known = sem("s_slots_known")
        s_small_in = sem("s_small_in")
        s_sp_steps = sem("s_sp_steps")
        s_sx_in = sem("s_sx_in")
        s_tables = sem("s_tables")
        s_tie_mm = sem("s_tie_mm")
        s_tie_ready = sem("s_tie_ready")
        s_tile_mm = sem("s_tile_mm")
        s_v_copied = sem("s_v_copied")
        s_v_moved = sem("s_v_moved")
        s_v_stored = sem("s_v_stored")
        s_var_ready = sem("s_var_ready")
        s_w1_in = sem("s_w1_in")
        s_w2_in = sem("s_w2_in")
        s_wproj_in = sem("s_wproj_in")
        s_wqkv_in = sem("s_wqkv_in")
        s_x_in = sem("s_x_in")
        s_xf_out = sem("s_xf_out")
        s_xf_ready = sem("s_xf_ready")
        s_xft_mm = sem("s_xft_mm")
        s_xft_ready = sem("s_xft_ready")
        s_xn_ready = sem("s_xn_ready")
        s_xs_cleared = sem("s_xs_cleared")
        s_xs_done = sem("s_xs_done")
        s_xs_out = sem("s_xs_out")
        s_xs_zero = sem("s_xs_zero")
        s_xt_mm = sem("s_xt_mm")
        s_xt_ready = sem("s_xt_ready")
        s_y_idx = sem("s_y_idx")
        s_y_mm = sem("s_y_mm")
        s_y_out = sem("s_y_out")
        s_sx_free = sem("s_sx_free")
        s_yo_free = sem("s_yo_free")
        s_y_ready = sem("s_y_ready")
        s_z_out = sem("s_z_out")
        s_zrow_in = sem("s_zrow_in")
        s_zt_ready = sem("s_zt_ready")

        block = ctx.enter_context(nc.Block())

        @block.sync
        def _(sp):
            sp.sem_inc(s_v_moved, 128)
            sp.sem_inc(s_xf_out, 16)
            sp.sem_inc(s_y_mm, 1)
            sp.sem_inc(s_pt_ready, 1)
            sp.sem_inc(s_emb_used, 1)
            sp.sem_inc(s_o_out, 16)
            sp.sem_inc(s_ob_ready, 1)
            sp.sem_inc(s_y_ready, 1)
            sp.sem_inc(s_sx_free, 1)
            sp.sem_inc(s_yo_free, 1)
            sp.dma_start(x_i[0:B, :], x).then_inc(s_x_in, 16)
            sp.dma_start(x_i[B:2 * B, :], x).then_inc(s_x_in, 16)
            sp.dma_start(wqkv_s[0:DH, 0, :], w_qkv[0:DH, :]).then_inc(s_wqkv_in, 16)
            sp.dma_start(wqkv_s[0:DH, 1, :], w_qkv[DH:D, :]).then_inc(s_wqkv_in, 16)
            sp.dma_start(wqkv_s[DH:DH + 1, 0, :], b_qkv.rearrange("(o n) -> o n", o=1)).then_inc(s_wqkv_in, 16)
            sp.wait_ge(s_best_out, 1)
            sp.dma_start(pred_d.rearrange("(b t) -> b t", t=T), best[0:B, :]).then_inc(s_pred_back, 16)
            sp.wait_ge(s_pred_back, 16)
            sp.dma_start(v4, pred_d.rearrange("(t p r) -> p t r", t=GC, r=GT)).then_inc(s_pred_back, 16)
            for f in range(FC):
                sp.dma_start(w2_s[:, f, :, :], w2.rearrange("e (c p) d -> c p e d", p=P)[f]).then_inc(s_w2_in, 16)

            sp.wait_ge(s_counts, 1)
            n = sp.value_load(counts_i[0:1, 0:1], min_val=1, max_val=CHUNKS)
            with sp.Fori(0, n) as c:
                sp.wait_ge(s_v_copied, c + 1)
                sp.sem_inc(s_sp_steps, 1)
                sp.wait_ge(s_y_mm, c + 1)
                sp.sem_inc(s_sp_steps, 1)
                sp.dma_start(v_d, vn).then_inc(s_v_stored, 16)
                sp.wait_ge(s_v_stored, c * 16 + 16)
                sp.sem_inc(s_sp_steps, 1)
                for j in range(HEADS):
                    sp.dma_start(vp[GT * j:GT * (j + 1), :, :],
                                 v_d[:, j * D:(j + 1) * D].rearrange("(g r) v -> r g v", r=GT)).then_inc(s_v_moved, 16)
                sp.wait_ge(s_xf_ready, c + 2)
                sp.sem_inc(s_sp_steps, 1)
                sp.dma_start(xh_d[bass.ds(c * P, P), :], xh[:, :]).then_inc(s_xf_out, 16)
                sp.wait_ge(s_xf_out, c * 16 + 32)
                sp.sem_inc(s_sp_steps, 1)

            sp.dma_start(xh0, xh_d[0:1, :].to_broadcast([P, 2 * D])).then_inc(s_zrow_in, 16)
            sp.dma_start(b2_s[0:1, :, :], b2.rearrange("(o e) d -> o e d", o=1)).then_inc(s_b2_in, 16)
            sp.wait_ge(s_probT_ready, 2)
            sp.dma_start(prob_d.rearrange("(c q) n -> c q n", q=CG),
                         pT[:, :, :, :].rearrange("c q w r -> c q (w r)")).then_inc(s_prob_out, 16)
            sp.wait_ge(s_slots_known, 1)
            m = sp.value_load(counts_i[0:1, 1:2], min_val=1, max_val=TILES)
            with sp.Fori(0, m) as t:
                sp.dma_start(xs_d[bass.ds(t * P, P), :], zero[:, :]).then_inc(s_xs_zero, 16)
                sp.wait_ge(s_xs_zero, t * 16 + 16)
                sp.sem_inc(s_sp_steps, 1)
            sp.sem_inc(s_xs_cleared, 1)
            with sp.Fori(0, n) as c:
                sp.wait_ge(s_sx_free, c + 1)
                sp.sem_inc(s_sp_steps, 1)
                sp.dma_start(sx, xh_d[bass.ds(c * P, P), :]).then_inc(s_sx_in, 16)
            sp.wait_ge(s_xs_done, 1)
            with sp.Fori(0, m) as t:
                sp.wait_ge(s_gxt_mm, t + 1)
                sp.sem_inc(s_sp_steps, 1)
                sp.dma_start(gx, xs_d[bass.ds(t * P, P), 0:D]).then_inc(s_gx_in, 16)
                sp.wait_ge(s_ob_ready, t + 1)
                sp.sem_inc(s_sp_steps, 1)
                sp.sem_inc(s_sp_steps, 1)
            sp.nop()

        @block.gpsimd
        def _(pool):
            pool.memset(ones[:, :], 1.0)
            pool.memset(ident[:, :], 0.0)
            pool.memset(first[:, :], 0.0)
            pool.drain()
            pool.memset(first[0:1, :], 1.0)
            pool.affine_select(out=ident[:, :], in_=ident[:, :], compare_op=ALU.not_equal, fill=1.0, base=0,
                               pattern=[[-1, P]], channel_multiplier=1)
            pool.affine_select(out=before[:, :], in_=ones[:, :], compare_op=ALU.is_gt, fill=0.0, base=0,
                               pattern=[[1, P]], channel_multiplier=-1)

            def iota(out_, pattern, base, mult):
                return pool.iota(out_, pattern, base=base, channel_multiplier=mult, allow_small_or_imprecise_dtypes=True)

            pool.drain()
            iota(match_j[0:B, :], [[2, B]], 1, 0)
            iota(match_j[B:2 * B, :], [[2, B]], 0, 0)
            pool.drain()
            iota(pred_base[:, :], [[1, T]], 2 - T, T)
            iota(iota_f[:, :], [[1, P]], 0, 0)
            iota(iota_q[:, :, :], [[1, CG], [0, GT]], 0, 0)
            iota(iota_g[:, :], [[P, GC]], 0, 1)
            iota(iota_z[:, :], [[1, GT]], 0, GT)
            iota(tok_of[:, :, :], [[P * GT, GC], [1, GT]], 0, GT)
            pool.drain()
            pool.memset(xt[DH:DH + 1, 0, :], 1.0)
            pool.memset(xft[DH:DH + 1, 0, :], 1.0)
            pool.drain()
            pool.memset(minus_half[:, :], -0.5)
            pool.memset(xf, 0.0)
            pool.memset(prob_c[:, :], 0.0)
            pool.memset(route_c[:, :], 0.0)
            pool.memset(zero[:, :], 0.0)
            pool.drain().then_inc(s_consts, 1)

            def fetch(c):
                pool.tensor_copy(idx_a[:, :], pred_i[:, bass.ds(c, 1)]).then_inc(s_idx_set, 1)
                pool.wait_ge(s_idx_set, c + 1)
                pool.sem_inc(s_pool_steps, 1)
                pool.indirect_dma_start(tid[:, :], None, x_rows, bass.IndirectOffsetOnAxis(ap=idx_a[:, 0:1], axis=0)).then_inc(s_id_in, 16)
                pool.wait_ge(s_id_in, c * 16 + 16)
                pool.sem_inc(s_pool_steps, 1)
                pool.wait_ge(s_emb_used, c + 1)
                pool.sem_inc(s_pool_steps, 1)
                pool.indirect_dma_start(emb_t[:, :], None, emb, bass.IndirectOffsetOnAxis(ap=tid[:, 0:1], axis=0)).then_inc(s_emb_in, 16)
                pool.wait_ge(s_emb_in, c * 16 + 16)
                pool.sem_inc(s_pool_steps, 1)

            pool.wait_ge(s_counts, 1)
            pool.wait_ge(s_tables, 1)
            n = pool.value_load(counts_i[0:1, 0:1], min_val=1, max_val=CHUNKS)
            def deviation(s, count):
                pool.wait_ge(s_var_ready, count)
                pool.sem_inc(s_pool_steps, 1)
                pool.tensor_scalar(s[:, 9:10], s[:, 7:8], EPS, None, ALU.add)
                pool.drain()
                pool.tensor_tensor(s[:, 8:9], s[:, 9:10], minus_half[:, :], ALU.pow).then_inc(s_dev_ready, 1)

            fetch(0)
            deviation(st, 1)
            fetch(1)
            with pool.Fori(0, n) as c:
                deviation(st, c * 2 + 2)
                fetch(c + 2)
                deviation(st2, c * 2 + 3)

            pool.wait_ge(s_prob_out, 16)
            for t in range(GC):
                pool.tensor_copy(idx_a[:, :], rank_i[:, t:t + 1])
                pool.drain()
                pool.indirect_dma_start(full[:, t, :, :].rearrange("p w r -> p (w r)"), None, prob_d,
                                        bass.IndirectOffsetOnAxis(ap=idx_a[:, 0:1], axis=0)).then_inc(s_full_in, 16)
                pool.wait_ge(s_full_in, 16 * (t + 1))
                pool.sem_inc(s_pool_steps, 1)

            pool.wait_ge(s_slots_known, 1)
            pool.wait_ge(s_xs_cleared, 1)
            with pool.Fori(0, n) as c:
                pool.tensor_copy(idx_a[:, :], slot_i[:, bass.ds(c, 1)]).then_inc(s_c_idx, 1)
                pool.wait_ge(s_c_idx, c + 1)
                pool.sem_inc(s_pool_steps, 1)
                pool.wait_ge(s_sx_in, c * 16 + 16)
                pool.sem_inc(s_pool_steps, 1)
                pool.indirect_dma_start(xs_d, bass.IndirectOffsetOnAxis(ap=idx_a[:, 0:1], axis=0), sx, None,
                                        bounds_check=TILES * P - 1, oob_is_err=False).then_inc(s_xs_out, 16)
                pool.wait_ge(s_xs_out, c * 16 + 16)
                pool.sem_inc(s_pool_steps, 1)
                pool.sem_inc(s_sx_free, 1)
            pool.sem_inc(s_xs_done, 1)

            pool.wait_ge(s_fill_out, 16 * FILLS)
            pool.wait_ge(s_zt_ready, 1)
            pool.indirect_dma_start(out_groups, bass.IndirectOffsetOnAxis(ap=zs_i[:, 0:1], axis=0),
                                    zt[:, :, :].rearrange("p r d -> p (r d)"), None,
                                    bounds_check=G - 1, oob_is_err=False).then_inc(s_z_out, 16)
            m = pool.value_load(counts_i[0:1, 1:2], min_val=1, max_val=TILES)
            with pool.Fori(0, m) as t:
                pool.tensor_copy(idx_b[:, :], list_i[:, bass.ds(t, 1)]).then_inc(s_y_idx, 1)
                pool.wait_ge(s_y_idx, t + 1)
                pool.sem_inc(s_pool_steps, 1)
                pool.wait_ge(s_y_ready, t + 2)
                pool.sem_inc(s_pool_steps, 1)
                pool.indirect_dma_start(out_rows, bass.IndirectOffsetOnAxis(ap=idx_b[:, 0:1], axis=0), yo, None,
                                        bounds_check=N - 1, oob_is_err=False).then_inc(s_y_out, 16)
                pool.wait_ge(s_y_out, t * 16 + 16)
                pool.sem_inc(s_pool_steps, 1)
                pool.sem_inc(s_yo_free, 1)
            pool.wait_ge(s_z_out, 16)
            pool.nop()

        @block.scalar
        def _(se):
            se.dma_start(bproj_s[:, :], b_proj.rearrange("(o n) -> o n", o=1)).then_inc(s_small_in, 16)
            se.dma_start(wsw_s[0:DH, :, :], sw.rearrange("(h p) e -> p h e", h=2)).then_inc(s_small_in, 16)
            se.dma_start(wsw_s[DH:DH + 1, 0, :], sb_.rearrange("(o n) -> o n", o=1)).then_inc(s_small_in, 16)
            se.dma_start(wproj_s[:, :, :], w_proj.rearrange("(j p) d -> p j d", p=DH)).then_inc(s_wproj_in, 16)
            se.dma_start(w1_s[0:DH, 0, :, :], w1[:, 0:DH, :].rearrange("e p f -> p e f")).then_inc(s_w1_in, 16)
            se.dma_start(w1_s[0:DH, 1, :, :], w1[:, DH:D, :].rearrange("e p f -> p e f")).then_inc(s_w1_in, 16)
            se.dma_start(w1_s[DH:DH + 1, 0, :, :], b1.rearrange("(o e) f -> o e f", o=1)).then_inc(s_w1_in, 16)
            se.sem_inc(s_act_tiles, 9)

            se.wait_ge(s_counts, 1)
            n = se.value_load(counts_i[0:1, 0:1], min_val=1, max_val=CHUNKS)
            with se.Fori(0, n) as c:
                se.wait_ge(s_v_moved, c * 128 + 128)
                for i in range(3):
                    se.wait_ge(s_tile_mm, c * 15 + i + 1)
                    se.copy(vn[:, 512 * i:512 * (i + 1)], mm[i % 4][:, :]).then_inc(s_act_tiles, 1)
                se.drain().then_inc(s_v_copied, 1)
                for i in range(4):
                    k = 3 + 2 * i
                    se.wait_ge(s_tile_mm, c * 15 + k + 1)
                    se.copy(qt[:, i % 2, :, 4 * (i // 2):4 * (i // 2) + 4, :].rearrange("p g j r -> p j g r"),
                            mm[k % 4][0:DH, :].rearrange("p (j g r) -> p j g r", j=4, g=CG)).then_inc(s_act_tiles, 1)
                for half in range(2):
                    se.wait_ge(s_max_ready, c * 2 + half + 1)
                    for g in range(4 * half, 4 * half + 4):
                        last = se.activation(ex[:, g, :], ps_s[half][:, P * (g % 4):P * (g % 4 + 1)], ACT.Exp,
                                             bias=sm[:, 1, g:g + 1], accum_out=sm[:, 2, g:g + 1])
                    last.then_inc(s_exp_ready, 1)
                se.wait_ge(s_lmax_ready, c + 1)
                se.activation(rt[:, 8:16], ps_l, ACT.Exp, bias=rt[:, 1:2], accum_out=rt[:, 2:3]).then_inc(s_lexp_ready, 1)
                for half in range(2):
                    se.wait_ge(s_pt_mm, c * 2 + half + 1)
                    se.copy(pt[:, 4 * half:4 * half + 4, :].rearrange("p g a -> p (g a)"), ps_t[:, :]).then_inc(s_pt_ready, 1)
                for i in range(2):
                    k = 11 + 2 * i
                    se.wait_ge(s_tile_mm, c * 15 + k + 1)
                    se.copy(ot[:, 0, :, 64 * i:64 * i + 64].rearrange("p j (g r) -> p g j r", r=GT),
                            mm[k % 4][0:DH, :].rearrange("p (g j r) -> p g j r", g=4, j=HEADS)).then_inc(s_act_tiles, 1)
            se.wait_ge(s_lmax_ready, n + 1)
            se.activation(rt[:, 8:16], ps_l, ACT.Exp, bias=rt[:, 1:2], accum_out=rt[:, 2:3]).then_inc(s_lexp_ready, 1)

            se.wait_ge(s_bz_ready, 1)
            for t in range(FILLS):
                se.dma_start(out_rows.rearrange("(t p r) d -> t p r d", t=FILLS, p=P)[t],
                             bz.rearrange("p (r d) -> p r d", r=1).to_broadcast([P, N // P // FILLS, D])).then_inc(s_fill_out, 16)
            se.wait_ge(s_slots_known, 1)
            m = se.value_load(counts_i[0:1, 1:2], min_val=1, max_val=TILES)
            with se.Fori(0, m) as t:
                se.wait_ge(s_ht_mm, t * 2 + 2)
                for i in range(2):
                    se.wait_ge(s_h_mm, t * 2 + i + 1)
                    se.activation(hs[:, 384 * i:384 * (i + 1)], mm[i][:, 0:384], ACT.Gelu).then_inc(s_hs_ready, 1)
                se.wait_ge(s_ht_mm, t * 2 + 4)
                se.copy(ht[:, 3:6, :].rearrange("p c t -> p (c t)"), mm[3][:, 0:384]).then_inc(s_ht_act, 1)
                se.wait_ge(s_ob_ready, t + 2)
                se.dma_start(o_d[bass.ds(t * P, P), :], ob).then_inc(s_o_out, 16)
                se.wait_ge(s_o_out, t * 16 + 32)
            z = se.value_load(slot_i[0:1, 0:1], min_val=0, max_val=TILES * P - 1)
            se.dma_start(oz, o_d[bass.ds(z, 1), :].to_broadcast([P, D])).then_inc(s_oz_in, 16)
            with se.Fori(0, m) as t:
                se.wait_ge(s_y_ready, t + 1)
                se.dma_start(og, o_d[bass.ds(t * P, P), :]).then_inc(s_cx_in, 16)
                se.dma_start(xg, xs_d[bass.ds(t * P, P), :]).then_inc(s_cx_in, 16)
            se.nop()

        @block.tensor
        def _(pe):
            pe.wait_ge(s_consts, 1)
            pe.wait_ge(s_act_ready, 1)
            pe.matmul(ps_m[:, 0:GC], before[:, :], act[:, :], start=True, stop=True)
            pe.matmul(ps_m[:, GC:2 * GC], ones[:, :], act[:, :], start=True, stop=True).then_inc(s_rank_mm, 1)
            pe.wait_ge(s_picks, 1)
            for dst, lhs in ((0, pick_v), (COLS, pick_t), (2 * COLS, pick_q)):
                for t in range(GC):
                    pe.matmul(mm[0][:, dst:dst + COLS], lhs[:, t, :], pick_c[:, t, :], start=t == 0, stop=t == GC - 1)
            for t in range(GC):
                last = pe.matmul(mm[0][:, 3 * COLS:3 * COLS + 1], pick_z[:, t, :], ones[:, 0:1], start=t == 0, stop=t == GC - 1)
            last.then_inc(s_picks_mm, 1)

            pe.wait_ge(s_wqkv_in, 48)
            pe.wait_ge(s_wproj_in, 16)
            pe.wait_ge(s_small_in, 48)
            pe.wait_ge(s_counts, 1)

            def turn_rows(src, a, b):
                pe.transpose(a[0:DH, :], src[:, 0:DH], ident[:, :])
                return pe.transpose(b[0:DH, :], src[:, DH:D], ident[:, :])

            pe.wait_ge(s_xn_ready, 1)
            turn_rows(xn, ps_x, ps_x2).then_inc(s_xt_mm, 1)

            act_tile = {0: 1, 1: 2, 2: 3, 3: 4, 5: 5, 7: 6, 9: 7, 11: 8, 13: 9}
            dve_tile = {4: 1, 6: 2, 8: 3, 10: 4, 12: 5, 14: 6}
            LEFT = {k: k - 4 for k in range(4, 15)}
            LEFT.update({0: 12, 1: 13, 2: 14, 3: 11})

            def bank_left(c, k):
                prev = LEFT[k]
                base = 0 if k < 4 else 1
                if prev in act_tile:
                    pe.wait_ge(s_act_tiles, c * 9 + 9 * base + act_tile[prev])
                else:
                    pe.wait_ge(s_dve_tiles, c * 6 + 6 * base + dve_tile[prev])

            def router(c):
                pe.wait_ge(s_xf_ready, c + 1)
                turn_rows(xf, ps_x, ps_x2).then_inc(s_xft_mm, 1)
                pe.wait_ge(s_xft_ready, c + 1)
                pe.matmul(ps_l, xft[:, 0, :], wsw_s[:, 0, :], start=True, stop=False)
                pe.matmul(ps_l, xft[0:DH, 1, :], wsw_s[0:DH, 1, :], start=False, stop=True).then_inc(s_l_mm, 1)

            n = pe.value_load(counts_i[0:1, 0:1], min_val=1, max_val=CHUNKS)
            with pe.Fori(0, n) as c:
                pe.wait_ge(s_xt_ready, c + 1)
                for i in range(3):
                    bank_left(c, i)
                    cols = slice(2 * HD + 512 * i, 2 * HD + 512 * (i + 1))
                    pe.matmul(mm[i][:, :], xt[:, 0, :], wqkv_s[:, 0, cols], start=True, stop=False)
                    pe.matmul(mm[i][:, :], xt[0:DH, 1, :], wqkv_s[0:DH, 1, cols], start=False, stop=True).then_inc(s_tile_mm, 1)
                for i in range(8):
                    k = 3 + i
                    which, half, jb = i % 2, (i // 2) % 2, i // 4
                    bank_left(c, k)
                    for j in range(4):
                        a = which * HD + (4 * jb + j) * D + half * DH
                        o_ = mm[k % 4][0:DH, P * j:P * (j + 1)]
                        pe.matmul(o_, wqkv_s[:, 0, a:a + DH], xt[:, 0, :], start=True, stop=False)
                        last = pe.matmul(o_, wqkv_s[0:DH, 1, a:a + DH], xt[0:DH, 1, :], start=False, stop=True)
                    last.then_inc(s_tile_mm, 1)
                pe.wait_ge(s_act_tiles, c * 9 + 16)
                pe.wait_ge(s_dve_tiles, c * 6 + 10)
                for half in range(2):
                    for g in range(4 * half, 4 * half + 4):
                        o_ = ps_s[half][:, P * (g % 4):P * (g % 4 + 1)]
                        for h in range(2):
                            last = pe.matmul(o_, qt[:, h, g, :, :].rearrange("p j r -> p (j r)"),
                                             kt[:, h, g, :, :].rearrange("p j r -> p (j r)"), start=h == 0, stop=h == 1)
                    last.then_inc(s_s_mm, 1)
                pe.wait_ge(s_xn_ready, c + 2)
                turn_rows(xn, ps_x, ps_x2).then_inc(s_xt_mm, 1)
                pe.wait_ge(s_xt_ready, c + 2)
                router(c)
                for half in range(2):
                    pe.wait_ge(s_p_ready, c * 2 + half + 1)
                    pe.wait_ge(s_pt_ready, c * 2 + half + 1)
                    for g in range(4 * half, 4 * half + 4):
                        last = pe.transpose(ps_t[:, P * (g % 4):P * (g % 4 + 1)], ex[:, g, :], ident[:, :])
                    last.then_inc(s_pt_mm, 1)
                pe.wait_ge(s_v_moved, c * 128 + 256)
                for i in range(4):
                    k = 11 + i
                    gq, half = i // 2, i % 2
                    pe.wait_ge(s_pt_ready, c * 2 + gq + 2)
                    bank_left(c, k)
                    for g in range(4 * gq, 4 * gq + 4):
                        last = pe.matmul(mm[k % 4][0:DH, P * (g % 4):P * (g % 4 + 1)],
                                         vp[:, g, half * DH:(half + 1) * DH], pt[:, g, :], start=True, stop=True)
                    last.then_inc(s_tile_mm, 1)
                pe.wait_ge(s_act_tiles, c * 9 + 18)
                pe.wait_ge(s_dve_tiles, c * 6 + 12)
                pe.matmul(ps_y, ones[0:1, :], bproj_s[0:1, :], start=True, stop=False)
                for j in range(HEADS):
                    for half in range(2):
                        last = pe.matmul(ps_y, ot[:, half, j, :], wproj_s[:, 2 * j + half, :],
                                         start=False, stop=j == HEADS - 1 and half == 1)
                last.then_inc(s_y_mm, 1)
            router(n)

            pe.wait_ge(s_probT_ready, 1)
            pe.matmul(mm[0][:, 0:1], first[:, :], prob_c[:, 1:2], start=True, stop=True).then_inc(s_p0_mm, 1)
            pe.transpose(mm[1][0:CHUNKS, 0:P], prob_c[:, 1:CHUNKS + 1], ident[:, :])
            pe.transpose(mm[1][0:CHUNKS, P:2 * P], route_c[:, 1:CHUNKS + 1], ident[:, :]).then_inc(s_probT_mm, 1)

            pe.wait_ge(s_eqc_ready, 1)
            half_e = E // 2
            for i in range(2):
                rows = eqc[:, half_e * i:half_e * (i + 1), :].rearrange("p e c -> p (e c)")
                pe.matmul(ps_s[i][:, 0:half_e * CHUNKS], before[:, :], rows, start=True, stop=True)
                last = pe.matmul(mm[2 + i][:, 0:half_e * CHUNKS], ones[:, :], rows, start=True, stop=True)
            last.then_inc(s_eqc_mm, 1)
            with pe.Fori(0, 28) as k:
                pe.wait_ge(s_red_ready, k + 1)
                pe.matmul(mm[1][:, 0:E], ones[:, :], red, start=True, stop=True).then_inc(s_red_mm, 1)
            pe.wait_ge(s_tie_ready, 1)
            pe.matmul(mm[1][:, 0:E], ones[:, :], red, start=True, stop=True)
            flat = trow[:, :, :].rearrange("p e t -> p (e t)")
            pe.matmul(mm[1][:, 64:64 + E * GC], before[:, :], flat, start=True, stop=True)
            pe.matmul(mm[1][:, 128:128 + E * GC], ones[:, :], flat, start=True, stop=True).then_inc(s_tie_mm, 1)
            pe.wait_ge(s_keep_ready, 1)
            pe.matmul(mm[1][:, 256:257], ones[:, :], keep_z[:, TR:TR + 1], start=True, stop=True)
            for t in range(GC):
                last = pe.matmul(mm[1][:, 300:300 + COLS], pick_k[:, t, :], pick_c[:, t, :], start=t == 0, stop=t == GC - 1)
            last.then_inc(s_keep_mm, 1)
            with pe.Fori(0, n) as c:
                pe.wait_ge(s_lists_ready, c + 1)
                for i in range(3):
                    last = pe.matmul(mm[0][:, COLS * i:COLS * (i + 1)], row_of[:, i, :], tile_of, start=True, stop=True)
                last.then_inc(s_lists_mm, 1)

            pe.wait_ge(s_w1_in, 48)
            pe.wait_ge(s_w2_in, 16 * FC)
            pe.wait_ge(s_b2_in, 16)
            pe.wait_ge(s_lists_read, 1)
            m = pe.value_load(counts_i[0:1, 1:2], min_val=1, max_val=TILES)
            pe.sem_inc(s_gxt_mm, 1)
            pe.sem_inc(s_ht_mm, 2)
            with pe.Fori(0, m) as t:
                e = pe.value_load(expert_i[0:1, bass.ds(t, 1)], min_val=0, max_val=E - 1)
                pe.wait_ge(s_gx_in, t * 16 + 16)
                turn_rows(gx, ps_s[0][:, 0:P], ps_s[0][:, P:2 * P]).then_inc(s_gxt_mm, 1)
                pe.wait_ge(s_gxt_ready, t + 1)
                for i in range(2):
                    fs = slice(384 * i, 384 * (i + 1))
                    pe.matmul(mm[i][:, 0:384], gxt[:, 0, :], w1_s[:, 0, bass.ds(e, 1), fs].rearrange("p e f -> p (e f)"), start=True, stop=False)
                    pe.matmul(mm[i][:, 0:384], gxt[0:DH, 1, :], w1_s[0:DH, 1, bass.ds(e, 1), fs].rearrange("p e f -> p (e f)"), start=False, stop=True).then_inc(s_h_mm, 1)
                for i in range(2):
                    pe.wait_ge(s_hs_ready, t * 2 + i + 1)
                    for f in range(3):
                        last = pe.transpose(mm[2 + i][:, P * f:P * (f + 1)], hs[:, 384 * i + P * f:384 * i + P * (f + 1)], ident[:, :])
                    last.then_inc(s_ht_mm, 1)
                pe.wait_ge(s_ob_ready, t + 1)
                pe.matmul(ps_y, ones[0:1, :], b2_s[0:1, bass.ds(e, 1), :].rearrange("p e d -> p (e d)"), start=True, stop=False)
                pe.wait_ge(s_ht_dve, t + 1)
                pe.wait_ge(s_ht_act, t + 1)
                for f in range(FC):
                    last = pe.matmul(ps_y, ht[:, f, :], w2_s[:, f, bass.ds(e, 1), :].rearrange("p e d -> p (e d)"), start=False, stop=f == FC - 1)
                last.then_inc(s_o_mm, 1)
            pe.nop()

        @block.vector
        def _(dve):
            def then(ins):
                dve.drain()

            dve.memset(x_pad, VOCAB_PAD)
            then(dve.memset(best, 0.0))
            dve.wait_ge(s_x_in, 32)
            then(dve.tensor_copy(x_f, x_i))
            dve.tensor_copy(x_pad[0:B, T:2 * T], x_f[0:B, :])
            then(dve.tensor_copy(x_pad[B:2 * B, T + 1:2 * T + 1], x_f[B:2 * B, :]))

            def blk(t, k):
                return t[:, offs[k]:offs[k + 1]].rearrange("p (r i) -> p r i", r=RB)

            for k in range(NB):
                shifted = bass.AP(work, x_pad_at + 1 + 2 * RB * k + starts[k], [[WORK, P], [2, RB], [1, lens[k]]])
                dve.tensor_tensor(blk(eq, k), x_f[:, starts[k]:T].rearrange("p (o i) -> p o i", o=1).to_broadcast([P, RB, lens[k]]),
                                  shifted, ALU.is_equal)
            dve.drain()
            then(dve.tensor_tensor_scan(run, eq, eq, 0.0, ALU.mult, ALU.add))
            dve.wait_ge(s_consts, 1)
            for k in range(NB):
                dve.scalar_tensor_tensor(out=blk(eq, k), in0=blk(run, k), scalar=128.0,
                                         in1=match_j[:, RB * k:RB * (k + 1)].rearrange("p (r o) -> p r o", o=1).to_broadcast([P, RB, lens[k]]),
                                         op0=ALU.mult, op1=ALU.add)
            dve.drain()
            for k in range(NB):
                then(dve.tensor_reduce(tmp_b[:, starts[k]:T], blk(eq, k).rearrange("p r i -> p i r"), AX.X, ALU.max))
                then(dve.tensor_tensor(best[:, starts[k]:T], best[:, starts[k]:T], tmp_b[:, starts[k]:T], ALU.max))
            then(dve.tensor_copy(tmp_b[0:B, :], best[B:2 * B, :]))
            then(dve.tensor_tensor(best[0:B, :], best[0:B, :], tmp_b[0:B, :], ALU.max))
            then(dve.tensor_copy(tmp_i[0:B, :], best[0:B, :]))
            then(dve.tensor_scalar(tmp_i[0:B, :], tmp_i[0:B, :], 127, None, ALU.bitwise_and))
            then(dve.tensor_copy(tmp_b[0:B, :], tmp_i[0:B, :]))
            then(dve.tensor_tensor(tmp_b[0:B, :], tmp_b[0:B, :], pred_base[:, :], ALU.add))
            dve.scalar_tensor_tensor(out=best[0:B, :], in0=best[0:B, :], scalar=128.0, in1=tmp_b[0:B, :],
                                     op0=ALU.is_ge, op1=ALU.mult).then_inc(s_best_out, 1)

            dve.wait_ge(s_pred_back, 32)
            then(dve.tensor_reduce(act[:, :], v4, AX.X, ALU.max))
            dve.tensor_scalar(act[:, :], act[:, :], 0.0, None, ALU.is_gt).then_inc(s_act_ready, 1)
            dve.wait_ge(s_rank_mm, 1)
            then(dve.tensor_copy(rk[:, 0:2, :].rearrange("p a t -> p (a t)"), ps_m[:, 0:2 * GC]))
            then(dve.tensor_tensor_scan(rk[:, 2, :], ones[:, 0:GC], rk[:, 1, :], 0.0, ALU.mult, ALU.add))
            then(dve.tensor_tensor(rk[:, 3, :], rk[:, 2, :], rk[:, 1, :], ALU.subtract))
            then(dve.tensor_tensor(rk[:, 3, :], rk[:, 3, :], rk[:, 0, :], ALU.add))
            then(dve.scalar_tensor_tensor(out=rk[:, 4, :], in0=rk[:, 3, :], scalar=2.0, in1=act[:, :], op0=ALU.add, op1=ALU.mult))
            dve.tensor_scalar(rk[:, 4, :], rk[:, 4, :], -1.0, None, ALU.add)
            dve.tensor_scalar(rk[:, 6, :], act[:, :], -1.0, 1.0, ALU.mult, ALU.add)
            then(dve.tensor_tensor(rk[:, 5, :], iota_g[:, :], rk[:, 3, :], ALU.subtract))
            then(dve.scalar_tensor_tensor(out=rk[:, 5, :], in0=rk[:, 5, :], scalar=1.0, in1=rk[:, 6, :], op0=ALU.add, op1=ALU.mult))
            dve.tensor_scalar(rk[:, 5, :], rk[:, 5, :], -1.0, None, ALU.add)
            then(dve.tensor_scalar(rk[:, 7, 0:1], rk[:, 2, GC - 1:GC], float(CG), None, ALU.add))
            then(dve.tensor_copy(rki[:, 0, 0:1], rk[:, 7, 0:1]))
            dve.tensor_scalar(counts_i[0:1, 0:1], rki[0:1, 0, 0:1], 3, None, ALU.arith_shift_right).then_inc(s_counts, 1)
            then(dve.tensor_scalar(rank_i[:, :], rk[:, 4, :], 0.0, None, ALU.max))
            dve.tensor_scalar(rki[:, 0, :], rank_i[:, :], CG - 1, None, ALU.bitwise_and)
            then(dve.tensor_scalar(rki[:, 1, :], rank_i[:, :], 3, None, ALU.arith_shift_right))
            dve.tensor_copy(rk[:, 8, :], rki[:, 0, :])
            then(dve.tensor_copy(rk[:, 9, :], rki[:, 1, :]))
            then(dve.scalar_tensor_tensor(out=rk[:, 9, :], in0=rk[:, 9, :], scalar=1.0, in1=act[:, :], op0=ALU.add, op1=ALU.mult))
            then(dve.tensor_scalar(rk[:, 9, :], rk[:, 9, :], -1.0, None, ALU.add))
            flat_q = iota_q[:, :, :].rearrange("p q r -> p (q r)")
            for t in range(GC):
                dve.tensor_scalar(pick_q[:, t, :], flat_q, rk[:, 8, t:t + 1], None, ALU.is_equal)
                dve.tensor_scalar(pick_c[:, t, :], iota_f[:, 0:COLS], rk[:, 9, t:t + 1], None, ALU.is_equal)
                dve.tensor_scalar(pick_z[:, t, :], iota_f[:, :], rk[:, 5, t:t + 1], iota_g[:, t:t + 1], ALU.is_equal, ALU.mult)
            dve.drain()

            def by_group(dst, t, values):
                return dve.tensor_tensor(dst[:, t, :].rearrange("p (q r) -> p q r", q=CG),
                                         pick_q[:, t, :].rearrange("p (q r) -> p q r", q=CG),
                                         values.rearrange("p (o r) -> p o r", o=1).to_broadcast([P, CG, GT]), ALU.mult)

            for t in range(GC):
                by_group(pick_v, t, v4[:, t, :])
                last = by_group(pick_t, t, tok_of[:, t, :])
            last.then_inc(s_picks, 1)
            dve.wait_ge(s_picks_mm, 1)
            dve.tensor_scalar(match_f[:, :], mm[0][:, 0:COLS], 0.0, None, ALU.is_gt)
            dve.tensor_scalar(pred_i[:, :], mm[0][:, 0:COLS], -1.0, 0.0, ALU.add, ALU.max)
            then(dve.tensor_copy(valid[:, :], mm[0][:, 2 * COLS:3 * COLS]))
            then(dve.tensor_scalar(place_v[:, :], valid[:, :], -NOWHERE, NOWHERE, ALU.mult, ALU.add))
            then(dve.tensor_tensor(tok_i[:, :], place_v[:, :], mm[0][:, COLS:2 * COLS], ALU.add))
            dve.memset(valid[0:GT, 0:1], 1.0)
            dve.tensor_copy(zlist[:, :], mm[0][:, 3 * COLS:3 * COLS + 1])
            dve.drain().then_inc(s_tables, 1)

            dve.sem_inc(s_dve_tiles, 6)
            dve.sem_inc(s_xf_ready, 1)
            n = dve.value_load(counts_i[0:1, 0:1], min_val=1, max_val=CHUNKS)

            def norm(dst, src, s, count):
                then(dve.bn_stats(s[:, 0:6], src))
                dve.bn_aggr(s[:, 6:8], s[:, 0:6]).then_inc(s_var_ready, 1)
                dve.wait_ge(s_dev_ready, count)
                return dve.tensor_scalar(dst, src, s[:, 6:7], s[:, 8:9], ALU.subtract, ALU.mult)

            def turned(dst, src=ps_m[:, D:D + 2 * P]):
                return dve.tensor_copy(dst[0:DH, :, :], src[0:DH, :].rearrange("p (h t) -> p h t", h=2))

            def embed(c, count):
                dve.wait_ge(s_emb_in, c * 16 + 16)
                then(dve.tensor_scalar(h_next[:, :], emb_t[:, :], match_f[:, bass.ds(c, 1)], None, ALU.mult))
                dve.sem_inc(s_emb_used, 1)
                norm(xn[:, :], h_next[:, :], st, count).then_inc(s_xn_ready, 1)

            def route_tail(c):
                dve.wait_ge(s_l_mm, c + 1)
                then(dve.tensor_reduce(rt[:, 0:1], ps_l, AX.X, ALU.max))
                dve.tensor_scalar(rt[:, 1:2], rt[:, 0:1], -1.0, None, ALU.mult).then_inc(s_lmax_ready, 1)
                dve.wait_ge(s_lexp_ready, c + 1)
                then(dve.reciprocal(rt[:, 3:4], rt[:, 2:3]))
                then(dve.tensor_scalar(rt[:, 16:24], rt[:, 8:16], rt[:, 3:4], None, ALU.mult))
                then(dve.tensor_reduce(rt[:, 4:5], rt[:, 16:24], AX.X, ALU.max))
                then(dve.tensor_scalar(rt[:, 24:32], rt[:, 16:24], rt[:, 4:5], float(E), ALU.is_lt, ALU.mult))
                dve.tensor_copy(prob_c[:, bass.ds(c, 1)], rt[:, 4:5])
                then(dve.tensor_tensor(rt[:, 24:32], rt[:, 24:32], iota_f[:, 0:E], ALU.add))
                dve.tensor_reduce(route_c[:, bass.ds(c, 1)], rt[:, 24:32], AX.X, ALU.min)

            embed(0, 1)
            dve.wait_ge(s_xt_mm, 1)
            turned(xt).then_inc(s_xt_ready, 1)
            with dve.Fori(0, n) as c:
                then(dve.tensor_copy(h_cur[:, :], h_next[:, :]))
                for i in range(4):
                    k = 4 + 2 * i
                    dve.wait_ge(s_tile_mm, c * 15 + k + 1)
                    dve.tensor_copy(kt[:, i % 2, :, 4 * (i // 2):4 * (i // 2) + 4, :].rearrange("p g j r -> p j g r"),
                                    mm[k % 4][0:DH, :].rearrange("p (j g r) -> p j g r", j=4, g=CG)).then_inc(s_dve_tiles, 1)
                    if i == 1:
                        embed(c + 1, c * 2 + 2)
                for half in range(2):
                    gs = slice(4 * half, 4 * half + 4)
                    dve.wait_ge(s_s_mm, c * 2 + half + 1)
                    then(dve.tensor_reduce(sm[:, 0, gs], ps_s[half][:, :].rearrange("p (g l) -> p g l", g=4), AX.X, ALU.max))
                    dve.tensor_scalar(sm[:, 1, gs], sm[:, 0, gs], -1.0, None, ALU.mult).then_inc(s_max_ready, 1)
                dve.wait_ge(s_xt_mm, c + 2)
                turned(xt).then_inc(s_xt_ready, 1)
                for half in range(2):
                    gs = slice(4 * half, 4 * half + 4)
                    dve.wait_ge(s_exp_ready, c * 2 + half + 1)
                    then(dve.tensor_scalar(sm[:, 3, gs], sm[:, 2, gs], float(D) ** 0.5, None, ALU.mult))
                    then(dve.reciprocal(sm[:, 3, gs], sm[:, 3, gs]))
                    if half == 0:
                        dve.wait_ge(s_xft_mm, c + 1)
                        turned(xft).then_inc(s_xft_ready, 1)
                    dve.tensor_tensor(ex[:, gs, :], ex[:, gs, :], sm[:, 3, gs].rearrange("p (g o) -> p g o", o=1).to_broadcast([P, 4, P]),
                                      ALU.mult).then_inc(s_p_ready, 1)
                route_tail(c)
                for i in range(2):
                    k = 12 + 2 * i
                    dve.wait_ge(s_tile_mm, c * 15 + k + 1)
                    dve.tensor_copy(ot[:, 1, :, 64 * i:64 * i + 64].rearrange("p j (g r) -> p g j r", r=GT),
                                    mm[k % 4][0:DH, :].rearrange("p (g j r) -> p g j r", g=4, j=HEADS)).then_inc(s_dve_tiles, 1)
                dve.wait_ge(s_y_mm, c + 2)
                dve.wait_ge(s_xf_out, c * 16 + 16)
                then(dve.tensor_tensor(h1, h_cur[:, :], ps_y, ALU.add))
                norm(xf, h1, st2, c * 2 + 3).then_inc(s_xf_ready, 1)
            dve.wait_ge(s_xft_mm, n + 1)
            turned(xft).then_inc(s_xft_ready, 1)
            route_tail(n)
            dve.drain().then_inc(s_probT_ready, 1)

            dve.wait_ge(s_probT_mm, 1)
            dve.tensor_copy(pT[:, :, 0, :], mm[1][0:CHUNKS, 0:P].rearrange("p (q r) -> p q r", q=CG))
            dve.tensor_copy(pT[:, :, 1, :], mm[1][0:CHUNKS, P:2 * P].rearrange("p (q r) -> p q r", q=CG))
            dve.drain().then_inc(s_probT_ready, 1)
            dve.wait_ge(s_p0_mm, 1)
            dve.wait_ge(s_zrow_in, 16)
            then(dve.tensor_copy(p0, mm[0][:, 0:1]))
            dve.scalar_tensor_tensor(out=bz, in0=xh0[:, 0:D], scalar=p0, in1=xh0[:, D:2 * D], op0=ALU.mult, op1=ALU.add).then_inc(s_bz_ready, 1)

            rc = route_c[:, 1:CHUNKS + 1]
            for e in range(E):
                dve.scalar_tensor_tensor(out=eqc[:, e, :], in0=rc, scalar=float(e), in1=valid[:, 0:CHUNKS], op0=ALU.is_equal, op1=ALU.mult)
            dve.memset(reset_c[:, :, :], 1.0)
            dve.memset(reset_r[:, :, :], 1.0)
            dve.drain().then_inc(s_eqc_ready, 1)
            dve.memset(reset_c[:, :, 0:1], 0.0)
            dve.memset(reset_r[:, :, 0:1], 0.0)
            dve.wait_ge(s_eqc_mm, 1)
            he = E // 2
            for i in range(2):
                dve.tensor_copy(csum[:, he * i:he * (i + 1), :].rearrange("p e c -> p (e c)"), mm[2 + i][:, 0:he * CHUNKS])
            dve.drain()
            then(dve.tensor_tensor_scan(cinc[:, :, :].rearrange("p e c -> p (e c)"), reset_c[:, :, :].rearrange("p e c -> p (e c)"),
                                        csum[:, :, :].rearrange("p e c -> p (e c)"), 0.0, ALU.mult, ALU.add))
            tot = cinc[:, :, CHUNKS - 1]
            dve.tensor_scalar(tl_i[:, 0, :], tot, float(P - 1), None, ALU.add)
            then(dve.tensor_tensor(posn[:, :, :], cinc[:, :, :], csum[:, :, :], ALU.subtract))
            then(dve.tensor_scalar(tl_i[:, 0, :], tl_i[:, 0, :], 7, None, ALU.arith_shift_right))
            then(dve.tensor_copy(tl[:, 0, :], tl_i[:, 0, :]))
            then(dve.tensor_tensor_scan(tl[:, 1, :], ones[:, 0:E], tl[:, 0, :], 0.0, ALU.mult, ALU.add))
            dve.tensor_copy(counts_i[0:1, 1:2], tl[0:1, 1, E - 1:E])
            then(dve.tensor_tensor(tl[:, 2, :], tl[:, 1, :], tl[:, 0, :], ALU.subtract))
            then(dve.tensor_scalar(tl[:, 3, :], tl[:, 2, :], float(P), None, ALU.mult))
            then(dve.tensor_tensor(tcmp[:, :, :], tl[0:1, 2, :].rearrange("p (o e) -> p o e", o=1).to_broadcast([1, TILES, E]),
                                   iota_f[0:1, 0:TILES].rearrange("p (t o) -> p t o", o=1).to_broadcast([1, TILES, E]), ALU.is_le))
            then(dve.tensor_reduce(texp, tcmp[:, :, :], AX.X, ALU.add))
            dve.tensor_scalar(expert_i[0:1, 0:TILES], texp, -1.0, None, ALU.add)
            then(dve.tensor_tensor(posn[:, :, :], posn[:, :, :], tl[:, 3, :].rearrange("p (e o) -> p e o", o=1).to_broadcast([P, E, CHUNKS]), ALU.add))
            for i in range(2):
                es = slice(he * i, he * (i + 1))
                dve.tensor_tensor(posn[:, es, :], posn[:, es, :], ps_s[i][:, 0:he * CHUNKS].rearrange("p (e c) -> p e c", e=he), ALU.add)
            dve.drain()
            then(dve.tensor_tensor(posn[:, :, :], posn[:, :, :], eqc[:, :, :], ALU.mult))
            dve.memset(slot_f[:, :], 0.0)
            dve.memset(sl_i[:, :, :], 0)
            dve.drain()
            then(dve.tensor_reduce(slot_f[:, 0:CHUNKS], posn[:, :, :].rearrange("p e c -> p c e"), AX.X, ALU.add))
            then(dve.tensor_copy(slot_i[:, :], slot_f[:, :]))
            dve.tensor_scalar(sl_i[:, 0, :], slot_i[:, :], P - 1, None, ALU.bitwise_and)
            dve.tensor_scalar(sl_i[:, 1, :], slot_i[:, :], 7, None, ALU.arith_shift_right)
            then(dve.tensor_scalar(place_v[:, :], valid[:, :], -NOWHERE, NOWHERE, ALU.mult, ALU.add))
            dve.tensor_tensor(slot_i[:, :], slot_f[:, :], place_v[:, :], ALU.add)
            dve.tensor_copy(slot_lo[:, :], sl_i[:, 0, :])
            then(dve.tensor_copy(slot_hi[:, :], sl_i[:, 1, :]))
            dve.sem_inc(s_slots_known, 1)

            dve.wait_ge(s_full_in, 16 * GC)
            fp = full[:, :, 0, :]
            fr = full[:, :, 1, :]

            def by_t(a):
                return a.rearrange("p (t r) -> p t r", t=GC)

            for e in range(E):
                dve.tensor_scalar(by_t(member[:, e, :]), fr, float(e), None, ALU.is_equal)
                dve.scalar_tensor_tensor(out=by_t(score[:, e, :]), in0=fr, scalar=float(e), in1=fp, op0=ALU.is_equal, op1=ALU.mult)
            dve.memset(thr, 0.0)
            dve.memset(step, 1.0)
            dve.drain()

            def per_expert(a):
                return a.rearrange("p (e o) -> p e o", o=1).to_broadcast([P, E, TR])

            with dve.Fori(0, 28) as k:
                then(dve.tensor_scalar(cand, thr, step, None, ALU.add))
                then(dve.tensor_tensor(cmp[:, :, :], score[:, :, :], per_expert(cand), ALU.is_ge))
                dve.tensor_reduce(red, cmp[:, :, :], AX.X, ALU.add).then_inc(s_red_ready, 1)
                dve.wait_ge(s_red_mm, k + 1)
                dve.tensor_scalar(step, step, 0.5, None, ALU.mult)
                then(dve.scalar_tensor_tensor(out=cand, in0=mm[1][:, 0:E], scalar=float(CAP), in1=cand, op0=ALU.is_ge, op1=ALU.mult))
                then(dve.tensor_tensor(thr, thr, cand, ALU.max))
            dve.tensor_tensor(cmp[:, :, :], score[:, :, :], per_expert(thr), ALU.is_gt)
            then(dve.tensor_tensor(tie[:, :, :], score[:, :, :], per_expert(thr), ALU.is_equal))
            dve.tensor_reduce(red, cmp[:, :, :], AX.X, ALU.add)
            then(dve.tensor_tensor(tie[:, :, :], tie[:, :, :], member[:, :, :], ALU.mult))
            dve.tensor_reduce(trow[:, :, :], tie[:, :, :].rearrange("p e (t r) -> p e t r", t=GC), AX.X, ALU.add)
            dve.drain().then_inc(s_tie_ready, 1)
            dve.tensor_tensor_scan(incl[:, :, :].rearrange("p e n -> p (e n)"), reset_r[:, :, :].rearrange("p n r -> p (n r)"),
                                   tie[:, :, :].rearrange("p e n -> p (e n)"), 0.0, ALU.mult, ALU.add)
            dve.wait_ge(s_tie_mm, 1)
            dve.tensor_scalar(rem, mm[1][:, 0:E], -1.0, float(CAP), ALU.mult, ALU.add)
            then(dve.tensor_copy(tsum[:, :, :].rearrange("p e t -> p (e t)"), mm[1][:, 128:128 + E * GC]))
            then(dve.tensor_copy(tbase[:, :, :].rearrange("p e t -> p (e t)"), mm[1][:, 64:64 + E * GC]))
            for t in range(1, GC):
                for u in range(t):
                    then(dve.tensor_tensor(tbase[:, :, t:t + 1], tbase[:, :, t:t + 1], tsum[:, :, u:u + 1], ALU.add))
            for t in range(GC):
                ts_ = slice(GT * t, GT * (t + 1))
                dve.tensor_tensor(incl[:, :, ts_], incl[:, :, ts_], tbase[:, :, t:t + 1].to_broadcast([P, E, GT]), ALU.add)
            dve.drain()
            then(dve.tensor_tensor(incl[:, :, :], incl[:, :, :], per_expert(rem), ALU.is_le))
            then(dve.tensor_tensor(tie[:, :, :], tie[:, :, :], incl[:, :, :], ALU.mult))
            then(dve.tensor_tensor(cmp[:, :, :], cmp[:, :, :], tie[:, :, :], ALU.add))
            then(dve.tensor_reduce(keep, cmp[:, :, :].rearrange("p e n -> p n e"), AX.X, ALU.add))
            then(dve.tensor_tensor(by_t(keep_z[:, 0:TR]), by_t(keep), rk[:, 6, :].rearrange("p (t o) -> p t o", o=1).to_broadcast([P, GC, GT]), ALU.mult))
            dve.tensor_reduce(keep_z[:, TR:TR + 1], keep_z[:, 0:TR], AX.X, ALU.add)
            for t in range(GC):
                by_group(pick_k, t, keep[:, GT * t:GT * (t + 1)])
            dve.drain().then_inc(s_keep_ready, 1)
            dve.wait_ge(s_keep_mm, 1)
            dve.tensor_copy(zs[:, 0:1], mm[1][:, 256:257])
            then(dve.tensor_copy(keep_c[:, :], mm[1][:, 300:300 + COLS]))
            then(dve.tensor_tensor(scale_o[:, 0:CHUNKS], keep_c[:, 0:CHUNKS], prob_c[:, 1:CHUNKS + 1], ALU.mult))
            dve.tensor_tensor(scale_x[:, 0:CHUNKS], prob_c[:, 1:CHUNKS + 1], scale_o[:, 0:CHUNKS], ALU.subtract)
            then(dve.tensor_scalar(zk[:, 0, :], iota_z[:, :], zs[:, 0:1], None, ALU.is_lt))
            dve.tensor_scalar(zk[:, 1, :], zk[:, 0, :], -1.0, 1.0, ALU.mult, ALU.add)
            then(dve.tensor_scalar(zs[:, 3:4], zk[:, 0, 0:1], -NOWHERE, NOWHERE, ALU.mult, ALU.add))
            then(dve.scalar_tensor_tensor(out=zs_i[:, 0:1], in0=zk[:, 0, 0:1], scalar=zlist[:, 0:1], in1=zs[:, 3:4], op0=ALU.mult, op1=ALU.add))
            then(dve.tensor_scalar(tok_v[:, :], tok_i[:, :], -1.0, NOWHERE, ALU.mult, ALU.add))
            dve.memset(lists[:, :, :], 0.0)
            with dve.Fori(0, n) as c:
                for i, values in enumerate((tok_v, scale_o, scale_x)):
                    dve.tensor_scalar(row_of[:, i, :], iota_f[:, :], slot_lo[:, bass.ds(c, 1)], values[:, bass.ds(c, 1)], ALU.is_equal, ALU.mult)
                dve.tensor_scalar(tile_of, iota_f[:, 0:COLS], slot_hi[:, bass.ds(c, 1)], valid[:, bass.ds(c, 1)], ALU.is_equal, ALU.mult)
                dve.drain().then_inc(s_lists_ready, 1)
                dve.wait_ge(s_lists_mm, c + 1)
                then(dve.tensor_tensor(lists[:, :, :].rearrange("p a c -> p (a c)"), lists[:, :, :].rearrange("p a c -> p (a c)"),
                                       mm[0][:, 0:3 * COLS], ALU.add))
            dve.tensor_scalar(list_i[:, :], lists[:, 0, :], -1.0, NOWHERE, ALU.mult, ALU.add)
            dve.drain().then_inc(s_lists_read, 1)
            for r_ in range(GT):
                dve.tensor_scalar(zt[:, r_, :], bz, zk[:, 1, r_:r_ + 1], None, ALU.mult)

            dve.memset(gxt[DH:DH + 1, 0, :], 1.0)
            dve.drain()
            m = dve.value_load(counts_i[0:1, 1:2], min_val=1, max_val=TILES)
            with dve.Fori(0, m) as t:
                dve.wait_ge(s_gxt_mm, t + 2)
                turned(gxt, ps_s[0][:, 0:2 * P]).then_inc(s_gxt_ready, 1)
                dve.wait_ge(s_ht_mm, t * 2 + 3)
                dve.tensor_copy(ht[:, 0:3, :].rearrange("p c t -> p (c t)"), mm[2][:, 0:384]).then_inc(s_ht_dve, 1)
                dve.wait_ge(s_o_mm, t + 1)
                dve.wait_ge(s_o_out, t * 16 + 16)
                dve.tensor_copy(ob, ps_y).then_inc(s_ob_ready, 1)

            dve.wait_ge(s_oz_in, 16)
            then(dve.scalar_tensor_tensor(out=az, in0=oz, scalar=p0, in1=xh0[:, D:2 * D], op0=ALU.mult, op1=ALU.add))
            for r_ in range(GT):
                dve.scalar_tensor_tensor(out=zt[:, r_, :], in0=az, scalar=zk[:, 0, r_:r_ + 1], in1=zt[:, r_, :], op0=ALU.mult, op1=ALU.add)
            dve.drain().then_inc(s_zt_ready, 1)
            with dve.Fori(0, m) as t:
                dve.wait_ge(s_cx_in, t * 32 + 32)
                dve.wait_ge(s_yo_free, t + 1)
                then(dve.scalar_tensor_tensor(out=yo, in0=og, scalar=lists[:, 1, bass.ds(t, 1)], in1=xg[:, D:2 * D], op0=ALU.mult, op1=ALU.add))
                dve.scalar_tensor_tensor(out=yo, in0=xg[:, 0:D], scalar=lists[:, 2, bass.ds(t, 1)], in1=yo, op0=ALU.mult, op1=ALU.add).then_inc(s_y_ready, 1)
            dve.nop()

_INS = ["x", "L0_tok_emb", "L0_attn_W_qkv", "L0_attn_b_qkv", "L0_attn_W_proj", "L0_attn_b_proj",
        "L0_ffn_switch_w", "L0_ffn_switch_b", "L0_ffn_w1", "L0_ffn_b1", "L0_ffn_w2", "L0_ffn_b2"]

def kernel(**inputs):
    import numpy as _np
    import concourse.bacc as _bacc
    from concourse.bass_utils import run_bass_kernel_spmd as _run

    nc = _bacc.Bacc("TRN2", target_bir_lowering=False, num_devices=1)
    arrays, args = {}, []
    for name in _INS:
        a = _np.ascontiguousarray(inputs[name])
        arrays[f"in_{name}"] = a
        args.append(nc.dram_tensor(f"in_{name}", a.shape, mybir.dt.from_np(a.dtype), kind="ExternalInput").ap())
    args.append(nc.dram_tensor("out_0", (B, T, D), F32, kind="ExternalOutput").ap())
    build(nc, *args)
    r = _run(nc, [arrays], core_ids=[0])
    return r.results[0]["out_0"]
```

```python
from contextlib import ExitStack

import concourse.bass as bass
from concourse import mybir

ALU = mybir.AluOpType
ACT = mybir.ActivationFunctionType
AX = mybir.AxisListType
F32 = mybir.dt.float32
BF16 = mybir.dt.bfloat16
I32 = mybir.dt.int32

P = 128
B, T = 64, 128
N = B * T
D = 192
HEADS = 8
HD = HEADS * D
DH = D // 2
GT = T // HEADS
G = N // GT
GC = G // P
CG = P // GT
UNIT = 4
CU = P // UNIT
BU = GT // UNIT
CHUNKS = (G + 1 + CG - 1) // CG
OC = BU * CHUNKS
COLS = 80
E = 8
F = 768
FC = F // P
CAP = int(1.25 * N / E)
TILES = (CHUNKS * P + E * (P - 1)) // P
FOUR = 4
PROBES = 28
EARLY = 6
ROW = D + 4
FILLS = 8
EPS = 1e-5
NOWHERE = 65536.0
VOCAB_PAD = -1.0
assert TILES + FOUR <= COLS and CHUNKS + 1 + FOUR <= COLS

def build(nc, x, emb, w_qkv, b_qkv, w_proj, b_proj, sw, sb_, w1, b1, w2, b2, out):
    ctx = ExitStack()
    with ctx:
        def sb(name, shape, dt=F32):
            return ctx.enter_context(nc.sbuf_tensor(name, shape, dt))

        def sem(name):
            return ctx.enter_context(nc.semaphore(name))

        pred_d = nc.dram_tensor("pred_d", (N,), F32, kind="Internal").ap()
        prob_d = nc.dram_tensor("prob_d", (CHUNKS * CU, 2 * GT), F32, kind="Internal").ap()
        xh_d = nc.dram_tensor("xh_d", ((CHUNKS + FOUR) * P, 2 * D), F32, kind="Internal").ap()
        xs_d = nc.dram_tensor("xs_d", ((TILES + E + FOUR) * P, ROW), F32, kind="Internal").ap()
        o_d = nc.dram_tensor("o_d", (CHUNKS * P, D), F32, kind="Internal").ap()
        v_d = nc.dram_tensor("v_d", (P, HD), F32, kind="Internal").ap()
        x_rows = x.rearrange("b (t o) -> (b t) o", o=1)
        out_rows = out.rearrange("b t d -> (b t) d")
        out_groups = out.rearrange("b (g r) d -> (b g) (r d)", r=GT)

        area = sb("area", [P, 2 * 3 * HD])
        wqkv_s = area[0:DH + 1, :].rearrange("p (h n) -> p h n", h=2)
        wproj_s = sb("wproj_s", [DH, 2 * HEADS, D])
        bproj_s = sb("bproj_s", [1, D])
        wsw_s = sb("wsw_s", [DH + 1, 2, E])
        w1_s = sb("w1_s", [DH + 1, 2, E, F])
        w2_s = sb("w2_s", [P, FC, E, D])
        WORK = 11264
        work = sb("work", [P, WORK])

        ident = sb("ident", [P, P])
        ones = sb("ones", [P, P])
        before = sb("before", [P, P])
        first = sb("first", [P, P])
        iota_f = sb("iota_f", [P, P])
        iota_q = sb("iota_q", [P, CG, GT])
        iota_g = sb("iota_g", [P, GC])
        iota_z = sb("iota_z", [P, GT])
        iota_u = sb("iota_u", [P, CU, UNIT])
        iota_k = sb("iota_k", [P, GT])
        iota_k1 = sb("iota_k1", [P, GT])
        iota_o = sb("iota_o", [P, OC])
        iota_b = sb("iota_b", [UNIT, CHUNKS * CG])
        tok_of = sb("tok_of", [P, GC, GT])
        place_of = sb("place_of", [P, COLS])
        units = sb("units", [UNIT, HEADS, GT], BF16)
        others = sb("others", [UNIT, HEADS, GT], BF16)
        pred_base = sb("pred_base", [B, T])
        minus_half = sb("minus_half", [P, 1])
        match_j = sb("match_j", [P, B])

        pred_i = sb("pred_i", [P, COLS], I32)
        match_f = sb("match_f", [P, COLS])
        mult_c = sb("mult_c", [P, COLS])
        valid = sb("valid", [P, COLS])
        prob_c = sb("prob_c", [P, COLS])
        route_c = sb("route_c", [P, COLS])
        not_big = sb("not_big", [UNIT, CHUNKS * CG])
        out_tok = sb("out_tok", [P, OC], I32)
        out_place = sb("out_place", [P, OC])
        out_keep = sb("out_keep", [P, OC])
        slot_f = sb("slot_f", [P, COLS])
        slot_i = sb("slot_i", [P, COLS], I32)
        place_v = sb("place_v", [P, COLS])
        zero = sb("zero", [P, 2 * D])
        ones_b = sb("ones_b", [P, P], BF16)
        idx_4 = sb("idx_4", [P, FOUR], I32)
        expert_i = sb("expert_i", [1, COLS], I32)
        zlist = sb("zlist", [P, 1])
        counts_i = sb("counts_i", [1, 3], I32)
        pick_c = sb("pick_c", [P, GC, COLS])
        classes = sb("classes", [P, 2, GC])
        act = sb("act", [P, GC])
        place_k = sb("place_k", [P, GC, GT])
        unit_i = sb("unit_i", [P, GC], I32)

        idx_a = sb("idx_a", [P, 1], I32)
        tid = sb("tid", [P, 1], I32)
        emb_t = sb("emb_t", [P, D])
        h_next = sb("h_next", [P, D])
        h_cur = sb("h_cur", [P, D])
        xn = sb("xn", [P, D])
        xh = sb("xh", [P, 2 * D])
        xf = xh[:, 0:D]
        h1 = xh[:, D:2 * D]
        xt = sb("xt", [DH + 1, 2, P])
        xft = sb("xft", [DH + 1, 2, P])
        st = sb("st", [P, 12])
        st2 = sb("st2", [P, 12])
        rt = sb("rt", [P, 64])
        sm = sb("sm", [P, 4, CG])
        rk = sb("rk", [P, 24, GC])
        rki = sb("rki", [P, 6, GC], I32)
        mrow = sb("mrow", [P, P])
        mdiag = sb("mdiag", [P, P])
        sides = sb("sides", [UNIT, CG, HEADS, GT], BF16)
        pl = sb("pl", [P, 2])

        banks = [ctx.enter_context(nc.psum_tensor(f"bank{i}", [P, 512], F32)) for i in range(8)]
        mm = banks[0:4]
        ps_s = banks[4:6]
        ps_t = banks[6]
        ps_m = banks[7]
        ps_y = ps_m[:, 0:D]
        ps_x = ps_m[:, D:D + P]
        ps_x2 = ps_m[:, D + P:D + 2 * P]
        ps_l = ps_m[:, D + 2 * P:D + 2 * P + E]

        RB = 8
        NB = B // RB
        starts = [T - 16 * (k + 1) for k in range(NB)]
        lens = [T - s for s in starts]
        offs = [RB * sum(lens[:k]) for k in range(NB + 1)]
        XW = 2 * T + 2

        TR = GC * GT
        used = [0]

        def cut(base, n):
            a = used[0]
            used[0] += n
            assert used[0] <= base.shape[1]
            return base[:, a:a + n]

        eq = cut(work, offs[-1])
        run = cut(work, offs[-1])
        x_i = cut(work, T).bitcast(I32)
        x_f = cut(work, T)
        x_pad_at = used[0]
        x_pad = cut(work, XW)
        best = cut(work, T)
        tmp_b = cut(work, T)
        tmp_i = cut(work, T).bitcast(I32)
        v4 = cut(work, N // P).rearrange("p (t r) -> p t r", t=GC)
        used[0] = 0
        v16 = cut(work, TR).rearrange("p (t k) -> p t k", t=GC)
        m16 = cut(work, TR).rearrange("p (t k) -> p t k", t=GC)
        m16b = cut(work, TR).rearrange("p (t k) -> p t k", t=GC)
        m4 = cut(work, TR).rearrange("p (t r) -> p t r", t=GC)
        cum = cut(work, TR).rearrange("p (t r) -> p t r", t=GC)
        reset_g = cut(work, TR).rearrange("p (t r) -> p t r", t=GC)
        spread = cut(work, TR * GT).rearrange("p (t k r) -> p t k r", t=GC, k=GT)
        pick_s = cut(work, GC * P).rearrange("p (t m) -> p t m", t=GC)
        pick_b = cut(work, GC * P).rearrange("p (t m) -> p t m", t=GC)
        pick_v = cut(work, GC * P).rearrange("p (t m) -> p t m", t=GC)
        pick_m = cut(work, GC * P).rearrange("p (t m) -> p t m", t=GC)
        pick_x = cut(work, GC * P).rearrange("p (t m) -> p t m", t=GC)
        pick_z = cut(work, GC * P).rearrange("p (t m) -> p t m", t=GC)
        assert used[0] <= 2 * offs[-1]

        used[0] = 0
        qt = cut(work, 2 * HEADS * P)[0:DH, :].rearrange("p (h g j r) -> p h g j r", h=2, g=CG, j=HEADS)
        kt = cut(work, 2 * HEADS * P)[0:DH, :].rearrange("p (h g j r) -> p h g j r", h=2, g=CG, j=HEADS)
        vn = cut(work, HD)
        vp = cut(work, CG * D).rearrange("p (g v) -> p g v", g=CG)
        ex = cut(work, CG * P).rearrange("p (g l) -> p g l", g=CG)
        pt = cut(work, CG * P).rearrange("p (g l) -> p g l", g=CG)
        ot = cut(work, 2 * HEADS * P)[0:DH, :].rearrange("p (h j t) -> p h j t", h=2, j=HEADS)

        used[0] = 0
        gx = cut(work, ROW)
        gxt = cut(work, 2 * P)[0:DH + 1, :].rearrange("p (h t) -> p h t", h=2)
        hs = cut(work, F)
        ht = cut(work, F).rearrange("p (c t) -> p c t", c=FC)
        ob = cut(work, D)
        b2_s = cut(work, E * D)[0:1, :].rearrange("p (e d) -> p e d", e=E)
        sx = cut(work, FOUR * ROW).rearrange("p (a n) -> p a n", a=FOUR)
        xg = cut(work, 2 * D)
        og = cut(work, D)
        rd = cut(work, 2 * D)
        sel_t = hs[:, 0:BU * P].rearrange("p (s m) -> p s m", s=BU)
        sel = ht[:, 0:BU, :]
        yo = cut(work, BU * D).rearrange("p (s n) -> p s n", s=BU)
        step_cols = cut(work, 2 * BU).rearrange("p (w s) -> p w s", w=2)
        xh0 = cut(work, 2 * D)
        bz = cut(work, D)
        az = cut(work, D)
        oz = cut(work, D)
        zt = cut(work, GT * D).rearrange("p (r d) -> p r d", r=GT)
        zk = cut(work, 2 * GT).rearrange("p (a r) -> p a r", a=2)
        p0 = cut(work, 1)
        zs = cut(work, 4)
        zs_i = cut(work, 2).bitcast(I32)

        used[0] = 0
        full = cut(area, GC * 2 * GT).rearrange("p (t w r) -> p t w r", t=GC, w=2)
        pT = cut(area, 2 * (P + GT))[0:CHUNKS, :].rearrange("p (w m) -> p w m", w=2)
        pT_at = GC * 2 * GT
        pTx = cut(area, CU * 2 * GT)[0:CHUNKS, :].rearrange("p (u w k) -> p u w k", u=CU, w=2)
        at_slots = used[0]
        member = cut(area, E * TR).rearrange("p (e n) -> p e n", e=E)
        score = cut(area, E * TR).rearrange("p (e n) -> p e n", e=E)
        at_cmp = used[0]
        cmp = cut(area, E * TR).rearrange("p (e n) -> p e n", e=E)
        tie = cut(area, E * TR).rearrange("p (e n) -> p e n", e=E)
        at_incl = used[0]
        incl = cut(area, E * TR).rearrange("p (e n) -> p e n", e=E)
        room = cut(area, E * TR)
        reset_r = cut(area, E * TR).rearrange("p (n r) -> p n r", r=GT)
        thr = cut(area, E)
        cand = cut(area, E)
        red = cut(area, E)
        rem = cut(area, E)
        step = cut(area, 1)
        trow = cut(area, E * GC).rearrange("p (e t) -> p e t", e=E)
        tbase = cut(area, E * GC).rearrange("p (e t) -> p e t", e=E)
        tsum = cut(area, E * GC).rearrange("p (e t) -> p e t", e=E)
        keep = cut(area, TR)
        keep_z = cut(area, TR + 1)
        pick_k = incl[:, :, :].rearrange("p e n -> p (e n)").rearrange("p (t m) -> p t m", t=GC)
        pick_s2 = tie[:, :, :].rearrange("p e n -> p (e n)").rearrange("p (t m) -> p t m", t=GC)
        pick_u = cut(area, GC * P).rearrange("p (t m) -> p t m", t=GC)
        pick_o = cut(area, GC * OC).rearrange("p (t n) -> p t n", t=GC)
        tl = cut(area, 8 * E).rearrange("p (a e) -> p a e", a=8)
        tl_i = cut(area, 2 * E).bitcast(I32).rearrange("p (a e) -> p a e", a=2)
        tcmp = cut(area, TILES * E).rearrange("p (t e) -> p t e", e=E)[0:1]
        texp = cut(area, TILES)[0:1, :]
        slot_v = cut(area, TR)
        hit = cut(area, E * TR // 2).bitcast(BF16).rearrange("p (e n) -> p e n", e=E)
        used[0] = at_slots
        reset_c = cut(area, E * CHUNKS).rearrange("p (e c) -> p e c", e=E)
        eqc = cut(area, E * CHUNKS).rearrange("p (e c) -> p e c", e=E)
        csum = cut(area, E * CHUNKS).rearrange("p (e c) -> p e c", e=E)
        cinc = cut(area, E * CHUNKS).rearrange("p (e c) -> p e c", e=E)
        posn = cut(area, E * CHUNKS).rearrange("p (e c) -> p e c", e=E)
        assert used[0] <= at_incl + 2 * E * TR
        at_place = area[:, at_cmp:at_cmp + TR * GT].rearrange("p (n k) -> p n k", k=GT)
        at_work = area[:, at_incl:at_incl + TR * GT].rearrange("p (n k) -> p n k", k=GT)

        s_act_ready = sem("s_act_ready")
        s_act_tiles = sem("s_act_tiles")
        s_b2_in = sem("s_b2_in")
        s_best_out = sem("s_best_out")
        s_bz_ready = sem("s_bz_ready")
        s_consts = sem("s_consts")
        s_counts = sem("s_counts")
        s_cx_in = sem("s_cx_in")
        s_dev_ready = sem("s_dev_ready")
        s_dve_tiles = sem("s_dve_tiles")
        s_emb_in = sem("s_emb_in")
        s_emb_used = sem("s_emb_used")
        s_eqc_mm = sem("s_eqc_mm")
        s_eqc_ready = sem("s_eqc_ready")
        s_exp_ready = sem("s_exp_ready")
        s_fill_out = sem("s_fill_out")
        s_full_in = sem("s_full_in")
        s_gx_in = sem("s_gx_in")
        s_gxt_mm = sem("s_gxt_mm")
        s_gxt_ready = sem("s_gxt_ready")
        s_h_mm = sem("s_h_mm")
        s_hit_mm = sem("s_hit_mm")
        s_hit_ready = sem("s_hit_ready")
        s_hs_ready = sem("s_hs_ready")
        s_ht_act = sem("s_ht_act")
        s_ht_dve = sem("s_ht_dve")
        s_ht_mm = sem("s_ht_mm")
        s_id_in = sem("s_id_in")
        s_idx_set = sem("s_idx_set")
        s_keep_mm = sem("s_keep_mm")
        s_keep_ready = sem("s_keep_ready")
        s_l_mm = sem("s_l_mm")
        s_lexp_ready = sem("s_lexp_ready")
        s_lmax_ready = sem("s_lmax_ready")
        s_max_ready = sem("s_max_ready")
        s_mdiag = sem("s_mdiag")
        s_mrow_mm = sem("s_mrow_mm")
        s_mrow_ready = sem("s_mrow_ready")
        s_o_clear = sem("s_o_clear")
        s_o_done = sem("s_o_done")
        s_o_mm = sem("s_o_mm")
        s_o_out = sem("s_o_out")
        s_ob_ready = sem("s_ob_ready")
        s_ob_stored = sem("s_ob_stored")
        s_oz_in = sem("s_oz_in")
        s_p0_mm = sem("s_p0_mm")
        s_p_ready = sem("s_p_ready")
        s_picks = sem("s_picks")
        s_picks_mm = sem("s_picks_mm")
        s_pool_steps = sem("s_pool_steps")
        s_pred_back = sem("s_pred_back")
        s_probT_mm = sem("s_probT_mm")
        s_probT_ready = sem("s_probT_ready")
        s_prob_out = sem("s_prob_out")
        s_pt_mm = sem("s_pt_mm")
        s_pt_ready = sem("s_pt_ready")
        s_rank_mm = sem("s_rank_mm")
        s_rd_ready = sem("s_rd_ready")
        s_row_mm = sem("s_row_mm")
        s_s_mm = sem("s_s_mm")
        s_sel_mm = sem("s_sel_mm")
        s_sel_ready = sem("s_sel_ready")
        s_selt_ready = sem("s_selt_ready")
        s_sides = sem("s_sides")
        s_slots_known = sem("s_slots_known")
        s_small_in = sem("s_small_in")
        s_sp_steps = sem("s_sp_steps")
        s_steps_mm = sem("s_steps_mm")
        s_steps_ready = sem("s_steps_ready")
        s_sx_free = sem("s_sx_free")
        s_sx_in = sem("s_sx_in")
        s_tables = sem("s_tables")
        s_tie_mm = sem("s_tie_mm")
        s_tie_ready = sem("s_tie_ready")
        s_tile_mm = sem("s_tile_mm")
        s_v_copied = sem("s_v_copied")
        s_v_moved = sem("s_v_moved")
        s_v_stored = sem("s_v_stored")
        s_var_ready = sem("s_var_ready")
        s_w1_in = sem("s_w1_in")
        s_w2_in = sem("s_w2_in")
        s_wproj_in = sem("s_wproj_in")
        s_wqkv_in = sem("s_wqkv_in")
        s_x_in = sem("s_x_in")
        s_xf_out = sem("s_xf_out")
        s_xf_ready = sem("s_xf_ready")
        s_xft_mm = sem("s_xft_mm")
        s_xft_ready = sem("s_xft_ready")
        s_xh_clear = sem("s_xh_clear")
        s_xn_ready = sem("s_xn_ready")
        s_xs_clear = sem("s_xs_clear")
        s_xs_done = sem("s_xs_done")
        s_xs_out = sem("s_xs_out")
        s_xt_mm = sem("s_xt_mm")
        s_xt_ready = sem("s_xt_ready")
        s_y_mm = sem("s_y_mm")
        s_y_out = sem("s_y_out")
        s_y_ready = sem("s_y_ready")
        s_yo_free = sem("s_yo_free")
        s_z_out = sem("s_z_out")
        s_zrow_in = sem("s_zrow_in")
        s_zt_ready = sem("s_zt_ready")

        block = ctx.enter_context(nc.Block())

        @block.sync
        def _(sp):
            sp.sem_inc(s_v_moved, 128)
            sp.sem_inc(s_xf_out, 16)
            sp.sem_inc(s_y_mm, 1)
            sp.sem_inc(s_pt_ready, 1)
            sp.sem_inc(s_emb_used, 1)
            sp.sem_inc(s_ob_stored, 1)
            sp.sem_inc(s_rd_ready, 1)
            sp.sem_inc(s_sx_free, 1)
            sp.sem_inc(s_yo_free, 1)
            sp.dma_start(x_i[0:B, :], x).then_inc(s_x_in, 16)
            sp.dma_start(x_i[B:2 * B, :], x).then_inc(s_x_in, 16)
            sp.dma_start(wqkv_s[0:DH, 0, :], w_qkv[0:DH, :]).then_inc(s_wqkv_in, 16)
            sp.dma_start(wqkv_s[0:DH, 1, :], w_qkv[DH:D, :]).then_inc(s_wqkv_in, 16)
            sp.dma_start(wqkv_s[DH:DH + 1, 0, :], b_qkv.rearrange("(o n) -> o n", o=1)).then_inc(s_wqkv_in, 16)
            sp.wait_ge(s_best_out, 1)
            sp.dma_start(pred_d.rearrange("(b t) -> b t", t=T), best[0:B, :]).then_inc(s_pred_back, 16)
            sp.wait_ge(s_pred_back, 16)
            sp.dma_start(v4, pred_d.rearrange("(t p r) -> p t r", t=GC, r=GT)).then_inc(s_pred_back, 16)
            for f in range(FC):
                sp.dma_start(w2_s[:, f, :, :], w2.rearrange("e (c p) d -> c p e d", p=P)[f]).then_inc(s_w2_in, 16)

            sp.wait_ge(s_counts, 1)
            n = sp.value_load(counts_i[0:1, 0:1], min_val=1, max_val=CHUNKS)
            sp.dma_start(xh_d[bass.ds(n * P, FOUR * P), :].rearrange("(a p) d -> p a d", p=P),
                         zero[:, 0:2 * D].rearrange("p (a d) -> p a d", a=1).to_broadcast([P, FOUR, 2 * D])).then_inc(s_xh_clear, 16)
            with sp.Fori(0, n) as c:
                sp.dma_start(o_d[bass.ds(c * P, P), :], zero[:, 0:D]).then_inc(s_o_clear, 16)
            with sp.Fori(0, n + E + FOUR) as t:
                sp.dma_start(xs_d[bass.ds(t * P, P), :], zero[:, 0:ROW]).then_inc(s_xs_clear, 16)
            with sp.Fori(0, n) as c:
                sp.wait_ge(s_v_copied, c + 1)
                sp.sem_inc(s_sp_steps, 1)
                sp.wait_ge(s_y_mm, c + 1)
                sp.sem_inc(s_sp_steps, 1)
                sp.dma_start(v_d, vn).then_inc(s_v_stored, 16)
                sp.wait_ge(s_v_stored, c * 16 + 16)
                sp.sem_inc(s_sp_steps, 1)
                for j in range(HEADS):
                    sp.dma_start(vp[GT * j:GT * (j + 1), :, :],
                                 v_d[:, j * D:(j + 1) * D].rearrange("(g r) v -> r g v", r=GT)).then_inc(s_v_moved, 16)
                sp.wait_ge(s_xf_ready, c + 2)
                sp.sem_inc(s_sp_steps, 1)
                sp.dma_start(xh_d[bass.ds(c * P, P), :], xh[:, :]).then_inc(s_xf_out, 16)
                sp.wait_ge(s_xf_out, c * 16 + 32)
                sp.sem_inc(s_sp_steps, 1)

            sp.wait_ge(s_xh_clear, 16)
            sp.dma_start(xh0, xh_d[0:1, :].to_broadcast([P, 2 * D])).then_inc(s_zrow_in, 16)
            sp.dma_start(b2_s[0:1, :, :], b2.rearrange("(o e) d -> o e d", o=1)).then_inc(s_b2_in, 16)
            sp.wait_ge(s_probT_ready, 2)
            sp.dma_start(prob_d.rearrange("(c u) n -> c u n", u=CU),
                         pTx[:, :, :, :].rearrange("c u w k -> c u (w k)")).then_inc(s_prob_out, 16)
            with sp.Fori(0, n, FOUR) as c:
                sp.wait_ge(s_sx_free, c + 1)
                sp.sem_inc(s_sp_steps, 1)
                sp.dma_start(sx[:, :, 0:D], xh_d[bass.ds(c * P, FOUR * P), 0:D].rearrange("(a p) d -> p a d", p=P)).then_inc(s_sx_in, 16)
            sp.wait_ge(s_slots_known, 1)
            m = sp.value_load(counts_i[0:1, 1:2], min_val=1, max_val=TILES)
            sp.wait_ge(s_xs_done, 1)
            sp.dma_start(gx, xs_d[0:P, :]).then_inc(s_gx_in, 16)
            with sp.Fori(0, m) as t:
                sp.wait_ge(s_gxt_ready, t + 1)
                sp.sem_inc(s_sp_steps, 1)
                sp.dma_start(gx, xs_d[bass.ds(t * P + P, P), :]).then_inc(s_gx_in, 16)
            sp.wait_ge(s_o_done, 1)
            sp.dma_start(oz, o_d[0:1, :].to_broadcast([P, D])).then_inc(s_oz_in, 16)
            with sp.Fori(0, n) as c:
                sp.wait_ge(s_rd_ready, c + 1)
                sp.sem_inc(s_sp_steps, 1)
                sp.dma_start(og, o_d[bass.ds(c * P, P), :]).then_inc(s_cx_in, 16)
                sp.dma_start(xg, xh_d[bass.ds(c * P, P), :]).then_inc(s_cx_in, 16)
            sp.nop()

        @block.gpsimd
        def _(pool):
            pool.memset(ones[:, :], 1.0)
            pool.memset(ident[:, :], 0.0)
            pool.memset(first[:, :], 0.0)
            pool.drain()
            pool.memset(first[0:1, :], 1.0)
            pool.affine_select(out=ident[:, :], in_=ident[:, :], compare_op=ALU.not_equal, fill=1.0, base=0,
                               pattern=[[-1, P]], channel_multiplier=1)
            pool.affine_select(out=before[:, :], in_=ones[:, :], compare_op=ALU.is_gt, fill=0.0, base=0,
                               pattern=[[1, P]], channel_multiplier=-1)

            def iota(out_, pattern, base, mult):
                return pool.iota(out_, pattern, base=base, channel_multiplier=mult, allow_small_or_imprecise_dtypes=True)

            pool.drain()
            iota(match_j[0:B, :], [[2, B]], 1, 0)
            iota(match_j[B:2 * B, :], [[2, B]], 0, 0)
            pool.drain()
            iota(pred_base[:, :], [[1, T]], 2 - T, T)
            iota(iota_f[:, :], [[1, P]], 0, 0)
            iota(iota_q[:, :, :], [[1, CG], [0, GT]], 0, 0)
            iota(iota_g[:, :], [[P, GC]], 0, 1)
            iota(iota_z[:, :], [[1, GT]], 0, GT)
            iota(iota_u[:, :, :], [[1, CU], [0, UNIT]], 0, 0)
            iota(iota_k[:, :], [[1, GT]], 0, 0)
            iota(iota_k1[:, :], [[1, GT]], 1, 0)
            iota(iota_o[:, :], [[1, OC]], 0, 0)
            iota(tok_of[:, :, :], [[-P * GT, GC], [-1, GT]], int(NOWHERE), -GT)
            iota(place_of[:, :], [[-P, COLS]], int(NOWHERE), -1)
            pool.drain()
            iota(iota_b[:, :], [[1, CHUNKS * CG]], 0, 0)
            pool.memset(units[:, :, :], 1.0)
            pool.memset(others[:, :, :], -1e30)
            pool.drain()
            pool.affine_select(out=units[:, :, :], in_=units[:, :, :], compare_op=ALU.is_ge, fill=0.0, base=0,
                               pattern=[[0, HEADS], [1, GT]], channel_multiplier=-UNIT)
            pool.drain()
            pool.affine_select(out=units[:, :, :], in_=units[:, :, :], compare_op=ALU.is_ge, fill=0.0, base=UNIT - 1,
                               pattern=[[0, HEADS], [-1, GT]], channel_multiplier=UNIT)
            pool.drain()
            pool.tensor_tensor(sides[:, 0, :, :], others[:, :, :], units[:, :, :], ALU.mult)
            pool.drain()
            pool.tensor_tensor(others[:, :, :], others[:, :, :], sides[:, 0, :, :], ALU.subtract)
            pool.drain()
            pool.memset(xt[DH:DH + 1, 0, :], 1.0)
            pool.memset(xft[DH:DH + 1, 0, :], 1.0)
            pool.drain()
            pool.memset(minus_half[:, :], -0.5)
            pool.memset(xf, 0.0)
            pool.memset(prob_c[:, :], 0.0)
            pool.memset(route_c[:, :], 0.0)
            pool.memset(zero[:, :], 0.0)
            pool.memset(ones_b[:, :], 1.0)
            pool.memset(expert_i[:, :], 0)
            pool.memset(pl[:, :], 0.0)
            pool.drain().then_inc(s_consts, 1)

            def fetch(c):
                pool.tensor_copy(idx_a[:, :], pred_i[:, bass.ds(c, 1)]).then_inc(s_idx_set, 1)
                pool.wait_ge(s_idx_set, c + 1)
                pool.sem_inc(s_pool_steps, 1)
                pool.indirect_dma_start(tid[:, :], None, x_rows, bass.IndirectOffsetOnAxis(ap=idx_a[:, 0:1], axis=0)).then_inc(s_id_in, 16)
                pool.wait_ge(s_id_in, c * 16 + 16)
                pool.sem_inc(s_pool_steps, 1)
                pool.wait_ge(s_emb_used, c + 1)
                pool.sem_inc(s_pool_steps, 1)
                pool.indirect_dma_start(emb_t[:, :], None, emb, bass.IndirectOffsetOnAxis(ap=tid[:, 0:1], axis=0)).then_inc(s_emb_in, 16)
                pool.wait_ge(s_emb_in, c * 16 + 16)
                pool.sem_inc(s_pool_steps, 1)

            pool.wait_ge(s_counts, 1)
            pool.wait_ge(s_tables, 1)
            pool.sem_inc(s_s_mm, 1)
            n = pool.value_load(counts_i[0:1, 0:1], min_val=1, max_val=CHUNKS)
            def deviation(s, count):
                pool.wait_ge(s_var_ready, count)
                pool.sem_inc(s_pool_steps, 1)
                pool.tensor_scalar(s[:, 9:10], s[:, 7:8], EPS, None, ALU.add)
                pool.drain()
                pool.tensor_tensor(s[:, 8:9], s[:, 9:10], minus_half[:, :], ALU.pow).then_inc(s_dev_ready, 1)

            fetch(0)
            deviation(st, 1)
            fetch(1)
            with pool.Fori(0, n) as c:
                pool.wait_ge(s_s_mm, c * 2 + 1)
                pool.sem_inc(s_pool_steps, 1)
                for q in range(CG):
                    pool.tensor_tensor(sides[:, q, :, :].rearrange("p j k -> p (j k)"), units[:, :, :].rearrange("p j k -> p (j k)"),
                                       not_big[:, bass.ds(c * CG + q, 1)].to_broadcast([UNIT, P]), ALU.mult)
                pool.drain().then_inc(s_sides, 1)
                deviation(st, c * 2 + 2)
                fetch(c + 2)
                deviation(st2, c * 2 + 3)

            pool.wait_ge(s_prob_out, 16)
            for t in range(GC):
                pool.indirect_dma_start(full[:, t, :, :].rearrange("p w r -> p (w r)"), None, prob_d,
                                        bass.IndirectOffsetOnAxis(ap=unit_i[:, t:t + 1], axis=0)).then_inc(s_full_in, 16)

            pool.wait_ge(s_slots_known, 1)
            pool.wait_ge(s_xs_clear, n * 16 + 16 * (E + FOUR))
            pool.sem_inc(s_pool_steps, 1)
            with pool.Fori(0, n, FOUR) as c:
                pool.wait_ge(s_sx_in, c * 4 + 16)
                pool.sem_inc(s_pool_steps, 1)
                pool.tensor_copy(idx_4[:, :], slot_i[:, bass.ds(c, FOUR)])
                pool.tensor_copy(sx[:, :, D], place_of[:, bass.ds(c, FOUR)])
                pool.tensor_copy(sx[:, :, D + 1:ROW], zero[:, 0:3 * FOUR].rearrange("p (a n) -> p a n", a=FOUR))
                pool.drain()
                for i in range(FOUR):
                    pool.indirect_dma_start(xs_d, bass.IndirectOffsetOnAxis(ap=idx_4[:, i:i + 1], axis=0), sx[:, i, :], None,
                                            bounds_check=TILES * P - 1, oob_is_err=False).then_inc(s_xs_out, 16)
                pool.wait_ge(s_xs_out, c * 16 + 64)
                pool.sem_inc(s_sx_free, 4)
            pool.sem_inc(s_xs_done, 1)

            pool.wait_ge(s_o_clear, n * 16)
            pool.sem_inc(s_pool_steps, 1)
            m = pool.value_load(counts_i[0:1, 1:2], min_val=1, max_val=TILES)
            with pool.Fori(0, m + 1) as t:
                pool.wait_ge(s_ob_ready, t + 1)
                pool.sem_inc(s_pool_steps, 1)
                pool.indirect_dma_start(o_d, bass.IndirectOffsetOnAxis(ap=idx_a[:, 0:1], axis=0), ob, None,
                                        bounds_check=CHUNKS * P - 1, oob_is_err=False).then_inc(s_o_out, 16)
                pool.wait_ge(s_o_out, t * 16 + 16)
                pool.sem_inc(s_ob_stored, 1)
            pool.sem_inc(s_o_done, 1)

            pool.wait_ge(s_fill_out, 16 * FILLS)
            pool.wait_ge(s_zt_ready, 1)
            pool.indirect_dma_start(out_groups, bass.IndirectOffsetOnAxis(ap=zs_i[:, 0:1], axis=0),
                                    zt[:, :, :].rearrange("p r d -> p (r d)"), None,
                                    bounds_check=G - 1, oob_is_err=False).then_inc(s_z_out, 16)
            with pool.Fori(0, n) as c:
                pool.tensor_copy(idx_4[:, :], out_tok[:, bass.ds(c * BU, BU)])
                pool.drain()
                for i in range(BU):
                    pool.wait_ge(s_y_ready, c * BU + i + 1)
                    pool.sem_inc(s_pool_steps, 1)
                    pool.indirect_dma_start(out_rows, bass.IndirectOffsetOnAxis(ap=idx_4[:, i:i + 1], axis=0), yo[:, i, :], None,
                                            bounds_check=N - 1, oob_is_err=False).then_inc(s_y_out, 16)
                pool.wait_ge(s_y_out, c * 64 + 64)
                pool.sem_inc(s_yo_free, 1)
            pool.wait_ge(s_z_out, 16)
            pool.nop()

        @block.scalar
        def _(se):
            se.dma_start(bproj_s[:, :], b_proj.rearrange("(o n) -> o n", o=1)).then_inc(s_small_in, 16)
            se.dma_start(wsw_s[0:DH, :, :], sw.rearrange("(h p) e -> p h e", h=2)).then_inc(s_small_in, 16)
            se.dma_start(wsw_s[DH:DH + 1, 0, :], sb_.rearrange("(o n) -> o n", o=1)).then_inc(s_small_in, 16)
            se.dma_start(wproj_s[:, :, :], w_proj.rearrange("(j p) d -> p j d", p=DH)).then_inc(s_wproj_in, 16)
            se.dma_start(w1_s[0:DH, 0, :, :], w1[:, 0:DH, :].rearrange("e p f -> p e f")).then_inc(s_w1_in, 16)
            se.dma_start(w1_s[0:DH, 1, :, :], w1[:, DH:D, :].rearrange("e p f -> p e f")).then_inc(s_w1_in, 16)
            se.dma_start(w1_s[DH:DH + 1, 0, :, :], b1.rearrange("(o e) f -> o e f", o=1)).then_inc(s_w1_in, 16)
            se.sem_inc(s_act_tiles, 9)

            se.wait_ge(s_counts, 1)
            n = se.value_load(counts_i[0:1, 0:1], min_val=1, max_val=CHUNKS)
            with se.Fori(0, n) as c:
                se.wait_ge(s_v_moved, c * 128 + 128)
                for i in range(3):
                    se.wait_ge(s_tile_mm, c * 15 + i + 1)
                    se.copy(vn[:, 512 * i:512 * (i + 1)], mm[i % 4][:, :]).then_inc(s_act_tiles, 1)
                se.drain().then_inc(s_v_copied, 1)
                for i in range(4):
                    k = 3 + 2 * i
                    se.wait_ge(s_tile_mm, c * 15 + k + 1)
                    se.copy(qt[:, i % 2, :, 4 * (i // 2):4 * (i // 2) + 4, :].rearrange("p g j r -> p j g r"),
                            mm[k % 4][0:DH, :].rearrange("p (j g r) -> p j g r", j=4, g=CG)).then_inc(s_act_tiles, 1)
                for half in range(2):
                    se.wait_ge(s_max_ready, c * 2 + half + 1)
                    for g in range(4 * half, 4 * half + 4):
                        last = se.activation(ex[:, g, :], ps_s[half][:, P * (g % 4):P * (g % 4 + 1)], ACT.Exp, bias=sm[:, 1, g:g + 1])
                    last.then_inc(s_exp_ready, 1)
                se.wait_ge(s_lmax_ready, c + 1)
                se.activation(rt[:, 8:16], ps_l, ACT.Exp, bias=rt[:, 1:2], accum_out=rt[:, 2:3]).then_inc(s_lexp_ready, 1)
                for half in range(2):
                    se.wait_ge(s_pt_mm, c * 2 + half + 1)
                    se.copy(pt[:, 4 * half:4 * half + 4, :].rearrange("p g a -> p (g a)"), ps_t[:, :]).then_inc(s_pt_ready, 1)
                for i in range(2):
                    k = 11 + 2 * i
                    se.wait_ge(s_tile_mm, c * 15 + k + 1)
                    se.copy(ot[:, 0, :, 64 * i:64 * i + 64].rearrange("p j (g r) -> p g j r", r=GT),
                            mm[k % 4][0:DH, :].rearrange("p (g j r) -> p g j r", g=4, j=HEADS)).then_inc(s_act_tiles, 1)
            se.wait_ge(s_lmax_ready, n + 1)
            se.activation(rt[:, 8:16], ps_l, ACT.Exp, bias=rt[:, 1:2], accum_out=rt[:, 2:3]).then_inc(s_lexp_ready, 1)

            se.wait_ge(s_bz_ready, 1)
            for t in range(FILLS):
                se.dma_start(out_rows.rearrange("(t p r) d -> t p r d", t=FILLS, p=P)[t],
                             bz.rearrange("p (r d) -> p r d", r=1).to_broadcast([P, N // P // FILLS, D])).then_inc(s_fill_out, 16)
            se.wait_ge(s_slots_known, 1)
            m = se.value_load(counts_i[0:1, 1:2], min_val=1, max_val=TILES)
            with se.Fori(0, m) as t:
                for i in range(2):
                    se.wait_ge(s_h_mm, t * 2 + i + 1)
                    se.activation(hs[:, 384 * i:384 * (i + 1)], mm[i][:, 0:384], ACT.Gelu).then_inc(s_hs_ready, 1)
                se.wait_ge(s_ht_mm, t * 2 + 2)
                se.copy(ht[:, 3:6, :].rearrange("p c t -> p (c t)"), mm[3][:, 0:384]).then_inc(s_ht_act, 1)
            se.nop()

        @block.tensor
        def _(pe):
            pe.wait_ge(s_consts, 1)
            pe.wait_ge(s_act_ready, 1)
            both = classes[:, :, :].rearrange("p a t -> p (a t)")
            pe.matmul(ps_m[:, 0:2 * GC], before[:, :], both, start=True, stop=True)
            pe.matmul(ps_m[:, 2 * GC:4 * GC], ones[:, :], both, start=True, stop=True).then_inc(s_rank_mm, 1)
            pe.wait_ge(s_picks, 1)
            for dst, lhs in ((0, pick_v), (COLS, pick_m)):
                for t in range(GC):
                    pe.matmul(mm[0][:, dst:dst + COLS], lhs[:, t, :], pick_c[:, t, :], start=t == 0, stop=t == GC - 1)
            for t in range(GC):
                last = pe.matmul(mm[0][:, 3 * COLS:3 * COLS + 1], pick_z[:, t, :], ones[:, 0:1], start=t == 0, stop=t == GC - 1)
            last.then_inc(s_picks_mm, 1)

            pe.wait_ge(s_wqkv_in, 48)
            pe.wait_ge(s_wproj_in, 16)
            pe.wait_ge(s_small_in, 48)
            pe.wait_ge(s_counts, 1)

            def turn_rows(src, a, b):
                pe.transpose(a[0:DH, :], src[:, 0:DH], ident[:, :])
                return pe.transpose(b[0:DH, :], src[:, DH:D], ident[:, :])

            pe.wait_ge(s_xn_ready, 1)
            turn_rows(xn, ps_x, ps_x2).then_inc(s_xt_mm, 1)

            act_tile = {0: 1, 1: 2, 2: 3, 3: 4, 5: 5, 7: 6, 9: 7, 11: 8, 13: 9}
            dve_tile = {4: 1, 6: 2, 8: 3, 10: 4, 12: 5, 14: 6}
            LEFT = {k: k - 4 for k in range(4, 15)}
            LEFT.update({0: 12, 1: 13, 2: 14, 3: 11})

            def bank_left(c, k):
                prev = LEFT[k]
                base = 0 if k < 4 else 1
                if prev in act_tile:
                    pe.wait_ge(s_act_tiles, c * 9 + 9 * base + act_tile[prev])
                else:
                    pe.wait_ge(s_dve_tiles, c * 6 + 6 * base + dve_tile[prev])

            def router(c):
                pe.wait_ge(s_xf_ready, c + 1)
                turn_rows(xf, ps_x, ps_x2).then_inc(s_xft_mm, 1)
                pe.wait_ge(s_xft_ready, c + 1)
                pe.matmul(ps_l, xft[:, 0, :], wsw_s[:, 0, :], start=True, stop=False)
                pe.matmul(ps_l, xft[0:DH, 1, :], wsw_s[0:DH, 1, :], start=False, stop=True).then_inc(s_l_mm, 1)

            n = pe.value_load(counts_i[0:1, 0:1], min_val=1, max_val=CHUNKS)
            with pe.Fori(0, n) as c:
                pe.wait_ge(s_xt_ready, c + 1)
                for i in range(3):
                    bank_left(c, i)
                    cols = slice(2 * HD + 512 * i, 2 * HD + 512 * (i + 1))
                    pe.matmul(mm[i][:, :], xt[:, 0, :], wqkv_s[:, 0, cols], start=True, stop=False)
                    pe.matmul(mm[i][:, :], xt[0:DH, 1, :], wqkv_s[0:DH, 1, cols], start=False, stop=True).then_inc(s_tile_mm, 1)
                for i in range(8):
                    k = 3 + i
                    which, half, jb = i % 2, (i // 2) % 2, i // 4
                    bank_left(c, k)
                    for j in range(4):
                        a = which * HD + (4 * jb + j) * D + half * DH
                        o_ = mm[k % 4][0:DH, P * j:P * (j + 1)]
                        pe.matmul(o_, wqkv_s[:, 0, a:a + DH], xt[:, 0, :], start=True, stop=False)
                        last = pe.matmul(o_, wqkv_s[0:DH, 1, a:a + DH], xt[0:DH, 1, :], start=False, stop=True)
                    last.then_inc(s_tile_mm, 1)
                pe.wait_ge(s_mdiag, c + 1)
                pe.wait_ge(s_pt_ready, c * 2 + 1)
                pe.matmul(ps_t[:, 0:P], ones[:, :], mdiag[:, :], start=True, stop=True).then_inc(s_mrow_mm, 1)
                pe.wait_ge(s_act_tiles, c * 9 + 16)
                pe.wait_ge(s_dve_tiles, c * 6 + 10)
                pe.wait_ge(s_sides, c + 1)
                for half in range(2):
                    for g in range(4 * half, 4 * half + 4):
                        o_ = ps_s[half][:, P * (g % 4):P * (g % 4 + 1)]
                        for h in range(2):
                            pe.matmul(o_, qt[:, h, g, :, :].rearrange("p j r -> p (j r)"),
                                      kt[:, h, g, :, :].rearrange("p j r -> p (j r)"), start=h == 0, stop=False)
                        last = pe.matmul(o_, sides[:, g, :, :].rearrange("p j k -> p (j k)"),
                                         others[:, :, :].rearrange("p j k -> p (j k)"), start=False, stop=True)
                    last.then_inc(s_s_mm, 1)
                pe.wait_ge(s_xn_ready, c + 2)
                turn_rows(xn, ps_x, ps_x2).then_inc(s_xt_mm, 1)
                pe.wait_ge(s_xt_ready, c + 2)
                router(c)
                pe.wait_ge(s_mrow_ready, c + 1)
                for half in range(2):
                    pe.wait_ge(s_p_ready, c * 2 + half + 1)
                    pe.wait_ge(s_pt_ready, c * 2 + half + 1)
                    for g in range(4 * half, 4 * half + 4):
                        last = pe.transpose(ps_t[:, P * (g % 4):P * (g % 4 + 1)], ex[:, g, :], ident[:, :])
                    last.then_inc(s_pt_mm, 1)
                pe.wait_ge(s_v_moved, c * 128 + 256)
                for i in range(4):
                    k = 11 + i
                    gq, half = i // 2, i % 2
                    pe.wait_ge(s_pt_ready, c * 2 + gq + 2)
                    bank_left(c, k)
                    for g in range(4 * gq, 4 * gq + 4):
                        last = pe.matmul(mm[k % 4][0:DH, P * (g % 4):P * (g % 4 + 1)],
                                         vp[:, g, half * DH:(half + 1) * DH], pt[:, g, :], start=True, stop=True)
                    last.then_inc(s_tile_mm, 1)
                pe.wait_ge(s_act_tiles, c * 9 + 18)
                pe.wait_ge(s_dve_tiles, c * 6 + 12)
                pe.matmul(ps_y, ones[0:1, :], bproj_s[0:1, :], start=True, stop=False)
                for j in range(HEADS):
                    for half in range(2):
                        last = pe.matmul(ps_y, ot[:, half, j, :], wproj_s[:, 2 * j + half, :],
                                         start=False, stop=j == HEADS - 1 and half == 1)
                last.then_inc(s_y_mm, 1)
            router(n)

            pe.wait_ge(s_probT_ready, 1)
            pe.matmul(mm[0][:, 0:1], first[:, :], prob_c[:, 1:2], start=True, stop=True).then_inc(s_p0_mm, 1)
            pe.transpose(mm[1][0:CHUNKS, 0:P], prob_c[:, 1:CHUNKS + 1], ident[:, :])
            pe.transpose(mm[1][0:CHUNKS, P:2 * P], route_c[:, 1:CHUNKS + 1], ident[:, :]).then_inc(s_probT_mm, 1)

            pe.wait_ge(s_eqc_ready, 1)
            half_e = E // 2
            for i in range(2):
                rows = eqc[:, half_e * i:half_e * (i + 1), :].rearrange("p e c -> p (e c)")
                pe.matmul(ps_s[i][:, 0:half_e * CHUNKS], before[:, :], rows, start=True, stop=True)
                last = pe.matmul(mm[2 + i][:, 0:half_e * CHUNKS], ones[:, :], rows, start=True, stop=True)
            last.then_inc(s_eqc_mm, 1)
            def probe(k):
                pe.wait_ge(s_hit_ready, k + 1)
                for i in range(8):
                    last = pe.matmul(ps_s[1][:, 0:E * 8], ones_b[:, :], hit[:, :, 8 * i:8 * i + 8], start=i == 0, stop=i == 7)
                last.then_inc(s_hit_mm, 1)

            pe.wait_ge(s_steps_ready, 1)
            for i, lhs in enumerate((pick_k, pick_s2)):
                for t in range(GC):
                    last = pe.matmul(mm[i][:, 0:OC], lhs[:, t, :], pick_o[:, t, :], start=t == 0, stop=t == GC - 1)
            last.then_inc(s_steps_mm, 1)

            with pe.Fori(0, EARLY) as k:
                probe(k)

            pe.wait_ge(s_w1_in, 48)
            pe.wait_ge(s_w2_in, 16 * FC)
            pe.wait_ge(s_b2_in, 16)
            m = pe.value_load(counts_i[0:1, 1:2], min_val=1, max_val=TILES)

            def expert_out(t, e):
                pe.wait_ge(s_ob_stored, t + 1)
                pe.wait_ge(s_ht_dve, t + 1)
                pe.wait_ge(s_ht_act, t + 1)
                pe.matmul(ps_y, ones[0:1, :], b2_s[0:1, bass.ds(e, 1), :].rearrange("p e d -> p (e d)"), start=True, stop=False)
                for f in range(FC):
                    last = pe.matmul(ps_y, ht[:, f, :], w2_s[:, f, bass.ds(e, 1), :].rearrange("p e d -> p (e d)"), start=False, stop=f == FC - 1)
                last.then_inc(s_o_mm, 1)

            pe.wait_ge(s_gx_in, 16)
            turn_rows(gx, ps_s[0][:, 0:P], ps_s[0][:, P:2 * P]).then_inc(s_gxt_mm, 1)
            with pe.Fori(0, m) as t:
                e_before = pe.value_load(expert_i[0:1, bass.ds(t, 1)], min_val=0, max_val=E - 1)
                e = pe.value_load(expert_i[0:1, bass.ds(t + 1, 1)], min_val=0, max_val=E - 1)
                pe.wait_ge(s_gxt_ready, t + 1)
                for i in range(2):
                    fs = slice(384 * i, 384 * (i + 1))
                    pe.matmul(mm[i][:, 0:384], gxt[:, 0, :], w1_s[:, 0, bass.ds(e, 1), fs].rearrange("p e f -> p (e f)"), start=True, stop=False)
                    pe.matmul(mm[i][:, 0:384], gxt[0:DH, 1, :], w1_s[0:DH, 1, bass.ds(e, 1), fs].rearrange("p e f -> p (e f)"), start=False, stop=True).then_inc(s_h_mm, 1)
                probe(t * 2 + EARLY)
                expert_out(t, e_before)
                pe.wait_ge(s_gx_in, t * 16 + 32)
                turn_rows(gx, ps_s[0][:, 0:P], ps_s[0][:, P:2 * P]).then_inc(s_gxt_mm, 1)
                probe(t * 2 + EARLY + 1)
                for i in range(2):
                    pe.wait_ge(s_hs_ready, t * 2 + i + 1)
                    for f in range(3):
                        last = pe.transpose(mm[2 + i][:, P * f:P * (f + 1)], hs[:, 384 * i + P * f:384 * i + P * (f + 1)], ident[:, :])
                    last.then_inc(s_ht_mm, 1)
            e_last = pe.value_load(expert_i[0:1, bass.ds(m, 1)], min_val=0, max_val=E - 1)
            expert_out(m, e_last)

            left = pe.value_load(counts_i[0:1, 2:3], min_val=1, max_val=PROBES)
            with pe.Fori(0, left) as k:
                probe(k + m * 2 + EARLY)
            pe.wait_ge(s_tie_ready, 1)
            pe.matmul(mm[1][:, 0:E], ones[:, :], red, start=True, stop=True)
            flat = trow[:, :, :].rearrange("p e t -> p (e t)")
            pe.matmul(mm[1][:, 64:64 + E * GC], before[:, :], flat, start=True, stop=True)
            pe.matmul(mm[1][:, 128:128 + E * GC], ones[:, :], flat, start=True, stop=True).then_inc(s_tie_mm, 1)
            pe.wait_ge(s_keep_ready, 1)
            pe.matmul(mm[1][:, 256:257], ones[:, :], keep_z[:, TR:TR + 1], start=True, stop=True)
            for t in range(GC):
                last = pe.matmul(mm[2][:, 0:OC], pick_k[:, t, :], pick_o[:, t, :], start=t == 0, stop=t == GC - 1)
            last.then_inc(s_keep_mm, 1)
            with pe.Fori(0, n) as c:
                pe.wait_ge(s_selt_ready, c + 1)
                for i in range(BU):
                    last = pe.transpose(ps_t[:, P * i:P * (i + 1)], sel_t[:, i, :], ident[:, :])
                last.then_inc(s_sel_mm, 1)
                pe.wait_ge(s_sel_ready, c + 1)
                for i in range(BU):
                    pe.matmul(mm[i][:, 0:2 * D], sel[:, i, :], rd, start=True, stop=True).then_inc(s_row_mm, 1)
            pe.nop()

        @block.vector
        def _(dve):
            def then(ins):
                dve.drain()

            dve.memset(x_pad, VOCAB_PAD)
            then(dve.memset(best, 0.0))
            dve.wait_ge(s_x_in, 32)
            then(dve.tensor_copy(x_f, x_i))
            dve.tensor_copy(x_pad[0:B, T:2 * T], x_f[0:B, :])
            then(dve.tensor_copy(x_pad[B:2 * B, T + 1:2 * T + 1], x_f[B:2 * B, :]))

            def blk(t, k):
                return t[:, offs[k]:offs[k + 1]].rearrange("p (r i) -> p r i", r=RB)

            for k in range(NB):
                shifted = bass.AP(work, x_pad_at + 1 + 2 * RB * k + starts[k], [[WORK, P], [2, RB], [1, lens[k]]])
                dve.tensor_tensor(blk(eq, k), x_f[:, starts[k]:T].rearrange("p (o i) -> p o i", o=1).to_broadcast([P, RB, lens[k]]),
                                  shifted, ALU.is_equal)
            dve.drain()
            then(dve.tensor_tensor_scan(run, eq, eq, 0.0, ALU.mult, ALU.add))
            dve.wait_ge(s_consts, 1)
            for k in range(NB):
                dve.scalar_tensor_tensor(out=blk(eq, k), in0=blk(run, k), scalar=128.0,
                                         in1=match_j[:, RB * k:RB * (k + 1)].rearrange("p (r o) -> p r o", o=1).to_broadcast([P, RB, lens[k]]),
                                         op0=ALU.mult, op1=ALU.add)
            dve.drain()
            for k in range(NB):
                then(dve.tensor_reduce(tmp_b[:, starts[k]:T], blk(eq, k).rearrange("p r i -> p i r"), AX.X, ALU.max))
                then(dve.tensor_tensor(best[:, starts[k]:T], best[:, starts[k]:T], tmp_b[:, starts[k]:T], ALU.max))
            then(dve.tensor_copy(tmp_b[0:B, :], best[B:2 * B, :]))
            then(dve.tensor_tensor(best[0:B, :], best[0:B, :], tmp_b[0:B, :], ALU.max))
            then(dve.tensor_copy(tmp_i[0:B, :], best[0:B, :]))
            then(dve.tensor_scalar(tmp_i[0:B, :], tmp_i[0:B, :], 127, None, ALU.bitwise_and))
            then(dve.tensor_copy(tmp_b[0:B, :], tmp_i[0:B, :]))
            then(dve.tensor_tensor(tmp_b[0:B, :], tmp_b[0:B, :], pred_base[:, :], ALU.add))
            dve.scalar_tensor_tensor(out=best[0:B, :], in0=best[0:B, :], scalar=128.0, in1=tmp_b[0:B, :],
                                     op0=ALU.is_ge, op1=ALU.mult).then_inc(s_best_out, 1)

            dve.wait_ge(s_pred_back, 32)
            def rows_of(a):
                return a.rearrange("p t r -> p (t r)")

            def over(a, dims):
                return a.to_broadcast([P] + dims)

            dve.memset(reset_g[:, :, :], 1.0)
            dve.tensor_scalar(m4[:, :, :], v4, 0.0, None, ALU.is_gt)
            dve.drain()
            then(dve.memset(reset_g[:, :, 0:1], 0.0))
            then(dve.tensor_tensor_scan(rows_of(cum[:, :, :]), rows_of(reset_g[:, :, :]), rows_of(m4[:, :, :]), 0.0, ALU.mult, ALU.add))
            then(dve.tensor_copy(rk[:, 0, :], cum[:, :, GT - 1]))
            cnt = rk[:, 0, :]
            dve.tensor_scalar(act[:, :], cnt, 0.0, None, ALU.is_gt)
            then(dve.tensor_scalar(classes[:, 1, :], cnt, float(UNIT), None, ALU.is_ge))
            dve.tensor_tensor(classes[:, 0, :], act[:, :], classes[:, 1, :], ALU.subtract).then_inc(s_act_ready, 1)
            then(dve.tensor_tensor(cum[:, :, :], cum[:, :, :], m4[:, :, :], ALU.mult))
            k_row = iota_k[:, :].rearrange("p (a k) -> p a k", a=1)
            cnt_k = over(cnt.rearrange("p (t o) -> p t o", o=1), [GC, GT])
            dve.tensor_tensor(spread[:, :, :, :], over(cum[:, :, :].rearrange("p t (o r) -> p t o r", o=1), [GC, GT, GT]),
                              over(iota_k1[:, :].rearrange("p (a k b) -> p a k b", a=1, b=1), [GC, GT, GT]), ALU.is_equal)
            dve.tensor_tensor(m16[:, :, :], over(k_row, [GC, GT]), cnt_k, ALU.is_lt)
            dve.tensor_tensor(m16b[:, :, :], over(k_row, [GC, GT]), cnt_k, ALU.is_equal)
            then(dve.tensor_scalar(rk[:, 1, :], cnt, -1.0, float(GT), ALU.mult, ALU.add))
            dve.tensor_tensor(m16b[:, :, :], m16b[:, :, :], over(rk[:, 1, :].rearrange("p (t o) -> p t o", o=1), [GC, GT]), ALU.mult)
            then(dve.tensor_tensor(spread[:, :, :, :], spread[:, :, :, :], over(v4.rearrange("p t (o r) -> p t o r", o=1), [GC, GT, GT]), ALU.mult))
            dve.tensor_tensor(m16[:, :, :], m16[:, :, :], m16b[:, :, :], ALU.add)
            then(dve.tensor_reduce(v16[:, :, :], spread[:, :, :, :], AX.X, ALU.add))
            dve.wait_ge(s_rank_mm, 1)
            then(dve.tensor_copy(rk[:, 2:6, :].rearrange("p a t -> p (a t)"), ps_m[:, 0:4 * GC]))
            for i in range(2):
                dve.tensor_tensor_scan(rk[:, 6 + i, :], ones[:, 0:GC], rk[:, 4 + i, :], 0.0, ALU.mult, ALU.add)
            dve.drain()
            then(dve.tensor_tensor(rk[:, 8:10, :], rk[:, 6:8, :], rk[:, 4:6, :], ALU.subtract))
            then(dve.tensor_tensor(rk[:, 8:10, :], rk[:, 8:10, :], rk[:, 2:4, :], ALU.add))
            then(dve.tensor_scalar(rki[:, 0, 0:1], rk[:, 6, GC - 1:GC], float(UNIT), None, ALU.add))
            then(dve.tensor_scalar(rki[:, 0, 0:1], rki[:, 0, 0:1], 2, None, ALU.arith_shift_right))
            then(dve.tensor_copy(rk[:, 10, 0:1], rki[:, 0, 0:1]))
            then(dve.tensor_scalar(rki[:, 1, 0:1], rk[:, 7, GC - 1:GC], rk[:, 10, 0:1], float(CG - 1), ALU.add, ALU.add))
            dve.tensor_scalar(counts_i[0:1, 0:1], rki[0:1, 1, 0:1], 3, None, ALU.arith_shift_right).then_inc(s_counts, 1)
            dve.tensor_scalar(not_big[:, :], iota_b[:, :], rk[0:UNIT, 10, 0:1], None, ALU.is_lt)
            dve.tensor_scalar(rk[:, 11, :], act[:, :], -1.0, 1.0, ALU.mult, ALU.add)
            dve.tensor_tensor(rk[:, 12, :], rk[:, 8, :], rk[:, 9, :], ALU.add)
            dve.tensor_scalar(rk[:, 13, :], rk[:, 9, :], rk[:, 10, 0:1], float(BU), ALU.add, ALU.mult)
            then(dve.scalar_tensor_tensor(out=rk[:, 14, :], in0=rk[:, 8, :], scalar=1.0, in1=classes[:, 0, :], op0=ALU.add, op1=ALU.mult))
            dve.tensor_tensor(rk[:, 13, :], rk[:, 13, :], classes[:, 1, :], ALU.mult)
            then(dve.tensor_tensor(rk[:, 15, :], iota_g[:, :], rk[:, 12, :], ALU.subtract))
            then(dve.scalar_tensor_tensor(out=rk[:, 15, :], in0=rk[:, 15, :], scalar=1.0, in1=rk[:, 11, :], op0=ALU.add, op1=ALU.mult))
            then(dve.tensor_tensor(unit_i[:, :], rk[:, 13, :], rk[:, 14, :], ALU.add))
            dve.tensor_scalar(rk[:, 15, :], rk[:, 15, :], -1.0, None, ALU.add)
            dve.tensor_scalar(rki[:, 0, :], unit_i[:, :], CU - 1, None, ALU.bitwise_and)
            dve.tensor_scalar(rki[:, 2, :], unit_i[:, :], 5, None, ALU.arith_shift_right)
            dve.tensor_scalar(rki[:, 3, :], unit_i[:, :], CG - 1, None, ALU.bitwise_and)
            then(dve.tensor_scalar(rki[:, 4, :], unit_i[:, :], 3, None, ALU.arith_shift_right))
            then(dve.tensor_scalar(rki[:, 1, :], rki[:, 0, :], 2, None, ALU.arith_shift_right))
            then(dve.tensor_copy(rk[:, 16:21, :], rki[:, 0:5, :]))
            for i in (18, 20):
                then(dve.scalar_tensor_tensor(out=rk[:, i, :], in0=rk[:, i, :], scalar=1.0, in1=act[:, :], op0=ALU.add, op1=ALU.mult))
                then(dve.tensor_scalar(rk[:, i, :], rk[:, i, :], -1.0, None, ALU.add))
            flat_q = iota_q[:, :, :].rearrange("p q r -> p (q r)")
            flat_u = iota_u[:, :, :].rearrange("p u k -> p (u k)")
            for t in range(GC):
                dve.tensor_scalar(pick_s[:, t, :], flat_u, rk[:, 16, t:t + 1], classes[:, 0, t:t + 1], ALU.is_equal, ALU.mult)
                dve.tensor_scalar(pick_b[:, t, :], flat_q, rk[:, 17, t:t + 1], classes[:, 1, t:t + 1], ALU.is_equal, ALU.mult)
                dve.tensor_scalar(pick_c[:, t, :], iota_f[:, 0:COLS], rk[:, 18, t:t + 1], None, ALU.is_equal)
                dve.tensor_scalar(pick_z[:, t, :], iota_f[:, :], rk[:, 15, t:t + 1], iota_g[:, t:t + 1], ALU.is_equal, ALU.mult)
            dve.drain()

            def in_chunk(dst, values):
                def cells(a, n_):
                    return a[:, :, :].rearrange("p t (n k) -> p t n k", n=n_)
                dve.tensor_tensor(cells(dst, CU), cells(pick_s, CU),
                                  over(values[:, :, 0:UNIT].rearrange("p t (o k) -> p t o k", o=1), [GC, CU, UNIT]), ALU.mult)
                then(dve.tensor_tensor(cells(pick_x, CG), cells(pick_b, CG),
                                       over(values[:, :, :].rearrange("p t (o k) -> p t o k", o=1), [GC, CG, GT]), ALU.mult))
                then(dve.tensor_tensor(dst[:, :, :], dst[:, :, :], pick_x[:, :, :], ALU.add))

            in_chunk(pick_v, v16)
            in_chunk(pick_m, m16)
            dve.sem_inc(s_picks, 1)
            then(dve.tensor_scalar(rk[:, 21, :], cnt, 1.0, None, ALU.add))
            then(dve.tensor_tensor(m4[:, :, :], m4[:, :, :], over(rk[:, 21, :].rearrange("p (t o) -> p t o", o=1), [GC, GT]), ALU.mult))
            then(dve.tensor_tensor(place_k[:, :, :], cum[:, :, :], m4[:, :, :], ALU.subtract))
            dve.tensor_tensor(place_k[:, :, :], place_k[:, :, :], cnt_k, ALU.add)
            dve.wait_ge(s_picks_mm, 1)
            dve.tensor_scalar(match_f[:, :], mm[0][:, 0:COLS], 0.0, None, ALU.is_gt)
            dve.tensor_scalar(pred_i[:, :], mm[0][:, 0:COLS], -1.0, 0.0, ALU.add, ALU.max)
            then(dve.tensor_copy(mult_c[:, :], mm[0][:, COLS:2 * COLS]))
            then(dve.memset(mult_c[0:1, 0:1], float(GT)))
            then(dve.tensor_scalar(valid[:, :], mult_c[:, :], 0.0, None, ALU.is_gt))
            dve.tensor_scalar(place_v[:, :], valid[:, :], -NOWHERE, NOWHERE, ALU.mult, ALU.add)
            dve.tensor_copy(zlist[:, :], mm[0][:, 3 * COLS:3 * COLS + 1])
            dve.drain().then_inc(s_tables, 1)

            dve.sem_inc(s_dve_tiles, 6)
            dve.sem_inc(s_xf_ready, 1)
            n = dve.value_load(counts_i[0:1, 0:1], min_val=1, max_val=CHUNKS)

            def norm(dst, src, s, count):
                then(dve.bn_stats(s[:, 0:6], src))
                dve.bn_aggr(s[:, 6:8], s[:, 0:6]).then_inc(s_var_ready, 1)
                dve.wait_ge(s_dev_ready, count)
                return dve.tensor_scalar(dst, src, s[:, 6:7], s[:, 8:9], ALU.subtract, ALU.mult)

            def turned(dst, src=ps_m[:, D:D + 2 * P]):
                return dve.tensor_copy(dst[0:DH, :, :], src[0:DH, :].rearrange("p (h t) -> p h t", h=2))

            def embed(c, count):
                dve.wait_ge(s_emb_in, c * 16 + 16)
                then(dve.tensor_scalar(h_next[:, :], emb_t[:, :], match_f[:, bass.ds(c, 1)], None, ALU.mult))
                dve.sem_inc(s_emb_used, 1)
                norm(xn[:, :], h_next[:, :], st, count).then_inc(s_xn_ready, 1)

            def route_tail(c):
                dve.wait_ge(s_l_mm, c + 1)
                then(dve.tensor_reduce(rt[:, 0:1], ps_l, AX.X, ALU.max))
                dve.tensor_scalar(rt[:, 1:2], rt[:, 0:1], -1.0, None, ALU.mult).then_inc(s_lmax_ready, 1)
                dve.wait_ge(s_lexp_ready, c + 1)
                then(dve.reciprocal(rt[:, 3:4], rt[:, 2:3]))
                then(dve.tensor_scalar(rt[:, 16:24], rt[:, 8:16], rt[:, 3:4], None, ALU.mult))
                then(dve.tensor_reduce(rt[:, 4:5], rt[:, 16:24], AX.X, ALU.max))
                then(dve.tensor_scalar(rt[:, 24:32], rt[:, 16:24], rt[:, 4:5], float(E), ALU.is_lt, ALU.mult))
                dve.tensor_copy(prob_c[:, bass.ds(c, 1)], rt[:, 4:5])
                then(dve.tensor_tensor(rt[:, 24:32], rt[:, 24:32], iota_f[:, 0:E], ALU.add))
                dve.tensor_reduce(route_c[:, bass.ds(c, 1)], rt[:, 24:32], AX.X, ALU.min)

            embed(0, 1)
            dve.wait_ge(s_xt_mm, 1)
            turned(xt).then_inc(s_xt_ready, 1)
            with dve.Fori(0, n) as c:
                dve.tensor_copy(h_cur[:, :], h_next[:, :])
                dve.tensor_scalar(mdiag[:, :], ident[:, :], mult_c[:, bass.ds(c, 1)], None, ALU.mult)
                dve.drain().then_inc(s_mdiag, 1)
                for i in range(4):
                    k = 4 + 2 * i
                    dve.wait_ge(s_tile_mm, c * 15 + k + 1)
                    dve.tensor_copy(kt[:, i % 2, :, 4 * (i // 2):4 * (i // 2) + 4, :].rearrange("p g j r -> p j g r"),
                                    mm[k % 4][0:DH, :].rearrange("p (j g r) -> p j g r", j=4, g=CG)).then_inc(s_dve_tiles, 1)
                    if i == 1:
                        embed(c + 1, c * 2 + 2)
                dve.wait_ge(s_mrow_mm, c + 1)
                dve.tensor_copy(mrow[:, :], ps_t[:, 0:P]).then_inc(s_mrow_ready, 1)
                for half in range(2):
                    gs = slice(4 * half, 4 * half + 4)
                    dve.wait_ge(s_s_mm, c * 2 + half + 2)
                    then(dve.tensor_reduce(sm[:, 0, gs], ps_s[half][:, :].rearrange("p (g l) -> p g l", g=4), AX.X, ALU.max))
                    dve.tensor_scalar(sm[:, 1, gs], sm[:, 0, gs], -1.0, None, ALU.mult).then_inc(s_max_ready, 1)
                dve.wait_ge(s_xt_mm, c + 2)
                turned(xt).then_inc(s_xt_ready, 1)
                for half in range(2):
                    gs = slice(4 * half, 4 * half + 4)
                    dve.wait_ge(s_exp_ready, c * 2 + half + 1)
                    then(dve.tensor_tensor(ex[:, gs, :].rearrange("p g (j k) -> p g j k", j=HEADS), ex[:, gs, :].rearrange("p g (j k) -> p g j k", j=HEADS),
                                           over(mrow[:, GT * 4 * half:GT * 4 * (half + 1)].rearrange("p (g o k) -> p g o k", g=4, o=1), [4, HEADS, GT]), ALU.mult))
                    then(dve.tensor_reduce(sm[:, 2, gs], ex[:, gs, :], AX.X, ALU.add))
                    then(dve.tensor_scalar(sm[:, 3, gs], sm[:, 2, gs], 1e-30, float(D) ** 0.5, ALU.max, ALU.mult))
                    then(dve.reciprocal(sm[:, 3, gs], sm[:, 3, gs]))
                    if half == 0:
                        dve.wait_ge(s_xft_mm, c + 1)
                        turned(xft).then_inc(s_xft_ready, 1)
                    dve.tensor_tensor(ex[:, gs, :], ex[:, gs, :], sm[:, 3, gs].rearrange("p (g o) -> p g o", o=1).to_broadcast([P, 4, P]),
                                      ALU.mult).then_inc(s_p_ready, 1)
                route_tail(c)
                for i in range(2):
                    k = 12 + 2 * i
                    dve.wait_ge(s_tile_mm, c * 15 + k + 1)
                    dve.tensor_copy(ot[:, 1, :, 64 * i:64 * i + 64].rearrange("p j (g r) -> p g j r", r=GT),
                                    mm[k % 4][0:DH, :].rearrange("p (g j r) -> p g j r", g=4, j=HEADS)).then_inc(s_dve_tiles, 1)
                dve.wait_ge(s_y_mm, c + 2)
                dve.wait_ge(s_xf_out, c * 16 + 16)
                then(dve.tensor_tensor(h1, h_cur[:, :], ps_y, ALU.add))
                norm(xf, h1, st2, c * 2 + 3).then_inc(s_xf_ready, 1)
            dve.wait_ge(s_xft_mm, n + 1)
            turned(xft).then_inc(s_xft_ready, 1)
            route_tail(n)
            dve.drain().then_inc(s_probT_ready, 1)

            dve.wait_ge(s_probT_mm, 1)
            dve.memset(pT[:, :, :], 0.0)
            dve.drain()
            then(dve.tensor_copy(pT[:, :, 0:P], mm[1][0:CHUNKS, 0:2 * P].rearrange("p (w m) -> p w m", w=2)))
            for i in range(2):
                windows = bass.AP(area, pT_at + (P + GT) * i, [[2 * 3 * HD, CHUNKS], [UNIT, CU], [1, GT]])
                dve.tensor_copy(pTx[:, :, i, :], windows)
            dve.drain().then_inc(s_probT_ready, 1)

            def by_t(a):
                return a.rearrange("p (t r) -> p t r", t=GC)

            def by_group(dst, values):
                return dve.tensor_tensor(dst[:, :, :].rearrange("p t (q r) -> p t q r", q=CG), pick_u[:, :, :].rearrange("p t (q r) -> p t q r", q=CG),
                                         over(values.rearrange("p t (o r) -> p t o r", o=1), [GC, CG, GT]), ALU.mult)

            rc = route_c[:, 1:CHUNKS + 1]
            for e in range(E):
                dve.scalar_tensor_tensor(out=eqc[:, e, :], in0=rc, scalar=float(e), in1=valid[:, 0:CHUNKS], op0=ALU.is_equal, op1=ALU.mult)
            dve.memset(reset_c[:, :, :], 1.0)
            dve.memset(reset_r[:, :, :], 1.0)
            dve.drain().then_inc(s_eqc_ready, 1)
            dve.memset(reset_c[:, :, 0:1], 0.0)
            dve.memset(reset_r[:, :, 0:1], 0.0)
            dve.wait_ge(s_p0_mm, 1)
            dve.wait_ge(s_zrow_in, 16)
            then(dve.tensor_copy(p0, mm[0][:, 0:1]))
            dve.scalar_tensor_tensor(out=bz, in0=xh0[:, 0:D], scalar=p0, in1=xh0[:, D:2 * D], op0=ALU.mult, op1=ALU.add).then_inc(s_bz_ready, 1)
            dve.wait_ge(s_eqc_mm, 1)
            he = E // 2
            for i in range(2):
                dve.tensor_copy(csum[:, he * i:he * (i + 1), :].rearrange("p e c -> p (e c)"), mm[2 + i][:, 0:he * CHUNKS])
            dve.drain()
            then(dve.tensor_tensor_scan(cinc[:, :, :].rearrange("p e c -> p (e c)"), reset_c[:, :, :].rearrange("p e c -> p (e c)"),
                                        csum[:, :, :].rearrange("p e c -> p (e c)"), 0.0, ALU.mult, ALU.add))
            tot = cinc[:, :, CHUNKS - 1]
            dve.tensor_scalar(tl_i[:, 0, :], tot, float(P - 1), None, ALU.add)
            then(dve.tensor_tensor(posn[:, :, :], cinc[:, :, :], csum[:, :, :], ALU.subtract))
            then(dve.tensor_scalar(tl_i[:, 0, :], tl_i[:, 0, :], 7, None, ALU.arith_shift_right))
            then(dve.tensor_copy(tl[:, 0, :], tl_i[:, 0, :]))
            then(dve.tensor_tensor_scan(tl[:, 1, :], ones[:, 0:E], tl[:, 0, :], 0.0, ALU.mult, ALU.add))
            dve.tensor_copy(counts_i[0:1, 1:2], tl[0:1, 1, E - 1:E])
            then(dve.tensor_tensor(tl[:, 2, :], tl[:, 1, :], tl[:, 0, :], ALU.subtract))
            then(dve.tensor_scalar(tl[:, 3, :], tl[:, 2, :], float(P), None, ALU.mult))
            then(dve.tensor_tensor(tcmp[:, :, :], tl[0:1, 2, :].rearrange("p (o e) -> p o e", o=1).to_broadcast([1, TILES, E]),
                                   iota_f[0:1, 0:TILES].rearrange("p (t o) -> p t o", o=1).to_broadcast([1, TILES, E]), ALU.is_le))
            then(dve.tensor_reduce(texp, tcmp[:, :, :], AX.X, ALU.add))
            then(dve.tensor_scalar(expert_i[0:1, 1:TILES + 1], texp, -1.0, None, ALU.add))
            then(dve.tensor_scalar(texp[:, 0:1], tl[0:1, 1, E - 1:E], -2.0, float(PROBES - EARLY), ALU.mult, ALU.add))
            dve.tensor_scalar(counts_i[0:1, 2:3], texp[:, 0:1], 1.0, None, ALU.max)
            then(dve.tensor_tensor(posn[:, :, :], posn[:, :, :], tl[:, 3, :].rearrange("p (e o) -> p e o", o=1).to_broadcast([P, E, CHUNKS]), ALU.add))
            for i in range(2):
                es = slice(he * i, he * (i + 1))
                dve.tensor_tensor(posn[:, es, :], posn[:, es, :], ps_s[i][:, 0:he * CHUNKS].rearrange("p (e c) -> p e c", e=he), ALU.add)
            dve.drain()
            then(dve.tensor_tensor(posn[:, :, :], posn[:, :, :], eqc[:, :, :], ALU.mult))
            dve.memset(slot_f[:, :], 0.0)
            dve.drain()
            then(dve.tensor_reduce(slot_f[:, 0:CHUNKS], posn[:, :, :].rearrange("p e c -> p c e"), AX.X, ALU.add))
            then(dve.tensor_copy(slot_i[:, :], slot_f[:, :]))
            dve.tensor_tensor(slot_i[:, :], slot_f[:, :], place_v[:, :], ALU.add)
            dve.drain()
            dve.sem_inc(s_slots_known, 1)
            then(dve.scalar_tensor_tensor(out=by_t(slot_v), in0=over(rk[:, 16, :].rearrange("p (t o) -> p t o", o=1), [GC, GT]), scalar=float(UNIT),
                                          in1=place_k[:, :, :], op0=ALU.mult, op1=ALU.add))
            for t in range(GC):
                dve.tensor_scalar(pick_u[:, t, :], flat_q, rk[:, 19, t:t + 1], None, ALU.is_equal)
                dve.tensor_scalar(pick_o[:, t, :], iota_o[:, :], rk[:, 20, t:t + 1], None, ALU.is_equal)
            dve.drain()
            by_group(pick_k, tok_of[:, :, :])
            by_group(pick_s2, by_t(slot_v))
            dve.drain().then_inc(s_steps_ready, 1)
            dve.wait_ge(s_steps_mm, 1)
            dve.tensor_scalar(out_tok[:, :], mm[0][:, 0:OC], -1.0, NOWHERE, ALU.mult, ALU.add)
            dve.tensor_copy(out_place[:, :], mm[1][:, 0:OC])

            dve.wait_ge(s_full_in, 16 * GC)
            then(dve.tensor_tensor(at_place, over(place_k[:, :, :].rearrange("p t (r o) -> p (t r) o", o=1), [TR, GT]),
                                   over(k_row, [TR, GT]), ALU.is_equal))
            fp = keep_z[:, 0:TR]
            fr = keep
            for i, dst in enumerate((fp, fr)):
                then(dve.tensor_tensor(at_work.rearrange("p (t r) k -> p t r k", t=GC), at_place.rearrange("p (t r) k -> p t r k", t=GC),
                                       over(full[:, :, i, :].rearrange("p t (o k) -> p t o k", o=1), [GC, GT, GT]), ALU.mult))
                then(dve.tensor_reduce(dst, at_work, AX.X, ALU.add))
            for e in range(E):
                dve.tensor_scalar(member[:, e, :], fr, float(e), None, ALU.is_equal)
                dve.scalar_tensor_tensor(out=score[:, e, :], in0=fr, scalar=float(e), in1=fp, op0=ALU.is_equal, op1=ALU.mult)
            dve.memset(thr, 0.0)
            dve.memset(step, 1.0)
            dve.drain()

            def per_expert(a):
                return a.rearrange("p (e o) -> p e o", o=1).to_broadcast([P, E, TR])

            def try_step():
                then(dve.tensor_scalar(cand, thr, step, None, ALU.add))
                dve.tensor_tensor(hit[:, :, :], score[:, :, :], per_expert(cand), ALU.is_ge).then_inc(s_hit_ready, 1)

            def take_step(k):
                dve.wait_ge(s_hit_mm, k + 1)
                dve.tensor_scalar(step, step, 0.5, None, ALU.mult)
                then(dve.tensor_reduce(red, ps_s[1][:, 0:E * 8].rearrange("p (e n) -> p e n", e=E), AX.X, ALU.add))
                then(dve.scalar_tensor_tensor(out=cand, in0=red, scalar=float(CAP), in1=cand, op0=ALU.is_ge, op1=ALU.mult))
                then(dve.tensor_tensor(thr, thr, cand, ALU.max))

            with dve.Fori(0, EARLY) as k:
                try_step()
                take_step(k)

            dve.memset(gxt[DH:DH + 1, 0, :], 1.0)
            dve.memset(ht[:, :, :], 0.0)
            dve.drain()
            dve.sem_inc(s_ht_dve, 1)
            dve.sem_inc(s_ht_act, 1)
            m = dve.value_load(counts_i[0:1, 1:2], min_val=1, max_val=TILES)

            def expert_row(t):
                dve.wait_ge(s_o_mm, t + 1)
                dve.wait_ge(s_ob_stored, t + 1)
                dve.tensor_copy(ob, ps_y)
                dve.tensor_scalar(idx_a[:, :], pl[:, 1:2], -1.0, NOWHERE, ALU.mult, ALU.add)
                dve.drain().then_inc(s_ob_ready, 1)
                then(dve.tensor_copy(pl[:, 1:2], pl[:, 0:1]))

            def take_rows():
                dve.tensor_copy(pl[:, 0:1], gx[:, D:D + 1])
                turned(gxt, ps_s[0][:, 0:2 * P])
                dve.drain().then_inc(s_gxt_ready, 1)

            dve.wait_ge(s_gxt_mm, 1)
            take_rows()
            with dve.Fori(0, m) as t:
                try_step()
                take_step(t * 2 + EARLY)
                try_step()
                expert_row(t)
                dve.wait_ge(s_gxt_mm, t + 2)
                take_rows()
                take_step(t * 2 + EARLY + 1)
                dve.wait_ge(s_ht_mm, t * 2 + 1)
                dve.tensor_copy(ht[:, 0:3, :].rearrange("p c t -> p (c t)"), mm[2][:, 0:384]).then_inc(s_ht_dve, 1)
            expert_row(m)
            left = dve.value_load(counts_i[0:1, 2:3], min_val=1, max_val=PROBES)
            with dve.Fori(0, left) as k:
                try_step()
                take_step(k + m * 2 + EARLY)

            dve.tensor_tensor(cmp[:, :, :], score[:, :, :], per_expert(thr), ALU.is_gt)
            then(dve.tensor_tensor(tie[:, :, :], score[:, :, :], per_expert(thr), ALU.is_equal))
            dve.tensor_reduce(red, cmp[:, :, :], AX.X, ALU.add)
            then(dve.tensor_tensor(tie[:, :, :], tie[:, :, :], member[:, :, :], ALU.mult))
            dve.tensor_reduce(trow[:, :, :], tie[:, :, :].rearrange("p e (t r) -> p e t r", t=GC), AX.X, ALU.add)
            dve.drain().then_inc(s_tie_ready, 1)
            dve.tensor_tensor_scan(incl[:, :, :].rearrange("p e n -> p (e n)"), reset_r[:, :, :].rearrange("p n r -> p (n r)"),
                                   tie[:, :, :].rearrange("p e n -> p (e n)"), 0.0, ALU.mult, ALU.add)
            dve.wait_ge(s_tie_mm, 1)
            dve.tensor_scalar(rem, mm[1][:, 0:E], -1.0, float(CAP), ALU.mult, ALU.add)
            then(dve.tensor_copy(tsum[:, :, :].rearrange("p e t -> p (e t)"), mm[1][:, 128:128 + E * GC]))
            then(dve.tensor_copy(tbase[:, :, :].rearrange("p e t -> p (e t)"), mm[1][:, 64:64 + E * GC]))
            for t in range(1, GC):
                for u in range(t):
                    then(dve.tensor_tensor(tbase[:, :, t:t + 1], tbase[:, :, t:t + 1], tsum[:, :, u:u + 1], ALU.add))
            for t in range(GC):
                ts_ = slice(GT * t, GT * (t + 1))
                dve.tensor_tensor(incl[:, :, ts_], incl[:, :, ts_], tbase[:, :, t:t + 1].to_broadcast([P, E, GT]), ALU.add)
            dve.drain()
            then(dve.tensor_tensor(incl[:, :, :], incl[:, :, :], per_expert(rem), ALU.is_le))
            then(dve.tensor_tensor(tie[:, :, :], tie[:, :, :], incl[:, :, :], ALU.mult))
            then(dve.tensor_tensor(cmp[:, :, :], cmp[:, :, :], tie[:, :, :], ALU.add))
            then(dve.tensor_reduce(keep, cmp[:, :, :].rearrange("p e n -> p n e"), AX.X, ALU.add))
            then(dve.tensor_tensor(by_t(keep_z[:, 0:TR]), by_t(keep), rk[:, 11, :].rearrange("p (t o) -> p t o", o=1).to_broadcast([P, GC, GT]), ALU.mult))
            dve.tensor_reduce(keep_z[:, TR:TR + 1], keep_z[:, 0:TR], AX.X, ALU.add)
            by_group(pick_k, by_t(keep))
            dve.drain().then_inc(s_keep_ready, 1)
            dve.wait_ge(s_keep_mm, 1)
            dve.tensor_copy(zs[:, 0:1], mm[1][:, 256:257])
            then(dve.tensor_copy(out_keep[:, :], mm[2][:, 0:OC]))
            then(dve.tensor_scalar(zk[:, 0, :], iota_z[:, :], zs[:, 0:1], None, ALU.is_lt))
            dve.tensor_scalar(zk[:, 1, :], zk[:, 0, :], -1.0, 1.0, ALU.mult, ALU.add)
            then(dve.tensor_scalar(zs[:, 3:4], zk[:, 0, 0:1], -NOWHERE, NOWHERE, ALU.mult, ALU.add))
            then(dve.scalar_tensor_tensor(out=zs_i[:, 0:1], in0=zk[:, 0, 0:1], scalar=zlist[:, 0:1], in1=zs[:, 3:4], op0=ALU.mult, op1=ALU.add))
            for r_ in range(GT):
                dve.tensor_scalar(zt[:, r_, :], bz, zk[:, 1, r_:r_ + 1], None, ALU.mult)

            dve.wait_ge(s_oz_in, 16)
            then(dve.scalar_tensor_tensor(out=az, in0=oz, scalar=p0, in1=xh0[:, D:2 * D], op0=ALU.mult, op1=ALU.add))
            for r_ in range(GT):
                dve.scalar_tensor_tensor(out=zt[:, r_, :], in0=az, scalar=zk[:, 0, r_:r_ + 1], in1=zt[:, r_, :], op0=ALU.mult, op1=ALU.add)
            dve.drain().then_inc(s_zt_ready, 1)
            with dve.Fori(0, n) as c:
                dve.drain()
                dve.tensor_copy(step_cols[:, 0, :], out_place[:, bass.ds(c * BU, BU)])
                then(dve.tensor_copy(step_cols[:, 1, :], out_keep[:, bass.ds(c * BU, BU)]))
                for i in range(BU):
                    last = dve.tensor_scalar(sel_t[:, i, :], iota_f[:, :], step_cols[:, 0, i:i + 1], None, ALU.is_equal)
                last.then_inc(s_selt_ready, 1)
                dve.wait_ge(s_cx_in, c * 32 + 32)
                dve.scalar_tensor_tensor(out=rd[:, 0:D], in0=xg[:, 0:D], scalar=prob_c[:, bass.ds(c + 1, 1)], in1=xg[:, D:2 * D], op0=ALU.mult, op1=ALU.add)
                then(dve.tensor_tensor(rd[:, D:2 * D], og, xg[:, 0:D], ALU.subtract))
                dve.tensor_scalar(rd[:, D:2 * D], rd[:, D:2 * D], prob_c[:, bass.ds(c + 1, 1)], None, ALU.mult)
                dve.drain().then_inc(s_rd_ready, 1)
                dve.wait_ge(s_sel_mm, c + 1)
                dve.tensor_copy(sel[:, :, :].rearrange("p s m -> p (s m)"), ps_t[:, :]).then_inc(s_sel_ready, 1)
                dve.wait_ge(s_yo_free, c + 1)
                for i in range(BU):
                    dve.wait_ge(s_row_mm, c * BU + i + 1)
                    then(dve.tensor_copy(yo[:, i, :], mm[i][:, 0:D]))
                    dve.scalar_tensor_tensor(out=yo[:, i, :], in0=mm[i][:, D:2 * D], scalar=step_cols[:, 1, i:i + 1], in1=yo[:, i, :],
                                             op0=ALU.mult, op1=ALU.add).then_inc(s_y_ready, 1)
            dve.nop()

_INS = ["x", "L0_tok_emb", "L0_attn_W_qkv", "L0_attn_b_qkv", "L0_attn_W_proj", "L0_attn_b_proj",
        "L0_ffn_switch_w", "L0_ffn_switch_b", "L0_ffn_w1", "L0_ffn_b1", "L0_ffn_w2", "L0_ffn_b2"]

def kernel(**inputs):
    import numpy as _np
    import concourse.bacc as _bacc
    from concourse.bass_utils import run_bass_kernel_spmd as _run

    nc = _bacc.Bacc("TRN2", target_bir_lowering=False, num_devices=1)
    arrays, args = {}, []
    for name in _INS:
        a = _np.ascontiguousarray(inputs[name])
        arrays[f"in_{name}"] = a
        args.append(nc.dram_tensor(f"in_{name}", a.shape, mybir.dt.from_np(a.dtype), kind="ExternalInput").ap())
    args.append(nc.dram_tensor("out_0", (B, T, D), F32, kind="ExternalOutput").ap())
    build(nc, *args)
    r = _run(nc, [arrays], core_ids=[0])
    return r.results[0]["out_0"]
```

```python
from contextlib import ExitStack

import concourse.bass as bass
from concourse import mybir

ALU = mybir.AluOpType
ACT = mybir.ActivationFunctionType
AX = mybir.AxisListType
F32 = mybir.dt.float32
BF16 = mybir.dt.bfloat16
I32 = mybir.dt.int32

P = 128
B, T = 64, 128
N = B * T
D = 192
HEADS = 8
HD = HEADS * D
DH = D // 2
GT = T // HEADS
G = N // GT
GC = G // P
CG = P // GT
UNIT = 2
CU = P // UNIT
BU = GT // UNIT
CHUNKS = (G + 1 + CG - 1) // CG
OC = BU * CHUNKS
OH = OC // 2
SET = 4
SETS = BU // SET
LOG_BU = BU.bit_length() - 1
LOG_CU = CU.bit_length() - 1
COLS = 80
E = 8
F = 768
FC = F // P
CAP = int(1.25 * N / E)
TILES = (CHUNKS * P + E * (P - 1)) // P
FOUR = 4
PAIR = 2
PROBES = 28
SPLIT = (2, 3, 4, 5, 6)
LEAST = SPLIT[-1] + 1
ROW = D + 4
FILLS = 8
FILLED = 4
EPS = 1e-5
NOWHERE = 65536.0
VOCAB_PAD = -1.0
assert TILES + FOUR <= COLS and CHUNKS + 1 + FOUR <= COLS

def build(nc, x, emb, w_qkv, b_qkv, w_proj, b_proj, sw, sb_, w1, b1, w2, b2, out):
    ctx = ExitStack()
    with ctx:
        def sb(name, shape, dt=F32):
            return ctx.enter_context(nc.sbuf_tensor(name, shape, dt))

        def sem(name):
            return ctx.enter_context(nc.semaphore(name))

        pred_d = nc.dram_tensor("pred_d", (N,), F32, kind="Internal").ap()
        prob_d = nc.dram_tensor("prob_d", (CHUNKS * CU, 2 * GT), F32, kind="Internal").ap()
        xh_d = nc.dram_tensor("xh_d", ((CHUNKS + FOUR) * P, 2 * D), F32, kind="Internal").ap()
        xs_d = nc.dram_tensor("xs_d", ((TILES + E + FOUR) * P, ROW), F32, kind="Internal").ap()
        o_d = nc.dram_tensor("o_d", ((CHUNKS + 1) * P, D), F32, kind="Internal").ap()
        v_d = nc.dram_tensor("v_d", (P, HD), F32, kind="Internal").ap()
        x_rows = x.rearrange("b (t o) -> (b t) o", o=1)
        out_rows = out.rearrange("b t d -> (b t) d")
        out_groups = out.rearrange("b (g r) d -> (b g) (r d)", r=GT)

        area = sb("area", [P, 2 * 3 * HD])
        wqkv_s = area[0:DH + 1, :].rearrange("p (h n) -> p h n", h=2)
        wproj_s = sb("wproj_s", [DH, 2 * HEADS, D])
        bproj_s = sb("bproj_s", [1, D])
        wsw_s = sb("wsw_s", [DH + 1, 2, E])
        w1_s = sb("w1_s", [DH + 1, 2, E, F])
        w2_s = sb("w2_s", [P, FC, E, D])
        WORK = 11264
        work = sb("work", [P, WORK])

        ident = sb("ident", [P, P])
        ones = sb("ones", [P, P])
        before = sb("before", [P, P])
        first = sb("first", [P, P])
        iota_f = sb("iota_f", [P, P])
        iota_q = sb("iota_q", [P, CG, GT])
        iota_g = sb("iota_g", [P, GC])
        iota_z = sb("iota_z", [P, GT])
        iota_u = sb("iota_u", [P, CU, UNIT])
        iota_k = sb("iota_k", [P, GT])
        iota_k1 = sb("iota_k1", [P, GT])
        iota_o = sb("iota_o", [P, OC])
        iota_b = sb("iota_b", [BU, CHUNKS * CG])
        tok_of = sb("tok_of", [P, GC, GT])
        place_of = sb("place_of", [P, COLS])
        units = sb("units", [BU, HEADS, GT], BF16)
        others = sb("others", [BU, HEADS, GT], BF16)
        pred_base = sb("pred_base", [B, T])
        minus_half = sb("minus_half", [P, 1])
        match_j = sb("match_j", [P, B])

        pred_i = sb("pred_i", [P, COLS], I32)
        match_f = sb("match_f", [P, COLS])
        mult_c = sb("mult_c", [P, COLS])
        valid = sb("valid", [P, COLS])
        prob_c = sb("prob_c", [P, COLS])
        route_c = sb("route_c", [P, COLS])
        not_big = sb("not_big", [BU, CHUNKS * CG])
        slot_f = sb("slot_f", [P, COLS])
        slot_i = sb("slot_i", [P, COLS], I32)
        place_v = sb("place_v", [P, COLS])
        zero = sb("zero", [P, 2 * D])
        ones_b = sb("ones_b", [P, P], BF16)
        idx_4 = sb("idx_4", [P, SET], I32)
        idx_2 = idx_4[:, 0:PAIR]
        zroute = sb("zroute", [P, 1])
        left_f = sb("left_f", [P, 1])
        place_1 = sb("place_1", [P, 1])
        expert_i = sb("expert_i", [1, COLS], I32)
        zlist = sb("zlist", [P, 1])
        counts_i = sb("counts_i", [1, 3], I32)
        pick_c = sb("pick_c", [P, GC, COLS])
        classes = sb("classes", [P, 2, GC])
        act = sb("act", [P, GC])
        place_k = sb("place_k", [P, GC, GT])
        unit_i = sb("unit_i", [P, GC], I32)

        idx_a = sb("idx_a", [P, 1], I32)
        tid = sb("tid", [P, 1], I32)
        emb_t = sb("emb_t", [P, D])
        h_next = sb("h_next", [P, D])
        h_cur = sb("h_cur", [P, D])
        xn = sb("xn", [P, D])
        xh = sb("xh", [P, 2 * D])
        xf = xh[:, 0:D]
        h1 = xh[:, D:2 * D]
        xt = sb("xt", [DH + 1, 2, P])
        xft = sb("xft", [DH + 1, 2, P])
        st = sb("st", [P, 12])
        st2 = sb("st2", [P, 12])
        rt = sb("rt", [P, 64])
        sm = sb("sm", [P, 4, CG])
        rk = sb("rk", [P, 24, GC])
        rki = sb("rki", [P, 6, GC], I32)
        mrow = sb("mrow", [P, P])
        mdiag = sb("mdiag", [P, P])
        sides = sb("sides", [BU, CG, HEADS, GT], BF16)
        pl = match_f

        banks = [ctx.enter_context(nc.psum_tensor(f"bank{i}", [P, 512], F32)) for i in range(8)]
        mm = banks[0:4]
        ps_s = banks[4:6]
        ps_t = banks[6]
        ps_m = banks[7]
        ps_y = ps_m[:, 0:D]
        ps_x = ps_m[:, D:D + P]
        ps_x2 = ps_m[:, D + P:D + 2 * P]
        ps_l = ps_m[:, D + 2 * P:D + 2 * P + E]

        RB = 8
        NB = B // RB
        starts = [T - 16 * (k + 1) for k in range(NB)]
        lens = [T - s for s in starts]
        offs = [RB * sum(lens[:k]) for k in range(NB + 1)]
        XW = 2 * T + 2

        TR = GC * GT
        used = [0]

        def cut(base, n):
            a = used[0]
            used[0] += n
            assert used[0] <= base.shape[1]
            return base[:, a:a + n]

        eq = cut(work, offs[-1])
        run = cut(work, offs[-1])
        x_i = cut(work, T).bitcast(I32)
        x_f = cut(work, T)
        x_pad_at = used[0]
        x_pad = cut(work, XW)
        best = cut(work, T)
        tmp_b = cut(work, T)
        tmp_i = cut(work, T).bitcast(I32)
        v4 = cut(work, N // P).rearrange("p (t r) -> p t r", t=GC)
        used[0] = 0
        v16 = cut(work, TR).rearrange("p (t k) -> p t k", t=GC)
        m16 = cut(work, TR).rearrange("p (t k) -> p t k", t=GC)
        m16b = cut(work, TR).rearrange("p (t k) -> p t k", t=GC)
        m4 = cut(work, TR).rearrange("p (t r) -> p t r", t=GC)
        cum = cut(work, TR).rearrange("p (t r) -> p t r", t=GC)
        reset_g = cut(work, TR).rearrange("p (t r) -> p t r", t=GC)
        spread = cut(work, TR * GT).rearrange("p (t k r) -> p t k r", t=GC, k=GT)
        pick_s = cut(work, GC * P).rearrange("p (t m) -> p t m", t=GC)
        pick_b = cut(work, GC * P).rearrange("p (t m) -> p t m", t=GC)
        pick_v = cut(work, GC * P).rearrange("p (t m) -> p t m", t=GC)
        pick_m = cut(work, GC * P).rearrange("p (t m) -> p t m", t=GC)
        pick_x = cut(work, GC * P).rearrange("p (t m) -> p t m", t=GC)
        pick_z = cut(work, GC * P).rearrange("p (t m) -> p t m", t=GC)
        assert used[0] <= 2 * offs[-1]

        used[0] = 0
        qt = cut(work, 2 * HEADS * P)[0:DH, :].rearrange("p (h g j r) -> p h g j r", h=2, g=CG, j=HEADS)
        kt = cut(work, 2 * HEADS * P)[0:DH, :].rearrange("p (h g j r) -> p h g j r", h=2, g=CG, j=HEADS)
        vn = cut(work, HD)
        vp = cut(work, CG * D).rearrange("p (g v) -> p g v", g=CG)
        ex = cut(work, CG * P).rearrange("p (g l) -> p g l", g=CG)
        pt = cut(work, CG * P).rearrange("p (g l) -> p g l", g=CG)
        ot = cut(work, 2 * HEADS * P)[0:DH, :].rearrange("p (h j t) -> p h j t", h=2, j=HEADS)

        used[0] = 0
        gx = cut(work, ROW)
        gxt = cut(work, 2 * P)[0:DH + 1, :].rearrange("p (h t) -> p h t", h=2)
        hs = cut(work, F)
        ht = cut(work, F).rearrange("p (c t) -> p c t", c=FC)
        ob = cut(work, D)
        b2_s = cut(work, E * D)[0:1, :].rearrange("p (e d) -> p e d", e=E)
        sx = cut(work, PAIR * ROW).rearrange("p (a n) -> p a n", a=PAIR)
        xg = cut(work, 2 * D)
        og = cut(work, D)
        rd = cut(work, 2 * D)
        yo = cut(work, SET * D).rearrange("p (s n) -> p s n", s=SET)
        step_cols = cut(work, 2 * SET).rearrange("p (w s) -> p w s", w=2)
        xh0 = cut(work, 2 * D)
        bz = cut(work, D)
        az = cut(work, D)
        oz = cut(work, D)
        zt_flat = cut(work, GT * D)
        zt = zt_flat.rearrange("p (r d) -> p r d", r=GT)
        zk = cut(work, 2 * GT).rearrange("p (a r) -> p a r", a=2)
        p0 = cut(work, 1)
        zs = cut(work, 4)
        zs_i = cut(work, 2).bitcast(I32)

        used[0] = 0
        full = cut(area, GC * 2 * GT).rearrange("p (t w r) -> p t w r", t=GC, w=2)
        pT = cut(area, 2 * (P + GT))[0:CHUNKS, :].rearrange("p (w m) -> p w m", w=2)
        pT_at = GC * 2 * GT
        pTx = zt_flat[0:CHUNKS, 0:CU * 2 * GT].rearrange("p (u w k) -> p u w k", u=CU, w=2)
        pick_o = zt_flat[:, 0:GC * OC].rearrange("p (t n) -> p t n", t=GC)
        at_slots = used[0]
        member = cut(area, E * TR).rearrange("p (e n) -> p e n", e=E)
        score = cut(area, E * TR).rearrange("p (e n) -> p e n", e=E)
        at_cmp = used[0]
        cmp = cut(area, E * TR).rearrange("p (e n) -> p e n", e=E)
        tie = cut(area, E * TR).rearrange("p (e n) -> p e n", e=E)
        at_incl = used[0]
        incl = cut(area, E * TR).rearrange("p (e n) -> p e n", e=E)
        room = cut(area, E * TR)
        reset_r = cut(area, E * TR).rearrange("p (n r) -> p n r", r=GT)
        thr = cut(area, E)
        cand = cut(area, E)
        red = cut(area, E)
        rem = cut(area, E)
        step = cut(area, 1)
        trow = cut(area, E * GC).rearrange("p (e t) -> p e t", e=E)
        tbase = cut(area, E * GC).rearrange("p (e t) -> p e t", e=E)
        tsum = cut(area, E * GC).rearrange("p (e t) -> p e t", e=E)
        keep = cut(area, TR)
        keep_z = cut(area, TR + 1)
        pick_k = incl[:, :, :].rearrange("p e n -> p (e n)").rearrange("p (t m) -> p t m", t=GC)
        pick_s2 = tie[:, :, :].rearrange("p e n -> p (e n)").rearrange("p (t m) -> p t m", t=GC)
        pick_u = cut(area, GC * P).rearrange("p (t m) -> p t m", t=GC)
        out_tok = cut(area, OC + SET).bitcast(I32)
        out_place = cut(area, OC + SET)
        out_keep = cut(area, OC + SET)
        tl = cut(area, 8 * E).rearrange("p (a e) -> p a e", a=8)
        tl_i = cut(area, 2 * E).bitcast(I32).rearrange("p (a e) -> p a e", a=2)
        tcmp = cut(area, TILES * E).rearrange("p (t e) -> p t e", e=E)[0:1]
        texp = cut(area, TILES)[0:1, :]
        slot_v = cut(area, TR)
        hit = cut(area, E * TR // 2).bitcast(BF16).rearrange("p (e n) -> p e n", e=E)
        used[0] = at_slots
        reset_c = cut(area, E * CHUNKS).rearrange("p (e c) -> p e c", e=E)
        eqc = cut(area, E * CHUNKS).rearrange("p (e c) -> p e c", e=E)
        csum = cut(area, E * CHUNKS).rearrange("p (e c) -> p e c", e=E)
        cinc = cut(area, E * CHUNKS).rearrange("p (e c) -> p e c", e=E)
        posn = cut(area, E * CHUNKS).rearrange("p (e c) -> p e c", e=E)
        assert used[0] <= at_incl + 2 * E * TR
        sel_t = score[:, 0:E, :].rearrange("p e n -> p (e n)").rearrange("p (s m) -> p s m", s=SET)
        sel = cmp[:, 0:E, :].rearrange("p e n -> p (e n)").rearrange("p (s m) -> p s m", s=SET)
        at_place = area[:, at_cmp:at_cmp + TR * GT].rearrange("p (n k) -> p n k", k=GT)
        at_work = area[:, at_incl:at_incl + TR * GT].rearrange("p (n k) -> p n k", k=GT)

        s_above_mm = sem("s_above_mm")
        s_above_ready = sem("s_above_ready")
        s_act_ready = sem("s_act_ready")
        s_act_tiles = sem("s_act_tiles")
        s_b2_in = sem("s_b2_in")
        s_best_out = sem("s_best_out")
        s_bz_ready = sem("s_bz_ready")
        s_consts = sem("s_consts")
        s_counts = sem("s_counts")
        s_cx_in = sem("s_cx_in")
        s_dev_ready = sem("s_dev_ready")
        s_dve_tiles = sem("s_dve_tiles")
        s_emb_in = sem("s_emb_in")
        s_emb_used = sem("s_emb_used")
        s_eqc_mm = sem("s_eqc_mm")
        s_eqc_ready = sem("s_eqc_ready")
        s_exp_ready = sem("s_exp_ready")
        s_fill_out = sem("s_fill_out")
        s_full_in = sem("s_full_in")
        s_gx_in = sem("s_gx_in")
        s_gxt_mm = sem("s_gxt_mm")
        s_gxt_ready = sem("s_gxt_ready")
        s_h_mm = sem("s_h_mm")
        s_hit_mm = sem("s_hit_mm")
        s_hit_ready = sem("s_hit_ready")
        s_hs_ready = sem("s_hs_ready")
        s_ht_act = sem("s_ht_act")
        s_ht_mm = sem("s_ht_mm")
        s_id_in = sem("s_id_in")
        s_idx_set = sem("s_idx_set")
        s_keep_mm = sem("s_keep_mm")
        s_keep_ready = sem("s_keep_ready")
        s_l_mm = sem("s_l_mm")
        s_left_known = sem("s_left_known")
        s_lexp_ready = sem("s_lexp_ready")
        s_lmax_ready = sem("s_lmax_ready")
        s_max_ready = sem("s_max_ready")
        s_mdiag = sem("s_mdiag")
        s_mrow_mm = sem("s_mrow_mm")
        s_mrow_ready = sem("s_mrow_ready")
        s_o_clear = sem("s_o_clear")
        s_o_done = sem("s_o_done")
        s_o_mm = sem("s_o_mm")
        s_o_out = sem("s_o_out")
        s_ob_ready = sem("s_ob_ready")
        s_ob_stored = sem("s_ob_stored")
        s_ones_set = sem("s_ones_set")
        s_oz_in = sem("s_oz_in")
        s_p0_mm = sem("s_p0_mm")
        s_p_ready = sem("s_p_ready")
        s_picks = sem("s_picks")
        s_picks_mm = sem("s_picks_mm")
        s_pl_ready = sem("s_pl_ready")
        s_pool_steps = sem("s_pool_steps")
        s_pred_back = sem("s_pred_back")
        s_probT_mm = sem("s_probT_mm")
        s_probT_ready = sem("s_probT_ready")
        s_prob_out = sem("s_prob_out")
        s_pt_mm = sem("s_pt_mm")
        s_pt_ready = sem("s_pt_ready")
        s_rank_mm = sem("s_rank_mm")
        s_rd_ready = sem("s_rd_ready")
        s_row_copied = sem("s_row_copied")
        s_row_mm = sem("s_row_mm")
        s_s_mm = sem("s_s_mm")
        s_sel_mm = sem("s_sel_mm")
        s_sel_ready = sem("s_sel_ready")
        s_selt_ready = sem("s_selt_ready")
        s_sides = sem("s_sides")
        s_slots_known = sem("s_slots_known")
        s_small_in = sem("s_small_in")
        s_sp_steps = sem("s_sp_steps")
        s_steps_mm = sem("s_steps_mm")
        s_steps_read = sem("s_steps_read")
        s_steps_ready = sem("s_steps_ready")
        s_sx_free = sem("s_sx_free")
        s_sx_in = sem("s_sx_in")
        s_tables = sem("s_tables")
        s_tie_mm = sem("s_tie_mm")
        s_tie_ready = sem("s_tie_ready")
        s_tile_mm = sem("s_tile_mm")
        s_v_copied = sem("s_v_copied")
        s_v_moved = sem("s_v_moved")
        s_v_stored = sem("s_v_stored")
        s_var_ready = sem("s_var_ready")
        s_w1_in = sem("s_w1_in")
        s_w2_in = sem("s_w2_in")
        s_wproj_in = sem("s_wproj_in")
        s_wqkv_in = sem("s_wqkv_in")
        s_x_in = sem("s_x_in")
        s_xf_out = sem("s_xf_out")
        s_xf_ready = sem("s_xf_ready")
        s_xft_mm = sem("s_xft_mm")
        s_xft_ready = sem("s_xft_ready")
        s_xh_clear = sem("s_xh_clear")
        s_xn_ready = sem("s_xn_ready")
        s_xs_clear = sem("s_xs_clear")
        s_xs_done = sem("s_xs_done")
        s_xs_out = sem("s_xs_out")
        s_xt_mm = sem("s_xt_mm")
        s_xt_ready = sem("s_xt_ready")
        s_y_mm = sem("s_y_mm")
        s_y_out = sem("s_y_out")
        s_y_ready = sem("s_y_ready")
        s_yo_free = sem("s_yo_free")
        s_z_out = sem("s_z_out")
        s_zrow_in = sem("s_zrow_in")
        s_zt_ready = sem("s_zt_ready")

        block = ctx.enter_context(nc.Block())

        @block.sync
        def _(sp):
            sp.sem_inc(s_v_moved, 128)
            sp.sem_inc(s_xf_out, 16)
            sp.sem_inc(s_y_mm, 1)
            sp.sem_inc(s_pt_ready, 1)
            sp.sem_inc(s_emb_used, 1)
            sp.sem_inc(s_ob_stored, 1)
            sp.sem_inc(s_sx_free, 1)
            sp.sem_inc(s_yo_free, 1)
            sp.dma_start(x_i[0:B, :], x).then_inc(s_x_in, 16)
            sp.dma_start(x_i[B:2 * B, :], x).then_inc(s_x_in, 16)
            sp.dma_start(wqkv_s[0:DH, 0, :], w_qkv[0:DH, :]).then_inc(s_wqkv_in, 16)
            sp.dma_start(wqkv_s[0:DH, 1, :], w_qkv[DH:D, :]).then_inc(s_wqkv_in, 16)
            sp.dma_start(wqkv_s[DH:DH + 1, 0, :], b_qkv.rearrange("(o n) -> o n", o=1)).then_inc(s_wqkv_in, 16)
            sp.wait_ge(s_best_out, 1)
            sp.dma_start(pred_d.rearrange("(b t) -> b t", t=T), best[0:B, :]).then_inc(s_pred_back, 16)
            sp.wait_ge(s_pred_back, 16)
            sp.dma_start(v4, pred_d.rearrange("(t p r) -> p t r", t=GC, r=GT)).then_inc(s_pred_back, 16)
            for f in range(FC):
                sp.dma_start(w2_s[:, f, :, :], w2.rearrange("e (c p) d -> c p e d", p=P)[f]).then_inc(s_w2_in, 16)

            sp.wait_ge(s_counts, 1)
            n = sp.value_load(counts_i[0:1, 0:1], min_val=1, max_val=CHUNKS)
            sp.dma_start(xh_d[bass.ds(n * P, FOUR * P), :].rearrange("(a p) d -> p a d", p=P),
                         zero[:, 0:2 * D].rearrange("p (a d) -> p a d", a=1).to_broadcast([P, FOUR, 2 * D])).then_inc(s_xh_clear, 16)
            with sp.Fori(0, n + 1) as c:
                sp.dma_start(o_d[bass.ds(c * P, P), :], zero[:, 0:D]).then_inc(s_o_clear, 16)
            with sp.Fori(0, n + E + FOUR) as t:
                sp.dma_start(xs_d[bass.ds(t * P, P), :], zero[:, 0:ROW]).then_inc(s_xs_clear, 16)
            with sp.Fori(0, n) as c:
                sp.wait_ge(s_v_copied, c + 1)
                sp.sem_inc(s_sp_steps, 1)
                sp.wait_ge(s_y_mm, c + 1)
                sp.sem_inc(s_sp_steps, 1)
                sp.dma_start(v_d, vn).then_inc(s_v_stored, 16)
                sp.wait_ge(s_v_stored, c * 16 + 16)
                sp.sem_inc(s_sp_steps, 1)
                for j in range(HEADS):
                    sp.dma_start(vp[GT * j:GT * (j + 1), :, :],
                                 v_d[:, j * D:(j + 1) * D].rearrange("(g r) v -> r g v", r=GT)).then_inc(s_v_moved, 16)
                sp.wait_ge(s_xf_ready, c + 2)
                sp.sem_inc(s_sp_steps, 1)
                sp.dma_start(xh_d[bass.ds(c * P, P), :], xh[:, :]).then_inc(s_xf_out, 16)
                sp.wait_ge(s_xf_out, c * 16 + 32)
                sp.sem_inc(s_sp_steps, 1)

            sp.wait_ge(s_xh_clear, 16)
            sp.dma_start(xh0, xh_d[0:1, :].to_broadcast([P, 2 * D])).then_inc(s_zrow_in, 16)
            sp.dma_start(b2_s[0:1, :, :], b2.rearrange("(o e) d -> o e d", o=1)).then_inc(s_b2_in, 16)
            sp.wait_ge(s_probT_ready, 2)
            sp.dma_start(prob_d.rearrange("(c u) n -> c u n", u=CU),
                         pTx[:, :, :, :].rearrange("c u w k -> c u (w k)")).then_inc(s_prob_out, 16)
            with sp.Fori(0, n, PAIR) as c:
                sp.wait_ge(s_sx_free, c + 1)
                sp.sem_inc(s_sp_steps, 1)
                sp.dma_start(sx[:, :, 0:D], xh_d[bass.ds(c * P, PAIR * P), 0:D].rearrange("(a p) d -> p a d", p=P)).then_inc(s_sx_in, 16)
            sp.wait_ge(s_slots_known, 1)
            m = sp.value_load(counts_i[0:1, 1:2], min_val=1, max_val=TILES)
            sp.wait_ge(s_xs_done, 1)
            sp.dma_start(gx, xs_d[0:P, :]).then_inc(s_gx_in, 16)
            with sp.Fori(0, m) as t:
                sp.wait_ge(s_gxt_ready, t + 1)
                sp.sem_inc(s_sp_steps, 1)
                sp.wait_ge(s_pl_ready, t + 1)
                sp.sem_inc(s_sp_steps, 1)
                sp.dma_start(gx, xs_d[bass.ds(t * P + P, P), :]).then_inc(s_gx_in, 16)
            sp.dma_start(xg, xh_d[0:P, :]).then_inc(s_cx_in, 16)
            sp.wait_ge(s_o_done, 1)
            sp.dma_start(og, o_d[0:P, :]).then_inc(s_cx_in, 16)
            sp.dma_start(oz, o_d[0:1, :].to_broadcast([P, D])).then_inc(s_oz_in, 16)
            with sp.Fori(0, n) as c:
                sp.wait_ge(s_rd_ready, c + 1)
                sp.sem_inc(s_sp_steps, 1)
                sp.dma_start(og, o_d[bass.ds(c * P + P, P), :]).then_inc(s_cx_in, 16)
                sp.dma_start(xg, xh_d[bass.ds(c * P + P, P), :]).then_inc(s_cx_in, 16)
            sp.wait_ge(s_cx_in, n * 32 + 32)
            sp.sem_inc(s_sp_steps, 1)
            sp.nop()

        @block.gpsimd
        def _(pool):
            pool.memset(ones[:, :], 1.0)
            pool.memset(ident[:, :], 0.0)
            pool.memset(first[:, :], 0.0)
            pool.drain()
            pool.memset(first[0:1, :], 1.0)
            pool.affine_select(out=ident[:, :], in_=ident[:, :], compare_op=ALU.not_equal, fill=1.0, base=0,
                               pattern=[[-1, P]], channel_multiplier=1)
            pool.affine_select(out=before[:, :], in_=ones[:, :], compare_op=ALU.is_gt, fill=0.0, base=0,
                               pattern=[[1, P]], channel_multiplier=-1)

            def iota(out_, pattern, base, mult):
                return pool.iota(out_, pattern, base=base, channel_multiplier=mult, allow_small_or_imprecise_dtypes=True)

            pool.drain()
            iota(match_j[0:B, :], [[2, B]], 1, 0)
            iota(match_j[B:2 * B, :], [[2, B]], 0, 0)
            pool.drain()
            iota(pred_base[:, :], [[1, T]], 2 - T, T)
            iota(iota_f[:, :], [[1, P]], 0, 0)
            iota(iota_q[:, :, :], [[1, CG], [0, GT]], 0, 0)
            iota(iota_g[:, :], [[P, GC]], 0, 1)
            iota(iota_z[:, :], [[1, GT]], 0, GT)
            iota(iota_u[:, :, :], [[1, CU], [0, UNIT]], 0, 0)
            iota(iota_k[:, :], [[1, GT]], 0, 0)
            iota(iota_k1[:, :], [[1, GT]], 1, 0)
            iota(iota_o[:, :], [[1, OC]], 0, 0)
            iota(tok_of[:, :, :], [[-P * GT, GC], [-1, GT]], int(NOWHERE), -GT)
            iota(place_of[:, :], [[-P, COLS]], int(NOWHERE), -1)
            pool.drain()
            iota(iota_b[:, :], [[1, CHUNKS * CG]], 0, 0)
            pool.memset(units[:, :, :], 1.0)
            pool.memset(others[:, :, :], -1e30)
            pool.drain()
            pool.affine_select(out=units[:, :, :], in_=units[:, :, :], compare_op=ALU.is_ge, fill=0.0, base=0,
                               pattern=[[0, HEADS], [1, GT]], channel_multiplier=-UNIT)
            pool.drain()
            pool.affine_select(out=units[:, :, :], in_=units[:, :, :], compare_op=ALU.is_ge, fill=0.0, base=UNIT - 1,
                               pattern=[[0, HEADS], [-1, GT]], channel_multiplier=UNIT)
            pool.drain()
            pool.tensor_tensor(sides[:, 0, :, :], others[:, :, :], units[:, :, :], ALU.mult)
            pool.drain()
            pool.tensor_tensor(others[:, :, :], others[:, :, :], sides[:, 0, :, :], ALU.subtract)
            pool.drain()
            pool.memset(xt[DH:DH + 1, 0, :], 1.0)
            pool.memset(xft[DH:DH + 1, 0, :], 1.0)
            pool.drain()
            pool.memset(minus_half[:, :], -0.5)
            pool.memset(xf, 0.0)
            pool.memset(prob_c[:, :], 0.0)
            pool.memset(route_c[:, :], 0.0)
            pool.memset(zero[:, :], 0.0)
            pool.memset(ones_b[:, :], 1.0)
            pool.memset(expert_i[:, :], 0)
            pool.drain().then_inc(s_consts, 1)

            def fetch(c):
                pool.tensor_copy(idx_a[:, :], pred_i[:, bass.ds(c, 1)]).then_inc(s_idx_set, 1)
                pool.wait_ge(s_idx_set, c + 1)
                pool.sem_inc(s_pool_steps, 1)
                pool.indirect_dma_start(tid[:, :], None, x_rows, bass.IndirectOffsetOnAxis(ap=idx_a[:, 0:1], axis=0)).then_inc(s_id_in, 16)
                pool.wait_ge(s_id_in, c * 16 + 16)
                pool.sem_inc(s_pool_steps, 1)
                pool.wait_ge(s_emb_used, c + 1)
                pool.sem_inc(s_pool_steps, 1)
                pool.indirect_dma_start(emb_t[:, :], None, emb, bass.IndirectOffsetOnAxis(ap=tid[:, 0:1], axis=0)).then_inc(s_emb_in, 16)
                pool.wait_ge(s_emb_in, c * 16 + 16)
                pool.sem_inc(s_pool_steps, 1)

            pool.wait_ge(s_counts, 1)
            pool.wait_ge(s_tables, 1)
            pool.sem_inc(s_s_mm, 1)
            n = pool.value_load(counts_i[0:1, 0:1], min_val=1, max_val=CHUNKS)
            def deviation(s, count):
                pool.wait_ge(s_var_ready, count)
                pool.sem_inc(s_pool_steps, 1)
                pool.tensor_scalar(s[:, 9:10], s[:, 7:8], EPS, None, ALU.add)
                pool.drain()
                pool.tensor_tensor(s[:, 8:9], s[:, 9:10], minus_half[:, :], ALU.pow).then_inc(s_dev_ready, 1)

            fetch(0)
            deviation(st, 1)
            fetch(1)
            with pool.Fori(0, n) as c:
                pool.wait_ge(s_s_mm, c * 2 + 1)
                pool.sem_inc(s_pool_steps, 1)
                for q in range(CG):
                    pool.tensor_tensor(sides[:, q, :, :].rearrange("p j k -> p (j k)"), units[:, :, :].rearrange("p j k -> p (j k)"),
                                       not_big[:, bass.ds(c * CG + q, 1)].to_broadcast([BU, P]), ALU.mult)
                pool.drain().then_inc(s_sides, 1)
                deviation(st, c * 2 + 2)
                fetch(c + 2)
                deviation(st2, c * 2 + 3)

            pool.wait_ge(s_prob_out, 16)
            for t in range(GC):
                pool.indirect_dma_start(full[:, t, :, :].rearrange("p w r -> p (w r)"), None, prob_d,
                                        bass.IndirectOffsetOnAxis(ap=unit_i[:, t:t + 1], axis=0)).then_inc(s_full_in, 16)

            pool.wait_ge(s_slots_known, 1)
            pool.wait_ge(s_xs_clear, n * 16 + 16 * (E + FOUR))
            pool.sem_inc(s_pool_steps, 1)
            with pool.Fori(0, n, PAIR) as c:
                pool.wait_ge(s_sx_in, c * (16 // PAIR) + 16)
                pool.sem_inc(s_pool_steps, 1)
                pool.tensor_copy(idx_2[:, :], slot_i[:, bass.ds(c, PAIR)])
                pool.tensor_copy(sx[:, :, D], place_of[:, bass.ds(c, PAIR)])
                pool.tensor_copy(sx[:, :, D + 1:ROW], zero[:, 0:3 * PAIR].rearrange("p (a n) -> p a n", a=PAIR))
                pool.drain()
                for i in range(PAIR):
                    pool.indirect_dma_start(xs_d, bass.IndirectOffsetOnAxis(ap=idx_2[:, i:i + 1], axis=0), sx[:, i, :], None,
                                            bounds_check=TILES * P - 1, oob_is_err=False).then_inc(s_xs_out, 16)
                pool.wait_ge(s_xs_out, c * 16 + PAIR * 16)
                pool.sem_inc(s_sx_free, PAIR)
            pool.sem_inc(s_xs_done, 1)

            pool.wait_ge(s_o_clear, n * 16 + 16)
            pool.sem_inc(s_pool_steps, 1)
            m = pool.value_load(counts_i[0:1, 1:2], min_val=1, max_val=TILES)
            with pool.Fori(0, m + 1) as t:
                pool.wait_ge(s_ob_ready, t + 1)
                pool.sem_inc(s_pool_steps, 1)
                pool.tensor_copy(place_1[:, :], pl[:, bass.ds(t, 1)])
                pool.drain()
                pool.tensor_scalar(idx_a[:, :], place_1[:, :], -1.0, NOWHERE, ALU.mult, ALU.add)
                pool.drain()
                pool.indirect_dma_start(o_d, bass.IndirectOffsetOnAxis(ap=idx_a[:, 0:1], axis=0), ob, None,
                                        bounds_check=CHUNKS * P - 1, oob_is_err=False).then_inc(s_o_out, 16)
                pool.wait_ge(s_o_out, t * 16 + 16)
                pool.sem_inc(s_ob_stored, 1)
            pool.sem_inc(s_o_done, 1)

            pool.wait_ge(s_fill_out, 16 * FILLS)
            pool.tensor_copy(idx_4[:, :], out_tok[:, 0:SET])
            pool.drain()
            pool.wait_ge(s_zt_ready, 1)
            pool.indirect_dma_start(out_groups, bass.IndirectOffsetOnAxis(ap=zs_i[:, 0:1], axis=0),
                                    zt[:, :, :].rearrange("p r d -> p (r d)"), None,
                                    bounds_check=G - 1, oob_is_err=False).then_inc(s_z_out, 16)
            with pool.Fori(0, n) as c:
                for h in range(SETS):
                    for i in range(SET):
                        pool.wait_ge(s_y_ready, c * BU + h * SET + i + 1)
                        pool.sem_inc(s_pool_steps, 1)
                        pool.indirect_dma_start(out_rows, bass.IndirectOffsetOnAxis(ap=idx_4[:, i:i + 1], axis=0), yo[:, i, :], None,
                                                bounds_check=N - 1, oob_is_err=False).then_inc(s_y_out, 16)
                    pool.wait_ge(s_y_out, c * (BU * 16) + (h + 1) * SET * 16)
                    pool.sem_inc(s_yo_free, 1)
                    pool.tensor_copy(idx_4[:, :], out_tok[:, bass.ds(c * BU + (h + 1) * SET, SET)])
                    pool.drain()
            pool.wait_ge(s_z_out, 16)
            pool.nop()

        @block.scalar
        def _(se):
            se.dma_start(bproj_s[:, :], b_proj.rearrange("(o n) -> o n", o=1)).then_inc(s_small_in, 16)
            se.dma_start(wsw_s[0:DH, :, :], sw.rearrange("(h p) e -> p h e", h=2)).then_inc(s_small_in, 16)
            se.dma_start(wsw_s[DH:DH + 1, 0, :], sb_.rearrange("(o n) -> o n", o=1)).then_inc(s_small_in, 16)
            se.dma_start(wproj_s[:, :, :], w_proj.rearrange("(j p) d -> p j d", p=DH)).then_inc(s_wproj_in, 16)
            se.dma_start(w1_s[0:DH, 0, :, :], w1[:, 0:DH, :].rearrange("e p f -> p e f")).then_inc(s_w1_in, 16)
            se.dma_start(w1_s[0:DH, 1, :, :], w1[:, DH:D, :].rearrange("e p f -> p e f")).then_inc(s_w1_in, 16)
            se.dma_start(w1_s[DH:DH + 1, 0, :, :], b1.rearrange("(o e) f -> o e f", o=1)).then_inc(s_w1_in, 16)
            se.sem_inc(s_act_tiles, 9)

            se.wait_ge(s_counts, 1)
            n = se.value_load(counts_i[0:1, 0:1], min_val=1, max_val=CHUNKS)
            with se.Fori(0, n) as c:
                se.wait_ge(s_v_moved, c * 128 + 128)
                for i in range(3):
                    se.wait_ge(s_tile_mm, c * 15 + i + 1)
                    se.copy(vn[:, 512 * i:512 * (i + 1)], mm[i % 4][:, :]).then_inc(s_act_tiles, 1)
                se.drain().then_inc(s_v_copied, 1)
                for i in range(4):
                    k = 3 + 2 * i
                    se.wait_ge(s_tile_mm, c * 15 + k + 1)
                    se.copy(qt[:, i % 2, :, 4 * (i // 2):4 * (i // 2) + 4, :].rearrange("p g j r -> p j g r"),
                            mm[k % 4][0:DH, :].rearrange("p (j g r) -> p j g r", j=4, g=CG)).then_inc(s_act_tiles, 1)
                for half in range(2):
                    se.wait_ge(s_max_ready, c * 2 + half + 1)
                    for g in range(4 * half, 4 * half + 4):
                        last = se.activation(ex[:, g, :], ps_s[half][:, P * (g % 4):P * (g % 4 + 1)], ACT.Exp, bias=sm[:, 1, g:g + 1])
                    last.then_inc(s_exp_ready, 1)
                se.wait_ge(s_lmax_ready, c + 1)
                se.activation(rt[:, 8:16], ps_l, ACT.Exp, bias=rt[:, 1:2], accum_out=rt[:, 2:3]).then_inc(s_lexp_ready, 1)
                for half in range(2):
                    se.wait_ge(s_pt_mm, c * 2 + half + 1)
                    se.copy(pt[:, 4 * half:4 * half + 4, :].rearrange("p g a -> p (g a)"), ps_t[:, :]).then_inc(s_pt_ready, 1)
                for i in range(2):
                    k = 11 + 2 * i
                    se.wait_ge(s_tile_mm, c * 15 + k + 1)
                    se.copy(ot[:, 0, :, 64 * i:64 * i + 64].rearrange("p j (g r) -> p g j r", r=GT),
                            mm[k % 4][0:DH, :].rearrange("p (g j r) -> p g j r", g=4, j=HEADS)).then_inc(s_act_tiles, 1)
            se.wait_ge(s_lmax_ready, n + 1)
            se.activation(rt[:, 8:16], ps_l, ACT.Exp, bias=rt[:, 1:2], accum_out=rt[:, 2:3]).then_inc(s_lexp_ready, 1)

            se.wait_ge(s_slots_known, 1)
            m = se.value_load(counts_i[0:1, 1:2], min_val=1, max_val=TILES)

            def take_rows(t):
                se.wait_ge(s_gxt_mm, t + 1)
                se.copy(gxt[0:DH, :, :], ps_s[0][0:DH, 0:2 * P].rearrange("p (h t) -> p h t", h=2)).then_inc(s_gxt_ready, 1)
                se.copy(pl[:, bass.ds(t + 1, 1)], gx[:, D:D + 1]).then_inc(s_pl_ready, 1)

            def expert_row(t):
                se.wait_ge(s_o_mm, t + 1)
                se.wait_ge(s_ob_stored, t + 1)
                se.copy(ob, ps_y).then_inc(s_ob_ready, 1)

            se.wait_ge(s_gx_in, 16)
            se.wait_ge(s_ones_set, 1)
            take_rows(0)

            def experts_tile(t):
                for i in range(2):
                    se.wait_ge(s_h_mm, t * 2 + i + 1)
                    se.activation(hs[:, 384 * i:384 * (i + 1)], mm[i][:, 0:384], ACT.Gelu).then_inc(s_hs_ready, 1)
                expert_row(t)
                take_rows(t + 1)
                for i in range(2):
                    se.wait_ge(s_ht_mm, t * 2 + i + 1)
                    se.copy(ht[:, 3 * i:3 * i + 3, :].rearrange("p c t -> p (c t)"), mm[2 + i][:, 0:384]).then_inc(s_ht_act, 1)

            se.wait_ge(s_bz_ready, 1)
            with se.Fori(0, FILLED) as t:
                for i in range(FILLS // FILLED):
                    se.dma_start(out_rows[bass.ds(t * (N // FILLED) + i * (N // FILLS), N // FILLS), :].rearrange("(p r) d -> p r d", p=P),
                                 bz.rearrange("p (r d) -> p r d", r=1).to_broadcast([P, N // P // FILLS, D])).then_inc(s_fill_out, 16)
                experts_tile(t)
            with se.Fori(FILLED, m) as t:
                experts_tile(t)
            expert_row(m)
            with se.Fori(0, n) as c:
                for h in range(SETS):
                    se.wait_ge(s_yo_free, c * SETS + h + 1)
                    for i in range(SET):
                        se.wait_ge(s_row_mm, c * BU + h * SET + i + 1)
                        se.copy(yo[:, i, :], mm[i][:, 0:D]).then_inc(s_row_copied, 1)
            se.nop()

        @block.tensor
        def _(pe):
            pe.wait_ge(s_consts, 1)
            pe.wait_ge(s_act_ready, 1)
            both = classes[:, :, :].rearrange("p a t -> p (a t)")
            pe.matmul(ps_m[:, 0:2 * GC], before[:, :], both, start=True, stop=True)
            pe.matmul(ps_m[:, 2 * GC:4 * GC], ones[:, :], both, start=True, stop=True).then_inc(s_rank_mm, 1)
            pe.wait_ge(s_picks, 1)
            for dst, lhs in ((0, pick_v), (COLS, pick_m)):
                for t in range(GC):
                    pe.matmul(mm[0][:, dst:dst + COLS], lhs[:, t, :], pick_c[:, t, :], start=t == 0, stop=t == GC - 1)
            for t in range(GC):
                last = pe.matmul(mm[0][:, 3 * COLS:3 * COLS + 1], pick_z[:, t, :], ones[:, 0:1], start=t == 0, stop=t == GC - 1)
            last.then_inc(s_picks_mm, 1)

            pe.wait_ge(s_wqkv_in, 48)
            pe.wait_ge(s_wproj_in, 16)
            pe.wait_ge(s_small_in, 48)
            pe.wait_ge(s_counts, 1)

            def turn_rows(src, a, b):
                pe.transpose(a[0:DH, :], src[:, 0:DH], ident[:, :])
                return pe.transpose(b[0:DH, :], src[:, DH:D], ident[:, :])

            pe.wait_ge(s_xn_ready, 1)
            turn_rows(xn, ps_x, ps_x2).then_inc(s_xt_mm, 1)

            act_tile = {0: 1, 1: 2, 2: 3, 3: 4, 5: 5, 7: 6, 9: 7, 11: 8, 13: 9}
            dve_tile = {4: 1, 6: 2, 8: 3, 10: 4, 12: 5, 14: 6}
            LEFT = {k: k - 4 for k in range(4, 15)}
            LEFT.update({0: 12, 1: 13, 2: 14, 3: 11})

            def bank_left(c, k):
                prev = LEFT[k]
                base = 0 if k < 4 else 1
                if prev in act_tile:
                    pe.wait_ge(s_act_tiles, c * 9 + 9 * base + act_tile[prev])
                else:
                    pe.wait_ge(s_dve_tiles, c * 6 + 6 * base + dve_tile[prev])

            def router(c):
                pe.wait_ge(s_xf_ready, c + 1)
                turn_rows(xf, ps_x, ps_x2).then_inc(s_xft_mm, 1)
                pe.wait_ge(s_xft_ready, c + 1)
                pe.matmul(ps_l, xft[:, 0, :], wsw_s[:, 0, :], start=True, stop=False)
                pe.matmul(ps_l, xft[0:DH, 1, :], wsw_s[0:DH, 1, :], start=False, stop=True).then_inc(s_l_mm, 1)

            n = pe.value_load(counts_i[0:1, 0:1], min_val=1, max_val=CHUNKS)
            with pe.Fori(0, n) as c:
                pe.wait_ge(s_xt_ready, c + 1)
                for i in range(3):
                    bank_left(c, i)
                    cols = slice(2 * HD + 512 * i, 2 * HD + 512 * (i + 1))
                    pe.matmul(mm[i][:, :], xt[:, 0, :], wqkv_s[:, 0, cols], start=True, stop=False)
                    pe.matmul(mm[i][:, :], xt[0:DH, 1, :], wqkv_s[0:DH, 1, cols], start=False, stop=True).then_inc(s_tile_mm, 1)
                for i in range(8):
                    k = 3 + i
                    which, half, jb = i % 2, (i // 2) % 2, i // 4
                    bank_left(c, k)
                    for j in range(4):
                        a = which * HD + (4 * jb + j) * D + half * DH
                        o_ = mm[k % 4][0:DH, P * j:P * (j + 1)]
                        pe.matmul(o_, wqkv_s[:, 0, a:a + DH], xt[:, 0, :], start=True, stop=False)
                        last = pe.matmul(o_, wqkv_s[0:DH, 1, a:a + DH], xt[0:DH, 1, :], start=False, stop=True)
                    last.then_inc(s_tile_mm, 1)
                pe.wait_ge(s_mdiag, c + 1)
                pe.wait_ge(s_pt_ready, c * 2 + 1)
                pe.matmul(ps_t[:, 0:P], ones[:, :], mdiag[:, :], start=True, stop=True).then_inc(s_mrow_mm, 1)
                pe.wait_ge(s_act_tiles, c * 9 + 16)
                pe.wait_ge(s_dve_tiles, c * 6 + 10)
                pe.wait_ge(s_sides, c + 1)
                for half in range(2):
                    for g in range(4 * half, 4 * half + 4):
                        o_ = ps_s[half][:, P * (g % 4):P * (g % 4 + 1)]
                        for h in range(2):
                            pe.matmul(o_, qt[:, h, g, :, :].rearrange("p j r -> p (j r)"),
                                      kt[:, h, g, :, :].rearrange("p j r -> p (j r)"), start=h == 0, stop=False)
                        last = pe.matmul(o_, sides[:, g, :, :].rearrange("p j k -> p (j k)"),
                                         others[:, :, :].rearrange("p j k -> p (j k)"), start=False, stop=True)
                    last.then_inc(s_s_mm, 1)
                pe.wait_ge(s_xn_ready, c + 2)
                turn_rows(xn, ps_x, ps_x2).then_inc(s_xt_mm, 1)
                pe.wait_ge(s_xt_ready, c + 2)
                router(c)
                pe.wait_ge(s_mrow_ready, c + 1)
                for half in range(2):
                    pe.wait_ge(s_p_ready, c * 2 + half + 1)
                    pe.wait_ge(s_pt_ready, c * 2 + half + 1)
                    for g in range(4 * half, 4 * half + 4):
                        last = pe.transpose(ps_t[:, P * (g % 4):P * (g % 4 + 1)], ex[:, g, :], ident[:, :])
                    last.then_inc(s_pt_mm, 1)
                pe.wait_ge(s_v_moved, c * 128 + 256)
                for i in range(4):
                    k = 11 + i
                    gq, half = i // 2, i % 2
                    pe.wait_ge(s_pt_ready, c * 2 + gq + 2)
                    bank_left(c, k)
                    for g in range(4 * gq, 4 * gq + 4):
                        last = pe.matmul(mm[k % 4][0:DH, P * (g % 4):P * (g % 4 + 1)],
                                         vp[:, g, half * DH:(half + 1) * DH], pt[:, g, :], start=True, stop=True)
                    last.then_inc(s_tile_mm, 1)
                pe.wait_ge(s_act_tiles, c * 9 + 18)
                pe.wait_ge(s_dve_tiles, c * 6 + 12)
                pe.matmul(ps_y, ones[0:1, :], bproj_s[0:1, :], start=True, stop=False)
                for j in range(HEADS):
                    for half in range(2):
                        last = pe.matmul(ps_y, ot[:, half, j, :], wproj_s[:, 2 * j + half, :],
                                         start=False, stop=j == HEADS - 1 and half == 1)
                last.then_inc(s_y_mm, 1)
            router(n)

            pe.wait_ge(s_probT_ready, 1)
            pe.matmul(mm[0][:, 0:1], first[:, :], prob_c[:, 1:2], start=True, stop=True)
            pe.matmul(mm[0][:, 1:2], first[:, :], route_c[:, 1:2], start=True, stop=True).then_inc(s_p0_mm, 1)
            pe.transpose(mm[1][0:CHUNKS, 0:P], prob_c[:, 1:CHUNKS + 1], ident[:, :])
            pe.transpose(mm[1][0:CHUNKS, P:2 * P], route_c[:, 1:CHUNKS + 1], ident[:, :]).then_inc(s_probT_mm, 1)

            pe.wait_ge(s_eqc_ready, 1)
            half_e = E // 2
            for i in range(2):
                rows = eqc[:, half_e * i:half_e * (i + 1), :].rearrange("p e c -> p (e c)")
                pe.matmul(ps_s[i][:, 0:half_e * CHUNKS], before[:, :], rows, start=True, stop=True)
                last = pe.matmul(mm[2 + i][:, 0:half_e * CHUNKS], ones[:, :], rows, start=True, stop=True)
            last.then_inc(s_eqc_mm, 1)
            def probe(k):
                pe.wait_ge(s_hit_ready, k + 1)
                for i in range(8):
                    last = pe.matmul(ps_s[1][:, 0:E * 8], ones_b[:, :], hit[:, :, 8 * i:8 * i + 8], start=i == 0, stop=i == 7)
                last.then_inc(s_hit_mm, 1)

            pe.wait_ge(s_steps_ready, 1)
            for dst, lhs, h in ((ps_t, pick_k, 0), (ps_s[1], pick_s2, 0), (mm[2], pick_k, 1), (mm[3], pick_s2, 1)):
                for t in range(GC):
                    last = pe.matmul(dst[:, 0:OH], lhs[:, t, :], pick_o[:, t, OH * h:OH * (h + 1)], start=t == 0, stop=t == GC - 1)
            last.then_inc(s_steps_mm, 1)

            pe.wait_ge(s_w1_in, 48)
            pe.wait_ge(s_w2_in, 16 * FC)
            pe.wait_ge(s_b2_in, 16)
            pe.wait_ge(s_slots_known, 1)
            m = pe.value_load(counts_i[0:1, 1:2], min_val=1, max_val=TILES)

            def expert_out(t, e):
                pe.wait_ge(s_ob_stored, t + 1)
                pe.wait_ge(s_ht_act, t * 2 + 2)
                pe.matmul(ps_y, ones[0:1, :], b2_s[0:1, bass.ds(e, 1), :].rearrange("p e d -> p (e d)"), start=True, stop=False)
                for f in range(FC):
                    last = pe.matmul(ps_y, ht[:, f, :], w2_s[:, f, bass.ds(e, 1), :].rearrange("p e d -> p (e d)"), start=False, stop=f == FC - 1)
                last.then_inc(s_o_mm, 1)

            def experts_tile(t):
                e_before = pe.value_load(expert_i[0:1, bass.ds(t, 1)], min_val=0, max_val=E - 1)
                e = pe.value_load(expert_i[0:1, bass.ds(t + 1, 1)], min_val=0, max_val=E - 1)
                pe.wait_ge(s_gxt_ready, t + 1)
                for i in range(2):
                    fs = slice(384 * i, 384 * (i + 1))
                    pe.matmul(mm[i][:, 0:384], gxt[:, 0, :], w1_s[:, 0, bass.ds(e, 1), fs].rearrange("p e f -> p (e f)"), start=True, stop=False)
                    pe.matmul(mm[i][:, 0:384], gxt[0:DH, 1, :], w1_s[0:DH, 1, bass.ds(e, 1), fs].rearrange("p e f -> p (e f)"), start=False, stop=True).then_inc(s_h_mm, 1)
                expert_out(t, e_before)
                pe.wait_ge(s_gx_in, t * 16 + 32)
                turn_rows(gx, ps_s[0][:, 0:P], ps_s[0][:, P:2 * P]).then_inc(s_gxt_mm, 1)
                for i in range(2):
                    pe.wait_ge(s_hs_ready, t * 2 + i + 1)
                    for f in range(3):
                        last = pe.transpose(mm[2 + i][:, P * f:P * (f + 1)], hs[:, 384 * i + P * f:384 * i + P * (f + 1)], ident[:, :])
                    last.then_inc(s_ht_mm, 1)

            pe.wait_ge(s_gx_in, 16)
            turn_rows(gx, ps_s[0][:, 0:P], ps_s[0][:, P:2 * P]).then_inc(s_gxt_mm, 1)
            pe.wait_ge(s_steps_read, 1)
            with pe.Fori(0, SPLIT[0]) as t:
                experts_tile(t)
            probe(0)
            with pe.Fori(SPLIT[0], SPLIT[1]) as t:
                experts_tile(t)
            pe.wait_ge(s_above_ready, 1)
            pe.matmul(ps_t[:, 320:320 + E], ones[:, :], red, start=True, stop=True).then_inc(s_above_mm, 1)
            with pe.Fori(SPLIT[1], SPLIT[2]) as t:
                experts_tile(t)
            pe.wait_ge(s_left_known, 1)
            left = pe.value_load(counts_i[0:1, 2:3], min_val=1, max_val=PROBES)
            with pe.Fori(0, left) as k:
                probe(k + 1)
            with pe.Fori(SPLIT[2], SPLIT[3]) as t:
                experts_tile(t)
            pe.wait_ge(s_tie_ready, 1)
            pe.matmul(ps_t[:, 0:E], ones[:, :], red, start=True, stop=True)
            flat = trow[:, :, :].rearrange("p e t -> p (e t)")
            pe.matmul(ps_t[:, 64:64 + E * GC], before[:, :], flat, start=True, stop=True)
            pe.matmul(ps_t[:, 128:128 + E * GC], ones[:, :], flat, start=True, stop=True).then_inc(s_tie_mm, 1)
            with pe.Fori(SPLIT[3], SPLIT[4]) as t:
                experts_tile(t)
            pe.wait_ge(s_keep_ready, 1)
            pe.matmul(ps_t[:, 300:301], ones[:, :], keep_z[:, TR:TR + 1], start=True, stop=True)
            for h, dst in enumerate((ps_s[1], ps_t)):
                for t in range(GC):
                    last = pe.matmul(dst[:, 0:OH], pick_k[:, t, :], pick_o[:, t, OH * h:OH * (h + 1)], start=t == 0, stop=t == GC - 1)
            last.then_inc(s_keep_mm, 1)
            with pe.Fori(SPLIT[4], m) as t:
                experts_tile(t)
            e_last = pe.value_load(expert_i[0:1, bass.ds(m, 1)], min_val=0, max_val=E - 1)
            expert_out(m, e_last)
            def turn_selection(k):
                pe.wait_ge(s_selt_ready, k + 1)
                for i in range(SET):
                    last = pe.transpose(ps_t[:, P * i:P * (i + 1)], sel_t[:, i, :], ident[:, :])
                last.then_inc(s_sel_mm, 1)

            turn_selection(0)
            with pe.Fori(0, n) as c:
                pe.wait_ge(s_rd_ready, c + 1)
                for h in range(SETS):
                    pe.wait_ge(s_sel_ready, c * SETS + h + 1)
                    for i in range(SET):
                        pe.matmul(mm[i][:, 0:2 * D], sel[:, i, :], rd, start=True, stop=True).then_inc(s_row_mm, 1)
                    turn_selection(c * SETS + h + 1)
            pe.nop()

        @block.vector
        def _(dve):
            def then(ins):
                dve.drain()

            dve.memset(x_pad, VOCAB_PAD)
            then(dve.memset(best, 0.0))
            dve.wait_ge(s_x_in, 32)
            then(dve.tensor_copy(x_f, x_i))
            dve.tensor_copy(x_pad[0:B, T:2 * T], x_f[0:B, :])
            then(dve.tensor_copy(x_pad[B:2 * B, T + 1:2 * T + 1], x_f[B:2 * B, :]))

            def blk(t, k):
                return t[:, offs[k]:offs[k + 1]].rearrange("p (r i) -> p r i", r=RB)

            for k in range(NB):
                shifted = bass.AP(work, x_pad_at + 1 + 2 * RB * k + starts[k], [[WORK, P], [2, RB], [1, lens[k]]])
                dve.tensor_tensor(blk(eq, k), x_f[:, starts[k]:T].rearrange("p (o i) -> p o i", o=1).to_broadcast([P, RB, lens[k]]),
                                  shifted, ALU.is_equal)
            dve.drain()
            then(dve.tensor_tensor_scan(run, eq, eq, 0.0, ALU.mult, ALU.add))
            dve.wait_ge(s_consts, 1)
            for k in range(NB):
                dve.scalar_tensor_tensor(out=blk(eq, k), in0=blk(run, k), scalar=128.0,
                                         in1=match_j[:, RB * k:RB * (k + 1)].rearrange("p (r o) -> p r o", o=1).to_broadcast([P, RB, lens[k]]),
                                         op0=ALU.mult, op1=ALU.add)
            dve.drain()
            for k in range(NB):
                then(dve.tensor_reduce(tmp_b[:, starts[k]:T], blk(eq, k).rearrange("p r i -> p i r"), AX.X, ALU.max))
                then(dve.tensor_tensor(best[:, starts[k]:T], best[:, starts[k]:T], tmp_b[:, starts[k]:T], ALU.max))
            then(dve.tensor_copy(tmp_b[0:B, :], best[B:2 * B, :]))
            then(dve.tensor_tensor(best[0:B, :], best[0:B, :], tmp_b[0:B, :], ALU.max))
            then(dve.tensor_copy(tmp_i[0:B, :], best[0:B, :]))
            then(dve.tensor_scalar(tmp_i[0:B, :], tmp_i[0:B, :], 127, None, ALU.bitwise_and))
            then(dve.tensor_copy(tmp_b[0:B, :], tmp_i[0:B, :]))
            then(dve.tensor_tensor(tmp_b[0:B, :], tmp_b[0:B, :], pred_base[:, :], ALU.add))
            dve.scalar_tensor_tensor(out=best[0:B, :], in0=best[0:B, :], scalar=128.0, in1=tmp_b[0:B, :],
                                     op0=ALU.is_ge, op1=ALU.mult).then_inc(s_best_out, 1)

            dve.wait_ge(s_pred_back, 32)
            def rows_of(a):
                return a.rearrange("p t r -> p (t r)")

            def over(a, dims):
                return a.to_broadcast([P] + dims)

            dve.memset(reset_g[:, :, :], 1.0)
            dve.tensor_scalar(m4[:, :, :], v4, 0.0, None, ALU.is_gt)
            dve.drain()
            then(dve.memset(reset_g[:, :, 0:1], 0.0))
            then(dve.tensor_tensor_scan(rows_of(cum[:, :, :]), rows_of(reset_g[:, :, :]), rows_of(m4[:, :, :]), 0.0, ALU.mult, ALU.add))
            then(dve.tensor_copy(rk[:, 0, :], cum[:, :, GT - 1]))
            cnt = rk[:, 0, :]
            dve.tensor_scalar(act[:, :], cnt, 0.0, None, ALU.is_gt)
            then(dve.tensor_scalar(classes[:, 1, :], cnt, float(UNIT), None, ALU.is_ge))
            dve.tensor_tensor(classes[:, 0, :], act[:, :], classes[:, 1, :], ALU.subtract).then_inc(s_act_ready, 1)
            then(dve.tensor_tensor(cum[:, :, :], cum[:, :, :], m4[:, :, :], ALU.mult))
            k_row = iota_k[:, :].rearrange("p (a k) -> p a k", a=1)
            cnt_k = over(cnt.rearrange("p (t o) -> p t o", o=1), [GC, GT])
            dve.tensor_tensor(spread[:, :, :, :], over(cum[:, :, :].rearrange("p t (o r) -> p t o r", o=1), [GC, GT, GT]),
                              over(iota_k1[:, :].rearrange("p (a k b) -> p a k b", a=1, b=1), [GC, GT, GT]), ALU.is_equal)
            dve.tensor_tensor(m16[:, :, :], over(k_row, [GC, GT]), cnt_k, ALU.is_lt)
            dve.tensor_tensor(m16b[:, :, :], over(k_row, [GC, GT]), cnt_k, ALU.is_equal)
            then(dve.tensor_scalar(rk[:, 1, :], cnt, -1.0, float(GT), ALU.mult, ALU.add))
            dve.tensor_tensor(m16b[:, :, :], m16b[:, :, :], over(rk[:, 1, :].rearrange("p (t o) -> p t o", o=1), [GC, GT]), ALU.mult)
            then(dve.tensor_tensor(spread[:, :, :, :], spread[:, :, :, :], over(v4.rearrange("p t (o r) -> p t o r", o=1), [GC, GT, GT]), ALU.mult))
            dve.tensor_tensor(m16[:, :, :], m16[:, :, :], m16b[:, :, :], ALU.add)
            then(dve.tensor_reduce(v16[:, :, :], spread[:, :, :, :], AX.X, ALU.add))
            dve.wait_ge(s_rank_mm, 1)
            then(dve.tensor_copy(rk[:, 2:6, :].rearrange("p a t -> p (a t)"), ps_m[:, 0:4 * GC]))
            for i in range(2):
                dve.tensor_tensor_scan(rk[:, 6 + i, :], ones[:, 0:GC], rk[:, 4 + i, :], 0.0, ALU.mult, ALU.add)
            dve.drain()
            then(dve.tensor_tensor(rk[:, 8:10, :], rk[:, 6:8, :], rk[:, 4:6, :], ALU.subtract))
            then(dve.tensor_tensor(rk[:, 8:10, :], rk[:, 8:10, :], rk[:, 2:4, :], ALU.add))
            then(dve.tensor_scalar(rki[:, 0, 0:1], rk[:, 6, GC - 1:GC], float(BU), None, ALU.add))
            then(dve.tensor_scalar(rki[:, 0, 0:1], rki[:, 0, 0:1], LOG_BU, None, ALU.arith_shift_right))
            then(dve.tensor_copy(rk[:, 10, 0:1], rki[:, 0, 0:1]))
            then(dve.tensor_scalar(rki[:, 1, 0:1], rk[:, 7, GC - 1:GC], rk[:, 10, 0:1], float(CG - 1), ALU.add, ALU.add))
            dve.tensor_scalar(counts_i[0:1, 0:1], rki[0:1, 1, 0:1], 3, None, ALU.arith_shift_right).then_inc(s_counts, 1)
            dve.tensor_scalar(not_big[:, :], iota_b[:, :], rk[0:BU, 10, 0:1], None, ALU.is_lt)
            dve.tensor_scalar(rk[:, 11, :], act[:, :], -1.0, 1.0, ALU.mult, ALU.add)
            dve.tensor_tensor(rk[:, 12, :], rk[:, 8, :], rk[:, 9, :], ALU.add)
            dve.tensor_scalar(rk[:, 13, :], rk[:, 9, :], rk[:, 10, 0:1], float(BU), ALU.add, ALU.mult)
            then(dve.scalar_tensor_tensor(out=rk[:, 14, :], in0=rk[:, 8, :], scalar=1.0, in1=classes[:, 0, :], op0=ALU.add, op1=ALU.mult))
            dve.tensor_tensor(rk[:, 13, :], rk[:, 13, :], classes[:, 1, :], ALU.mult)
            then(dve.tensor_tensor(rk[:, 15, :], iota_g[:, :], rk[:, 12, :], ALU.subtract))
            then(dve.scalar_tensor_tensor(out=rk[:, 15, :], in0=rk[:, 15, :], scalar=1.0, in1=rk[:, 11, :], op0=ALU.add, op1=ALU.mult))
            then(dve.tensor_tensor(unit_i[:, :], rk[:, 13, :], rk[:, 14, :], ALU.add))
            dve.tensor_scalar(rk[:, 15, :], rk[:, 15, :], -1.0, None, ALU.add)
            dve.tensor_scalar(rki[:, 0, :], unit_i[:, :], CU - 1, None, ALU.bitwise_and)
            dve.tensor_scalar(rki[:, 2, :], unit_i[:, :], LOG_CU, None, ALU.arith_shift_right)
            dve.tensor_scalar(rki[:, 3, :], unit_i[:, :], CG - 1, None, ALU.bitwise_and)
            then(dve.tensor_scalar(rki[:, 4, :], unit_i[:, :], 3, None, ALU.arith_shift_right))
            then(dve.tensor_scalar(rki[:, 1, :], rki[:, 0, :], LOG_BU, None, ALU.arith_shift_right))
            then(dve.tensor_copy(rk[:, 16:21, :], rki[:, 0:5, :]))
            for i in (18, 20):
                then(dve.scalar_tensor_tensor(out=rk[:, i, :], in0=rk[:, i, :], scalar=1.0, in1=act[:, :], op0=ALU.add, op1=ALU.mult))
                then(dve.tensor_scalar(rk[:, i, :], rk[:, i, :], -1.0, None, ALU.add))
            flat_q = iota_q[:, :, :].rearrange("p q r -> p (q r)")
            flat_u = iota_u[:, :, :].rearrange("p u k -> p (u k)")
            for t in range(GC):
                dve.tensor_scalar(pick_s[:, t, :], flat_u, rk[:, 16, t:t + 1], classes[:, 0, t:t + 1], ALU.is_equal, ALU.mult)
                dve.tensor_scalar(pick_b[:, t, :], flat_q, rk[:, 17, t:t + 1], classes[:, 1, t:t + 1], ALU.is_equal, ALU.mult)
                dve.tensor_scalar(pick_c[:, t, :], iota_f[:, 0:COLS], rk[:, 18, t:t + 1], None, ALU.is_equal)
                dve.tensor_scalar(pick_z[:, t, :], iota_f[:, :], rk[:, 15, t:t + 1], iota_g[:, t:t + 1], ALU.is_equal, ALU.mult)
            dve.drain()

            def in_chunk(dst, values):
                def cells(a, n_):
                    return a[:, :, :].rearrange("p t (n k) -> p t n k", n=n_)
                dve.tensor_tensor(cells(dst, CU), cells(pick_s, CU),
                                  over(values[:, :, 0:UNIT].rearrange("p t (o k) -> p t o k", o=1), [GC, CU, UNIT]), ALU.mult)
                then(dve.tensor_tensor(cells(pick_x, CG), cells(pick_b, CG),
                                       over(values[:, :, :].rearrange("p t (o k) -> p t o k", o=1), [GC, CG, GT]), ALU.mult))
                then(dve.tensor_tensor(dst[:, :, :], dst[:, :, :], pick_x[:, :, :], ALU.add))

            in_chunk(pick_v, v16)
            in_chunk(pick_m, m16)
            dve.sem_inc(s_picks, 1)
            then(dve.tensor_scalar(rk[:, 21, :], cnt, 1.0, None, ALU.add))
            then(dve.tensor_tensor(m4[:, :, :], m4[:, :, :], over(rk[:, 21, :].rearrange("p (t o) -> p t o", o=1), [GC, GT]), ALU.mult))
            then(dve.tensor_tensor(place_k[:, :, :], cum[:, :, :], m4[:, :, :], ALU.subtract))
            dve.tensor_tensor(place_k[:, :, :], place_k[:, :, :], cnt_k, ALU.add)
            dve.wait_ge(s_picks_mm, 1)
            dve.tensor_scalar(match_f[:, :], mm[0][:, 0:COLS], 0.0, None, ALU.is_gt)
            dve.tensor_scalar(pred_i[:, :], mm[0][:, 0:COLS], -1.0, 0.0, ALU.add, ALU.max)
            then(dve.tensor_copy(mult_c[:, :], mm[0][:, COLS:2 * COLS]))
            then(dve.memset(mult_c[0:1, 0:1], float(GT)))
            then(dve.tensor_scalar(valid[:, :], mult_c[:, :], 0.0, None, ALU.is_gt))
            dve.tensor_scalar(place_v[:, :], valid[:, :], -NOWHERE, NOWHERE, ALU.mult, ALU.add)
            dve.tensor_copy(zlist[:, :], mm[0][:, 3 * COLS:3 * COLS + 1])
            dve.drain().then_inc(s_tables, 1)

            dve.sem_inc(s_dve_tiles, 6)
            dve.sem_inc(s_xf_ready, 1)
            n = dve.value_load(counts_i[0:1, 0:1], min_val=1, max_val=CHUNKS)

            def norm(dst, src, s, count):
                then(dve.bn_stats(s[:, 0:6], src))
                dve.bn_aggr(s[:, 6:8], s[:, 0:6]).then_inc(s_var_ready, 1)
                dve.wait_ge(s_dev_ready, count)
                return dve.tensor_scalar(dst, src, s[:, 6:7], s[:, 8:9], ALU.subtract, ALU.mult)

            def turned(dst, src=ps_m[:, D:D + 2 * P]):
                return dve.tensor_copy(dst[0:DH, :, :], src[0:DH, :].rearrange("p (h t) -> p h t", h=2))

            def embed(c, count):
                dve.wait_ge(s_emb_in, c * 16 + 16)
                then(dve.tensor_scalar(h_next[:, :], emb_t[:, :], match_f[:, bass.ds(c, 1)], None, ALU.mult))
                dve.sem_inc(s_emb_used, 1)
                norm(xn[:, :], h_next[:, :], st, count).then_inc(s_xn_ready, 1)

            def route_tail(c):
                dve.wait_ge(s_l_mm, c + 1)
                then(dve.tensor_reduce(rt[:, 0:1], ps_l, AX.X, ALU.max))
                dve.tensor_scalar(rt[:, 1:2], rt[:, 0:1], -1.0, None, ALU.mult).then_inc(s_lmax_ready, 1)
                dve.wait_ge(s_lexp_ready, c + 1)
                then(dve.reciprocal(rt[:, 3:4], rt[:, 2:3]))
                then(dve.tensor_scalar(rt[:, 16:24], rt[:, 8:16], rt[:, 3:4], None, ALU.mult))
                then(dve.tensor_reduce(rt[:, 4:5], rt[:, 16:24], AX.X, ALU.max))
                then(dve.tensor_scalar(rt[:, 24:32], rt[:, 16:24], rt[:, 4:5], float(E), ALU.is_lt, ALU.mult))
                dve.tensor_copy(prob_c[:, bass.ds(c, 1)], rt[:, 4:5])
                then(dve.tensor_tensor(rt[:, 24:32], rt[:, 24:32], iota_f[:, 0:E], ALU.add))
                dve.tensor_reduce(route_c[:, bass.ds(c, 1)], rt[:, 24:32], AX.X, ALU.min)

            embed(0, 1)
            dve.wait_ge(s_xt_mm, 1)
            turned(xt).then_inc(s_xt_ready, 1)
            with dve.Fori(0, n) as c:
                dve.tensor_copy(h_cur[:, :], h_next[:, :])
                dve.tensor_scalar(mdiag[:, :], ident[:, :], mult_c[:, bass.ds(c, 1)], None, ALU.mult)
                dve.drain().then_inc(s_mdiag, 1)
                for i in range(4):
                    k = 4 + 2 * i
                    dve.wait_ge(s_tile_mm, c * 15 + k + 1)
                    dve.tensor_copy(kt[:, i % 2, :, 4 * (i // 2):4 * (i // 2) + 4, :].rearrange("p g j r -> p j g r"),
                                    mm[k % 4][0:DH, :].rearrange("p (j g r) -> p j g r", j=4, g=CG)).then_inc(s_dve_tiles, 1)
                    if i == 1:
                        embed(c + 1, c * 2 + 2)
                dve.wait_ge(s_mrow_mm, c + 1)
                dve.tensor_copy(mrow[:, :], ps_t[:, 0:P]).then_inc(s_mrow_ready, 1)
                for half in range(2):
                    gs = slice(4 * half, 4 * half + 4)
                    dve.wait_ge(s_s_mm, c * 2 + half + 2)
                    then(dve.tensor_reduce(sm[:, 0, gs], ps_s[half][:, :].rearrange("p (g l) -> p g l", g=4), AX.X, ALU.max))
                    dve.tensor_scalar(sm[:, 1, gs], sm[:, 0, gs], -1.0, None, ALU.mult).then_inc(s_max_ready, 1)
                dve.wait_ge(s_xt_mm, c + 2)
                turned(xt).then_inc(s_xt_ready, 1)
                for half in range(2):
                    gs = slice(4 * half, 4 * half + 4)
                    dve.wait_ge(s_exp_ready, c * 2 + half + 1)
                    then(dve.tensor_tensor(ex[:, gs, :].rearrange("p g (j k) -> p g j k", j=HEADS), ex[:, gs, :].rearrange("p g (j k) -> p g j k", j=HEADS),
                                           over(mrow[:, GT * 4 * half:GT * 4 * (half + 1)].rearrange("p (g o k) -> p g o k", g=4, o=1), [4, HEADS, GT]), ALU.mult))
                    then(dve.tensor_reduce(sm[:, 2, gs], ex[:, gs, :], AX.X, ALU.add))
                    then(dve.tensor_scalar(sm[:, 3, gs], sm[:, 2, gs], 1e-30, float(D) ** 0.5, ALU.max, ALU.mult))
                    then(dve.reciprocal(sm[:, 3, gs], sm[:, 3, gs]))
                    if half == 0:
                        dve.wait_ge(s_xft_mm, c + 1)
                        turned(xft).then_inc(s_xft_ready, 1)
                    dve.tensor_tensor(ex[:, gs, :], ex[:, gs, :], sm[:, 3, gs].rearrange("p (g o) -> p g o", o=1).to_broadcast([P, 4, P]),
                                      ALU.mult).then_inc(s_p_ready, 1)
                route_tail(c)
                for i in range(2):
                    k = 12 + 2 * i
                    dve.wait_ge(s_tile_mm, c * 15 + k + 1)
                    dve.tensor_copy(ot[:, 1, :, 64 * i:64 * i + 64].rearrange("p j (g r) -> p g j r", r=GT),
                                    mm[k % 4][0:DH, :].rearrange("p (g j r) -> p g j r", g=4, j=HEADS)).then_inc(s_dve_tiles, 1)
                dve.wait_ge(s_y_mm, c + 2)
                dve.wait_ge(s_xf_out, c * 16 + 16)
                then(dve.tensor_tensor(h1, h_cur[:, :], ps_y, ALU.add))
                norm(xf, h1, st2, c * 2 + 3).then_inc(s_xf_ready, 1)
            dve.wait_ge(s_xft_mm, n + 1)
            turned(xft).then_inc(s_xft_ready, 1)
            route_tail(n)
            dve.drain().then_inc(s_probT_ready, 1)

            def by_t(a):
                return a.rearrange("p (t r) -> p t r", t=GC)

            def by_group(dst, values):
                return dve.tensor_tensor(dst[:, :, :].rearrange("p t (q r) -> p t q r", q=CG), pick_u[:, :, :].rearrange("p t (q r) -> p t q r", q=CG),
                                         over(values.rearrange("p t (o r) -> p t o r", o=1), [GC, CG, GT]), ALU.mult)

            rc = route_c[:, 1:CHUNKS + 1]
            for e in range(E):
                dve.scalar_tensor_tensor(out=eqc[:, e, :], in0=rc, scalar=float(e), in1=valid[:, 0:CHUNKS], op0=ALU.is_equal, op1=ALU.mult)
            dve.drain().then_inc(s_eqc_ready, 1)
            dve.wait_ge(s_probT_mm, 1)
            dve.memset(pT[:, :, :], 0.0)
            dve.drain()
            then(dve.tensor_copy(pT[:, :, 0:P], mm[1][0:CHUNKS, 0:2 * P].rearrange("p (w m) -> p w m", w=2)))
            for i in range(2):
                windows = bass.AP(area, pT_at + (P + GT) * i, [[2 * 3 * HD, CHUNKS], [UNIT, CU], [1, GT]])
                dve.tensor_copy(pTx[:, :, i, :], windows)
            dve.drain().then_inc(s_probT_ready, 1)

            dve.memset(reset_c[:, :, :], 1.0)
            dve.memset(reset_r[:, :, :], 1.0)
            dve.drain()
            dve.memset(reset_c[:, :, 0:1], 0.0)
            dve.memset(reset_r[:, :, 0:1], 0.0)
            dve.memset(gxt[DH:DH + 1, 0, :], 1.0)
            dve.memset(ht[:, :, :], 0.0)
            dve.memset(pl[:, :], 0.0)
            dve.drain().then_inc(s_ones_set, 1)
            dve.sem_inc(s_ht_act, 2)
            dve.wait_ge(s_p0_mm, 1)
            dve.wait_ge(s_zrow_in, 16)
            dve.tensor_copy(zroute[:, :], mm[0][:, 1:2])
            then(dve.tensor_copy(p0, mm[0][:, 0:1]))
            dve.scalar_tensor_tensor(out=bz, in0=xh0[:, 0:D], scalar=p0, in1=xh0[:, D:2 * D], op0=ALU.mult, op1=ALU.add).then_inc(s_bz_ready, 1)
            dve.wait_ge(s_eqc_mm, 1)
            he = E // 2
            for i in range(2):
                dve.tensor_copy(csum[:, he * i:he * (i + 1), :].rearrange("p e c -> p (e c)"), mm[2 + i][:, 0:he * CHUNKS])
            dve.drain()
            then(dve.tensor_tensor_scan(cinc[:, :, :].rearrange("p e c -> p (e c)"), reset_c[:, :, :].rearrange("p e c -> p (e c)"),
                                        csum[:, :, :].rearrange("p e c -> p (e c)"), 0.0, ALU.mult, ALU.add))
            tot = cinc[:, :, CHUNKS - 1]
            dve.tensor_scalar(tl_i[:, 0, :], tot, float(P - 1), None, ALU.add)
            then(dve.tensor_tensor(posn[:, :, :], cinc[:, :, :], csum[:, :, :], ALU.subtract))
            then(dve.tensor_scalar(tl_i[:, 0, :], tl_i[:, 0, :], 7, None, ALU.arith_shift_right))
            then(dve.tensor_copy(tl[:, 0, :], tl_i[:, 0, :]))
            then(dve.tensor_tensor_scan(tl[:, 1, :], ones[:, 0:E], tl[:, 0, :], 0.0, ALU.mult, ALU.add))
            dve.tensor_scalar(counts_i[0:1, 1:2], tl[0:1, 1, E - 1:E], float(LEAST), None, ALU.max)
            then(dve.tensor_tensor(tl[:, 2, :], tl[:, 1, :], tl[:, 0, :], ALU.subtract))
            then(dve.tensor_scalar(tl[:, 3, :], tl[:, 2, :], float(P), None, ALU.mult))
            then(dve.tensor_tensor(tcmp[:, :, :], tl[0:1, 2, :].rearrange("p (o e) -> p o e", o=1).to_broadcast([1, TILES, E]),
                                   iota_f[0:1, 0:TILES].rearrange("p (t o) -> p t o", o=1).to_broadcast([1, TILES, E]), ALU.is_le))
            then(dve.tensor_reduce(texp, tcmp[:, :, :], AX.X, ALU.add))
            then(dve.tensor_scalar(expert_i[0:1, 1:TILES + 1], texp, -1.0, None, ALU.add))
            then(dve.tensor_tensor(posn[:, :, :], posn[:, :, :], tl[:, 3, :].rearrange("p (e o) -> p e o", o=1).to_broadcast([P, E, CHUNKS]), ALU.add))
            for i in range(2):
                es = slice(he * i, he * (i + 1))
                dve.tensor_tensor(posn[:, es, :], posn[:, es, :], ps_s[i][:, 0:he * CHUNKS].rearrange("p (e c) -> p e c", e=he), ALU.add)
            dve.drain()
            then(dve.tensor_tensor(posn[:, :, :], posn[:, :, :], eqc[:, :, :], ALU.mult))
            dve.memset(slot_f[:, :], 0.0)
            dve.drain()
            then(dve.tensor_reduce(slot_f[:, 0:CHUNKS], posn[:, :, :].rearrange("p e c -> p c e"), AX.X, ALU.add))
            then(dve.tensor_copy(slot_i[:, :], slot_f[:, :]))
            dve.tensor_tensor(slot_i[:, :], slot_f[:, :], place_v[:, :], ALU.add)
            dve.drain()
            dve.sem_inc(s_slots_known, 1)
            dve.wait_ge(s_prob_out, 16)
            then(dve.scalar_tensor_tensor(out=by_t(slot_v), in0=over(rk[:, 16, :].rearrange("p (t o) -> p t o", o=1), [GC, GT]), scalar=float(UNIT),
                                          in1=place_k[:, :, :], op0=ALU.mult, op1=ALU.add))
            for t in range(GC):
                dve.tensor_scalar(pick_u[:, t, :], flat_q, rk[:, 19, t:t + 1], None, ALU.is_equal)
                dve.tensor_scalar(pick_o[:, t, :], iota_o[:, :], rk[:, 20, t:t + 1], None, ALU.is_equal)
            dve.drain()
            by_group(pick_k, tok_of[:, :, :])
            by_group(pick_s2, by_t(slot_v))
            dve.drain().then_inc(s_steps_ready, 1)

            dve.wait_ge(s_steps_mm, 1)
            dve.tensor_scalar(out_tok[:, OH:OC], mm[2][:, 0:OH], -1.0, NOWHERE, ALU.mult, ALU.add)
            dve.tensor_copy(out_place[:, OH:OC], mm[3][:, 0:OH]).then_inc(s_steps_read, 1)
            dve.tensor_scalar(out_tok[:, 0:OH], ps_t[:, 0:OH], -1.0, NOWHERE, ALU.mult, ALU.add)
            dve.tensor_copy(out_place[:, 0:OH], ps_s[1][:, 0:OH])
            dve.memset(out_tok[:, OC:OC + SET], 0)
            dve.memset(out_place[:, OC:OC + SET], 0.0)
            dve.memset(out_keep[:, OC:OC + SET], 0.0)
            dve.drain()
            dve.wait_ge(s_full_in, 16 * GC)
            then(dve.tensor_tensor(at_place, over(place_k[:, :, :].rearrange("p t (r o) -> p (t r) o", o=1), [TR, GT]),
                                   over(k_row, [TR, GT]), ALU.is_equal))
            fp = keep_z[:, 0:TR]
            fr = keep
            for i, dst in enumerate((fp, fr)):
                then(dve.tensor_tensor(at_work.rearrange("p (t r) k -> p t r k", t=GC), at_place.rearrange("p (t r) k -> p t r k", t=GC),
                                       over(full[:, :, i, :].rearrange("p t (o k) -> p t o k", o=1), [GC, GT, GT]), ALU.mult))
                then(dve.tensor_reduce(dst, at_work, AX.X, ALU.add))
            for e in range(E):
                dve.tensor_scalar(member[:, e, :], fr, float(e), None, ALU.is_equal)
                dve.scalar_tensor_tensor(out=score[:, e, :], in0=fr, scalar=float(e), in1=fp, op0=ALU.is_equal, op1=ALU.mult)
            dve.memset(thr, 0.0)
            dve.memset(step, 1.0)
            dve.drain()

            def per_expert(a):
                return a.rearrange("p (e o) -> p e o", o=1).to_broadcast([P, E, TR])

            def mark(count_from):
                return dve.tensor_tensor(hit[:, :, :], score[:, :, :], per_expert(count_from), ALU.is_ge).then_inc(s_hit_ready, 1)

            def take(count):
                dve.wait_ge(s_hit_mm, count)
                then(dve.tensor_reduce(red, ps_s[1][:, 0:E * 8].rearrange("p (e n) -> p e n", e=E), AX.X, ALU.add))
                then(dve.scalar_tensor_tensor(out=cand, in0=red, scalar=float(CAP), in1=cand, op0=ALU.is_ge, op1=ALU.mult))
                then(dve.tensor_tensor(thr, thr, cand, ALU.max))

            then(dve.tensor_scalar(cand, iota_f[:, 0:E], zroute[:, :], None, ALU.is_equal))
            then(dve.tensor_scalar(cand, cand, p0, None, ALU.mult))
            then(dve.tensor_scalar(rem, cand, 0.0, 2.0, ALU.is_equal, ALU.mult))
            then(dve.tensor_tensor(cand, cand, rem, ALU.add))
            mark(cand)
            take(1)
            dve.tensor_tensor(cmp[:, :, :], score[:, :, :], per_expert(thr), ALU.is_gt)
            dve.drain()
            dve.tensor_reduce(red, cmp[:, :, :], AX.X, ALU.add).then_inc(s_above_ready, 1)
            dve.wait_ge(s_above_mm, 1)
            then(dve.tensor_scalar(rem, ps_t[:, 320:320 + E], float(CAP), None, ALU.is_gt))
            then(dve.tensor_reduce(left_f[:, :], rem, AX.X, ALU.max))
            dve.tensor_scalar(rem[:, 0:1], left_f[:, :], float(PROBES - 1), 1.0, ALU.mult, ALU.add)
            dve.tensor_scalar(left_f[:, :], left_f[:, :], -1.0, 1.0, ALU.mult, ALU.add)
            dve.drain()
            dve.tensor_scalar(thr, thr, left_f[:, :], None, ALU.mult)
            dve.tensor_copy(counts_i[0:1, 2:3], rem[0:1, 0:1])
            dve.drain().then_inc(s_left_known, 1)
            left = dve.value_load(counts_i[0:1, 2:3], min_val=1, max_val=PROBES)
            with dve.Fori(0, left) as k:
                then(dve.tensor_scalar(cand, thr, step, None, ALU.add))
                mark(cand)
                take(k + 2)
                then(dve.tensor_scalar(step, step, 0.5, None, ALU.mult))

            dve.tensor_tensor(cmp[:, :, :], score[:, :, :], per_expert(thr), ALU.is_gt)
            then(dve.tensor_tensor(tie[:, :, :], score[:, :, :], per_expert(thr), ALU.is_equal))
            dve.tensor_reduce(red, cmp[:, :, :], AX.X, ALU.add)
            then(dve.tensor_tensor(tie[:, :, :], tie[:, :, :], member[:, :, :], ALU.mult))
            dve.tensor_reduce(trow[:, :, :], tie[:, :, :].rearrange("p e (t r) -> p e t r", t=GC), AX.X, ALU.add)
            dve.drain().then_inc(s_tie_ready, 1)
            dve.tensor_tensor_scan(incl[:, :, :].rearrange("p e n -> p (e n)"), reset_r[:, :, :].rearrange("p n r -> p (n r)"),
                                   tie[:, :, :].rearrange("p e n -> p (e n)"), 0.0, ALU.mult, ALU.add)
            dve.wait_ge(s_tie_mm, 1)
            dve.tensor_scalar(rem, ps_t[:, 0:E], -1.0, float(CAP), ALU.mult, ALU.add)
            then(dve.tensor_copy(tsum[:, :, :].rearrange("p e t -> p (e t)"), ps_t[:, 128:128 + E * GC]))
            then(dve.tensor_copy(tbase[:, :, :].rearrange("p e t -> p (e t)"), ps_t[:, 64:64 + E * GC]))
            for t in range(1, GC):
                for u in range(t):
                    then(dve.tensor_tensor(tbase[:, :, t:t + 1], tbase[:, :, t:t + 1], tsum[:, :, u:u + 1], ALU.add))
            for t in range(GC):
                ts_ = slice(GT * t, GT * (t + 1))
                dve.tensor_tensor(incl[:, :, ts_], incl[:, :, ts_], tbase[:, :, t:t + 1].to_broadcast([P, E, GT]), ALU.add)
            dve.drain()
            then(dve.tensor_tensor(incl[:, :, :], incl[:, :, :], per_expert(rem), ALU.is_le))
            then(dve.tensor_tensor(tie[:, :, :], tie[:, :, :], incl[:, :, :], ALU.mult))
            then(dve.tensor_tensor(cmp[:, :, :], cmp[:, :, :], tie[:, :, :], ALU.add))
            then(dve.tensor_reduce(keep, cmp[:, :, :].rearrange("p e n -> p n e"), AX.X, ALU.add))
            then(dve.tensor_tensor(by_t(keep_z[:, 0:TR]), by_t(keep), rk[:, 11, :].rearrange("p (t o) -> p t o", o=1).to_broadcast([P, GC, GT]), ALU.mult))
            dve.tensor_reduce(keep_z[:, TR:TR + 1], keep_z[:, 0:TR], AX.X, ALU.add)
            by_group(pick_k, by_t(keep))
            dve.drain().then_inc(s_keep_ready, 1)
            dve.wait_ge(s_keep_mm, 1)
            dve.tensor_copy(zs[:, 0:1], ps_t[:, 300:301])
            dve.tensor_copy(out_keep[:, 0:OH], ps_s[1][:, 0:OH])
            then(dve.tensor_copy(out_keep[:, OH:OC], ps_t[:, 0:OH]))
            then(dve.tensor_scalar(zk[:, 0, :], iota_z[:, :], zs[:, 0:1], None, ALU.is_lt))
            dve.tensor_scalar(zk[:, 1, :], zk[:, 0, :], -1.0, 1.0, ALU.mult, ALU.add)
            then(dve.tensor_scalar(zs[:, 3:4], zk[:, 0, 0:1], -NOWHERE, NOWHERE, ALU.mult, ALU.add))
            then(dve.scalar_tensor_tensor(out=zs_i[:, 0:1], in0=zk[:, 0, 0:1], scalar=zlist[:, 0:1], in1=zs[:, 3:4], op0=ALU.mult, op1=ALU.add))
            for r_ in range(GT):
                dve.tensor_scalar(zt[:, r_, :], bz, zk[:, 1, r_:r_ + 1], None, ALU.mult)

            def select(k):
                dve.tensor_copy(step_cols[:, 0, :], out_place[:, bass.ds(k * SET, SET)])
                then(dve.tensor_copy(step_cols[:, 1, :], out_keep[:, bass.ds(k * SET, SET)]))
                for i in range(SET):
                    last = dve.tensor_scalar(sel_t[:, i, :], iota_f[:, :], step_cols[:, 0, i:i + 1], None, ALU.is_equal)
                last.then_inc(s_selt_ready, 1)
                dve.wait_ge(s_sel_mm, k + 1)
                dve.tensor_copy(sel[:, :, :].rearrange("p s m -> p (s m)"), ps_t[:, :]).then_inc(s_sel_ready, 1)

            def both_rows(c, count):
                dve.wait_ge(s_cx_in, count)
                dve.scalar_tensor_tensor(out=rd[:, 0:D], in0=xg[:, 0:D], scalar=prob_c[:, bass.ds(c + 1, 1)], in1=xg[:, D:2 * D], op0=ALU.mult, op1=ALU.add)
                then(dve.tensor_tensor(rd[:, D:2 * D], og, xg[:, 0:D], ALU.subtract))
                dve.tensor_scalar(rd[:, D:2 * D], rd[:, D:2 * D], prob_c[:, bass.ds(c + 1, 1)], None, ALU.mult)
                dve.drain().then_inc(s_rd_ready, 1)

            dve.drain()
            select(0)
            both_rows(0, 32)
            dve.wait_ge(s_oz_in, 16)
            then(dve.scalar_tensor_tensor(out=az, in0=oz, scalar=p0, in1=xh0[:, D:2 * D], op0=ALU.mult, op1=ALU.add))
            for r_ in range(GT):
                dve.scalar_tensor_tensor(out=zt[:, r_, :], in0=az, scalar=zk[:, 0, r_:r_ + 1], in1=zt[:, r_, :], op0=ALU.mult, op1=ALU.add)
            dve.drain().then_inc(s_zt_ready, 1)
            with dve.Fori(0, n) as c:
                for h in range(SETS):
                    for i in range(SET):
                        dve.wait_ge(s_row_copied, c * BU + h * SET + i + 1)
                        dve.scalar_tensor_tensor(out=yo[:, i, :], in0=mm[i][:, D:2 * D], scalar=step_cols[:, 1, i:i + 1], in1=yo[:, i, :],
                                                 op0=ALU.mult, op1=ALU.add).then_inc(s_y_ready, 1)
                    dve.drain()
                    select(c * SETS + h + 1)
                both_rows(c + 1, c * 32 + 64)
            dve.nop()

_INS = ["x", "L0_tok_emb", "L0_attn_W_qkv", "L0_attn_b_qkv", "L0_attn_W_proj", "L0_attn_b_proj",
        "L0_ffn_switch_w", "L0_ffn_switch_b", "L0_ffn_w1", "L0_ffn_b1", "L0_ffn_w2", "L0_ffn_b2"]

def kernel(**inputs):
    import numpy as _np
    import concourse.bacc as _bacc
    from concourse.bass_utils import run_bass_kernel_spmd as _run

    nc = _bacc.Bacc("TRN2", target_bir_lowering=False, num_devices=1)
    arrays, args = {}, []
    for name in _INS:
        a = _np.ascontiguousarray(inputs[name])
        arrays[f"in_{name}"] = a
        args.append(nc.dram_tensor(f"in_{name}", a.shape, mybir.dt.from_np(a.dtype), kind="ExternalInput").ap())
    args.append(nc.dram_tensor("out_0", (B, T, D), F32, kind="ExternalOutput").ap())
    build(nc, *args)
    r = _run(nc, [arrays], core_ids=[0])
    return r.results[0]["out_0"]
```
